# Optimizing a Trainium2 kernel written in Bass

```python
import numpy as np
import jax
import jax.numpy as jnp

def _softmax(x, axis=-1):
    return jax.nn.softmax(x, axis=axis)

def _gelu(x):
    return jax.nn.gelu(x, approximate=True)

def _silu(x):
    return jax.nn.silu(x)

def _sigmoid(x):
    return jax.nn.sigmoid(x)

def _layernorm(x, axis=-1, eps=1e-05):
    m = jnp.mean(x, axis=axis, keepdims=True)
    v = jnp.var(x, axis=axis, keepdims=True)
    return (x - m) / jnp.sqrt(v + eps)

def _scatter_add(tgt, idx, src, axis=0):
    return tgt.at[idx].add(src)

def _segment_sum(src, seg, n):
    return jax.ops.segment_sum(src, seg, n)
kernel_name = 'mk_seq_postln_d2_jaxref_r4_005492'

def setup_inputs(seed: int=0):
    np.random.seed(seed)
    _w = jnp.asarray

    def _L0_attn_setup():
        import jax, jax.numpy as jnp
        import numpy as np
        N_EMBD = 256
        QK_DIM = 16
        key = jax.random.key(seed)
        k1, k2, k3, k4, k5 = jax.random.split(key, 5)
        b, s = (8, 512)
        lim = 1.0 / np.sqrt(N_EMBD)
        return {'x': jax.random.normal(k1, (b, s, N_EMBD), dtype=jnp.float32), 'w_q': jax.random.uniform(k2, (QK_DIM, N_EMBD), minval=-lim, maxval=lim, dtype=jnp.float32), 'b_q': jax.random.uniform(k3, (QK_DIM,), minval=-lim, maxval=lim, dtype=jnp.float32), 'w_k': jax.random.uniform(k4, (QK_DIM, N_EMBD), minval=-lim, maxval=lim, dtype=jnp.float32), 'b_k': jax.random.uniform(k5, (QK_DIM,), minval=-lim, maxval=lim, dtype=jnp.float32)}
    _L0_attn_in = _L0_attn_setup()

    def _L0_ffn_setup():
        import jax, jax.numpy as jnp
        import numpy as np
        EPS = 1e-05

        @jax.custom_vjp
        def ste_quantize(w):
            scale = jnp.maximum(jnp.mean(jnp.abs(w)), EPS)
            return jnp.clip(jnp.round(w / scale), -1.0, 1.0)

        def _ste_fwd(w):
            return (ste_quantize(w), None)

        def _ste_bwd(_, g):
            return (g,)
        ste_quantize.defvjp(_ste_fwd, _ste_bwd)
        key = jax.random.key(seed)
        k1, k2 = jax.random.split(key)
        x = jax.random.normal(k1, (8, 2048, 256), dtype=jnp.float32)
        weight = jax.random.normal(k2, (256, 256), dtype=jnp.float32) * 0.02
        return {'x': x, 'weight': weight}
    _L0_ffn_in = _L0_ffn_setup()

    def _L1_attn_setup():
        import jax, jax.numpy as jnp
        import numpy as np
        from jax import lax
        B, N, C, RED = (8, 512, 256, 4)
        GN_EPS = 1e-05

        def _conv1d(x, w):
            return lax.conv_general_dilated(x, w, (1,), [(1, 1)], dimension_numbers=('NCH', 'OIH', 'NCH'))

        def _ode_func(A, conv1_w, gn_g, gn_b, conv2_w, conv2_b):
            h = _conv1d(A[:, None, :], conv1_w)
            b, _, n = h.shape
            hg = h.reshape(b, 2, 2, n)
            mu = hg.mean((2, 3), keepdims=True)
            var = hg.var((2, 3), keepdims=True)
            h = ((hg - mu) * lax.rsqrt(var + GN_EPS)).reshape(b, 4, n)
            h = jax.nn.relu(h * gn_g[None, :, None] + gn_b[None, :, None])
            y = _conv1d(h, conv2_w) + conv2_b[None, :, None]
            return y[:, 0, :]
        key = jax.random.key(seed)
        ks = jax.random.split(key, 8)
        s = lambda k, shp, sc: jax.random.normal(k, shp, jnp.float32) * sc
        return dict(x=jax.random.normal(ks[0], (B, N, C), jnp.float32), qkv_w=s(ks[1], (C, 3 * C), 0.02), c1=jnp.float32(0.01 ** 2), c2=jnp.float32(0.03 ** 2), conv1_w=s(ks[2], (4, 1, 3), 0.3), gn_g=jnp.ones(4, jnp.float32), gn_b=jnp.zeros(4, jnp.float32), conv2_w=s(ks[3], (1, 4, 3), 0.3), conv2_b=jnp.zeros(1, jnp.float32), ch_w1=s(ks[4], (C, C // RED), 0.02), ch_b1=jnp.zeros(C // RED, jnp.float32), ch_w2=s(ks[5], (C // RED, C), 0.02), ch_b2=jnp.zeros(C, jnp.float32), proj_w=s(ks[6], (C, C), 0.02), proj_b=jnp.zeros(C, jnp.float32))
    _L1_attn_in = _L1_attn_setup()

    def _L1_ffn_setup():
        import jax, jax.numpy as jnp
        import numpy as np
        D_MODEL = 256
        EXPERT_DIM = 512
        N_EXPERTS = 8
        LN_EPS = 1e-05

        def _bit_quant(W):
            scale = jnp.clip(jnp.mean(jnp.abs(W), axis=-1, keepdims=True), 1e-05, None)
            w_q = jnp.clip(jnp.round(W / scale), -1.0, 1.0) * scale
            return W + jax.lax.stop_gradient(w_q - W)
        key = jax.random.key(seed)
        ks = jax.random.split(key, 7)
        x = jax.random.normal(ks[0], (4, 512, D_MODEL), dtype=jnp.float32)
        shared_w1 = jax.random.normal(ks[1], (EXPERT_DIM, D_MODEL), dtype=jnp.float32) / np.sqrt(EXPERT_DIM)
        shared_w2 = jax.random.normal(ks[2], (D_MODEL, EXPERT_DIM), dtype=jnp.float32) / np.sqrt(D_MODEL)
        expert_w1 = jax.random.normal(ks[3], (N_EXPERTS, EXPERT_DIM, D_MODEL), dtype=jnp.float32) / np.sqrt(EXPERT_DIM)
        expert_w2 = jax.random.normal(ks[4], (N_EXPERTS, D_MODEL, EXPERT_DIM), dtype=jnp.float32) / np.sqrt(D_MODEL)
        router_w = 0.02 * jax.random.normal(ks[5], (N_EXPERTS, D_MODEL), dtype=jnp.float32)
        ln_gamma = jnp.ones((D_MODEL,), dtype=jnp.float32)
        ln_beta = jnp.zeros((D_MODEL,), dtype=jnp.float32)
        return {'x': x, 'shared_w1': shared_w1, 'shared_w2': shared_w2, 'expert_w1': expert_w1, 'expert_w2': expert_w2, 'router_w': router_w, 'ln_gamma': ln_gamma, 'ln_beta': ln_beta}
    _L1_ffn_in = _L1_ffn_setup()
    _d = {'L0_attn_x': _L0_attn_in['x'], 'L0_attn_w_q': _L0_attn_in['w_q'], 'L0_attn_b_q': _L0_attn_in['b_q'], 'L0_attn_w_k': _L0_attn_in['w_k'], 'L0_attn_b_k': _L0_attn_in['b_k'], 'L0_ffn_weight': _L0_ffn_in['weight'], 'L1_attn_qkv_w': _L1_attn_in['qkv_w'], 'L1_attn_c1': _L1_attn_in['c1'], 'L1_attn_c2': _L1_attn_in['c2'], 'L1_attn_conv1_w': _L1_attn_in['conv1_w'], 'L1_attn_gn_g': _L1_attn_in['gn_g'], 'L1_attn_gn_b': _L1_attn_in['gn_b'], 'L1_attn_conv2_w': _L1_attn_in['conv2_w'], 'L1_attn_conv2_b': _L1_attn_in['conv2_b'], 'L1_attn_ch_w1': _L1_attn_in['ch_w1'], 'L1_attn_ch_b1': _L1_attn_in['ch_b1'], 'L1_attn_ch_w2': _L1_attn_in['ch_w2'], 'L1_attn_ch_b2': _L1_attn_in['ch_b2'], 'L1_attn_proj_w': _L1_attn_in['proj_w'], 'L1_attn_proj_b': _L1_attn_in['proj_b'], 'L1_ffn_shared_w1': _L1_ffn_in['shared_w1'], 'L1_ffn_shared_w2': _L1_ffn_in['shared_w2'], 'L1_ffn_expert_w1': _L1_ffn_in['expert_w1'], 'L1_ffn_expert_w2': _L1_ffn_in['expert_w2'], 'L1_ffn_router_w': _L1_ffn_in['router_w'], 'L1_ffn_ln_gamma': _L1_ffn_in['ln_gamma'], 'L1_ffn_ln_beta': _L1_ffn_in['ln_beta']}
    _x0 = _d['L0_attn_x']
    _d['L0_attn_x'] = jax.random.normal(jax.random.fold_in(jax.random.key(seed), 1), (16, 512, 256), dtype=_x0.dtype)
    del _x0
    return _d

def reference(L0_attn_x, L0_attn_w_q, L0_attn_b_q, L0_attn_w_k, L0_attn_b_k, L0_ffn_weight, L1_attn_qkv_w, L1_attn_c1, L1_attn_c2, L1_attn_conv1_w, L1_attn_gn_g, L1_attn_gn_b, L1_attn_conv2_w, L1_attn_conv2_b, L1_attn_ch_w1, L1_attn_ch_b1, L1_attn_ch_w2, L1_attn_ch_b2, L1_attn_proj_w, L1_attn_proj_b, L1_ffn_shared_w1, L1_ffn_shared_w2, L1_ffn_expert_w1, L1_ffn_expert_w2, L1_ffn_router_w, L1_ffn_ln_gamma, L1_ffn_ln_beta):

    def _L0_attn_ref(x, w_q, b_q, w_k, b_k):
        import jax, jax.numpy as jnp
        import numpy as np
        N_EMBD = 256
        QK_DIM = 16
        s = x.shape[-2]
        q = jnp.einsum('bsd,ed->bse', x, w_q) + b_q
        k = jnp.einsum('bsd,ed->bse', x, w_k) + b_k
        scale = 1.0 / jnp.sqrt(jnp.asarray(QK_DIM, dtype=x.dtype))
        mask = jnp.arange(s)[:, None] >= jnp.arange(s)[None, :]
        scores = jnp.einsum('bqe,bke->bqk', q, k) * scale
        scores = jnp.where(mask[None], scores, jnp.asarray(-10000.0, dtype=x.dtype))
        probs = jax.nn.softmax(scores, axis=-1)
        return jnp.einsum('bqk,bkv->bqv', probs, x)

    def _L0_ffn_ref(x, weight):
        import jax, jax.numpy as jnp
        import numpy as np
        EPS = 1e-05

        @jax.custom_vjp
        def ste_quantize(w):
            scale = jnp.maximum(jnp.mean(jnp.abs(w)), EPS)
            return jnp.clip(jnp.round(w / scale), -1.0, 1.0)

        def _ste_fwd(w):
            return (ste_quantize(w), None)

        def _ste_bwd(_, g):
            return (g,)
        ste_quantize.defvjp(_ste_fwd, _ste_bwd)
        w_ternary = ste_quantize(weight)
        scale = jnp.maximum(jnp.mean(jnp.abs(weight)), EPS)
        return jnp.einsum('bsi,oi->bso', x, w_ternary * scale)

    def _L1_attn_ref(x, qkv_w, c1, c2, conv1_w, gn_g, gn_b, conv2_w, conv2_b, ch_w1, ch_b1, ch_w2, ch_b2, proj_w, proj_b):
        import jax, jax.numpy as jnp
        import numpy as np
        from jax import lax
        B, N, C, RED = (8, 512, 256, 4)
        GN_EPS = 1e-05

        def _conv1d(x, w):
            return lax.conv_general_dilated(x, w, (1,), [(1, 1)], dimension_numbers=('NCH', 'OIH', 'NCH'))

        def _ode_func(A, conv1_w, gn_g, gn_b, conv2_w, conv2_b):
            h = _conv1d(A[:, None, :], conv1_w)
            b, _, n = h.shape
            hg = h.reshape(b, 2, 2, n)
            mu = hg.mean((2, 3), keepdims=True)
            var = hg.var((2, 3), keepdims=True)
            h = ((hg - mu) * lax.rsqrt(var + GN_EPS)).reshape(b, 4, n)
            h = jax.nn.relu(h * gn_g[None, :, None] + gn_b[None, :, None])
            y = _conv1d(h, conv2_w) + conv2_b[None, :, None]
            return y[:, 0, :]
        Bx, Nx, Cx = x.shape
        qkv = (x @ qkv_w).reshape(Bx, Nx, 3, Cx)
        q, k, v = (qkv[..., 0, :], qkv[..., 1, :], qkv[..., 2, :])
        mu_q = q.mean(-1, keepdims=True)
        mu_k = k.mean(-1, keepdims=True)
        dq, dk = (q - mu_q, k - mu_k)
        inv_cm1 = 1.0 / (Cx - 1)
        sigma_qk = (dq * dk).sum(-1, keepdims=True) * inv_cm1
        sigma_q2 = (dq * dq).sum(-1, keepdims=True) * inv_cm1
        sigma_k2 = (dk * dk).sum(-1, keepdims=True) * inv_cm1
        num = (2 * mu_q * mu_k + c1) * (2 * sigma_qk + c2)
        den = (mu_q ** 2 + mu_k ** 2 + c1) * (sigma_q2 + sigma_k2 + c2)
        attn_base = ((num / (den + 1e-07)) ** 2)[..., 0]
        steps = 2
        ts = jnp.linspace(0.0, 1.0, steps)
        dts = ts[1:] - ts[:-1]

        def step(A, dt):
            return (A + dt * _ode_func(A, conv1_w, gn_g, gn_b, conv2_w, conv2_b), None)
        A, _ = lax.scan(step, attn_base, dts)
        final_a = jax.nn.sigmoid(A)
        weights = jax.nn.softmax(final_a, axis=1)
        m = x.mean(axis=1, keepdims=True)
        ch_w = jax.nn.sigmoid(jax.nn.relu(m @ ch_w1 + ch_b1) @ ch_w2 + ch_b2)
        out_low = weights[..., None] * v * ch_w
        return out_low @ proj_w + proj_b

    def _L1_ffn_ref(x, shared_w1, shared_w2, expert_w1, expert_w2, router_w, ln_gamma, ln_beta):
        import jax, jax.numpy as jnp
        import numpy as np
        D_MODEL = 256
        EXPERT_DIM = 512
        N_EXPERTS = 8
        LN_EPS = 1e-05

        def _bit_quant(W):
            scale = jnp.clip(jnp.mean(jnp.abs(W), axis=-1, keepdims=True), 1e-05, None)
            w_q = jnp.clip(jnp.round(W / scale), -1.0, 1.0) * scale
            return W + jax.lax.stop_gradient(w_q - W)
        mu = jnp.mean(x, axis=-1, keepdims=True)
        var = jnp.mean(jnp.square(x - mu), axis=-1, keepdims=True)
        h = (x - mu) / jnp.sqrt(var + LN_EPS) * ln_gamma + ln_beta
        sw1, sw2 = (_bit_quant(shared_w1), _bit_quant(shared_w2))
        shared_out = jax.nn.silu(jnp.einsum('btd,fd->btf', h, sw1)) @ sw2.T
        probs = jax.nn.softmax(h @ router_w.T, axis=-1)
        top_prob = jnp.max(probs, axis=-1)
        top_idx = jnp.argmax(probs, axis=-1)
        ew1, ew2 = (_bit_quant(expert_w1), _bit_quant(expert_w2))
        h1 = jax.nn.silu(jnp.einsum('btd,efd->ebtf', h, ew1))
        eo = jnp.einsum('ebtf,edf->ebtd', h1, ew2)
        gate = jax.nn.one_hot(top_idx, N_EXPERTS, dtype=h.dtype) * top_prob[..., None]
        routed_out = jnp.einsum('ebtd,bte->btd', eo, gate)
        return shared_out + routed_out
    x = L0_attn_x
    x = _layernorm(x + _L0_attn_ref(x, L0_attn_w_q, L0_attn_b_q, L0_attn_w_k, L0_attn_b_k), axis=-1)
    x = _layernorm(x + _L0_ffn_ref(x, L0_ffn_weight), axis=-1)
    x = _layernorm(x + _L1_attn_ref(x, L1_attn_qkv_w, L1_attn_c1, L1_attn_c2, L1_attn_conv1_w, L1_attn_gn_g, L1_attn_gn_b, L1_attn_conv2_w, L1_attn_conv2_b, L1_attn_ch_w1, L1_attn_ch_b1, L1_attn_ch_w2, L1_attn_ch_b2, L1_attn_proj_w, L1_attn_proj_b), axis=-1)
    x = _layernorm(x + _L1_ffn_ref(x, L1_ffn_shared_w1, L1_ffn_shared_w2, L1_ffn_expert_w1, L1_ffn_expert_w2, L1_ffn_router_w, L1_ffn_ln_gamma, L1_ffn_ln_beta), axis=-1)
    return x

_drawn_inputs = setup_inputs


def setup_inputs(seed=0):
    import zlib

    import numpy as np

    out = dict(_drawn_inputs(seed))
    spreads = {'L1_attn_gn_g': (1.0, 0.6),
     'L1_attn_gn_b': (0.0, 2.0),
     'L1_attn_ch_b1': (0.0, 2.0),
     'L1_attn_ch_b2': (0.0, 2.0),
     'L1_attn_proj_b': (0.0, 0.1),
     'L1_ffn_ln_gamma': (1.0, 0.2),
     'L1_ffn_ln_beta': (0.0, 0.291)}
    factors = {'L0_attn_b_q': 23.965,
     'L0_attn_b_k': 64.0,
     'L1_attn_qkv_w': 55.594,
     'L1_attn_conv1_w': 64.0,
     'L1_attn_conv2_w': 64.0,
     'L1_attn_ch_w1': 64.0,
     'L1_attn_ch_w2': 64.0,
     'L1_attn_proj_w': 56.645}
    for name, (base, spread) in spreads.items():
        noise = np.random.default_rng([zlib.crc32(name.encode()), seed]).standard_normal(out[name].shape)
        drawn = base * np.exp(spread * noise) if base else spread * noise
        out[name] = jnp.asarray(drawn.astype(out[name].dtype))
    for name, factor in factors.items():
        out[name] = (out[name] * factor).astype(out[name].dtype)
    return out
```

```python
import numpy as np

import concourse.bass as bass
from concourse import mybir
from contextlib import ExitStack

F32 = mybir.dt.float32
F32R = mybir.dt.float32r
F16 = mybir.dt.float16
BF16 = mybir.dt.bfloat16
I32 = mybir.dt.int32
ALU = mybir.AluOpType
ACT = mybir.ActivationFunctionType
AX = mybir.AxisListType

P = 128
B, SEQ, D = 16, 512, 256
TOK = B * SEQ
NT = SEQ // P
NTILE = TOK // P
DC = D // P
QK = 16
RED = D // 4
FF = 512
FC = FF // P
NE = 8
CH = 4
TAPS = 3
GB = 4
GC = GB * NT
SLOT = 256
NG = (TOK + NE * (SLOT - 1)) // SLOT
NST = NG * SLOT // P
REC = 2 * D + 2
LN_EPS = 1e-5
HELD = 3
FSKEW = GB + 2
RNE = 12582912.0
NEG = -1e30
BANK = 512


class Steps:

    def __init__(self, nc, ctx):
        self.nc, self.ctx = nc, ctx
        self.engines = {"pe": nc.tensor, "act": nc.scalar, "dve": nc.vector, "pool": nc.gpsimd, "sp": nc.sync}
        self.sems, self.count, self.at, self.seen = {}, {}, {}, {}

    def sem(self, name):
        if name not in self.sems:
            self.sems[name] = self.ctx.enter_context(self.nc.semaphore(name))
            self.count[name] = 0
        return self.sems[name]

    def done(self, eng, ins, *key):
        ins.then_inc(self.sem("s_" + eng), 1)
        self.count["s_" + eng] += 1
        self.at[key] = ("s_" + eng, self.count["s_" + eng])

    def moved(self, ins, lane, *key):
        ins.then_inc(self.sem("d_" + lane), 16)
        self.count["d_" + lane] += 16
        self.at[key] = ("d_" + lane, self.count["d_" + lane])

    def need(self, eng, *keys):
        for key in keys:
            name, value = self.at[key]
            if self.seen.get((eng, name), 0) < value:
                self.engines[eng].wait_ge(self.sems[name], value)
                self.seen[eng, name] = value


def build_program(nc, t):
    ctx = ExitStack()
    with ctx:
        program(nc, t, ctx)


def program(nc, t, ctx):
    pe, act, dve, pool, sp = nc.tensor, nc.scalar, nc.vector, nc.gpsimd, nc.sync
    st = Steps(nc, ctx)
    done, need, moved = st.done, st.need, st.moved

    start = -(-nc.sbuf_base // 64) * 64
    here = [start]

    def sb(name, shape, dt=F32):
        size = 4 if dt in (F32, F32R, I32) else 2
        for d in shape[1:]:
            size *= d
        at = here[0]
        here[0] = -(-(at + size) // 64) * 64
        assert here[0] <= nc.sbuf_usable_end, (name, here[0])
        return nc.alloc_sbuf_tensor_at(name, list(shape), dt, offset=at, align_bytes=32)

    def ring(name, n, shape, dt=F32):
        return [sb(f"{name}{i}", shape, dt) for i in range(n)]

    banks = [ctx.enter_context(nc.psum_tensor(f"bank{i}", [P, BANK], F32)) for i in range(8)]
    turn = [0]
    readers = [[] for _ in banks]
    kept = []

    def take():
        i = turn[0] % len(banks)
        if i in kept:
            i = (i + 1) % len(banks)
            turn[0] += 1
        turn[0] += 1
        need("pe", *readers[i])
        readers[i] = []
        return banks[i], readers[i]

    rec = nc.dram_tensor("rec", [TOK + 1, REC], F32)

    ident = sb("ident", [P, P])
    ident16 = sb("ident16", [P, P], F16)
    identb = sb("identb", [P, P], BF16)
    maskb = sb("maskb", [P, P], BF16)
    ones = sb("ones", [P, P])
    onesb = sb("onesb", [P, P], BF16)
    before = sb("before", [P, P], BF16)
    from_prev = sb("from_prev", [P, P])
    from_next = sb("from_next", [P, P])
    edge_prev = sb("edge_prev", [P, P])
    edge_next = sb("edge_next", [P, P])
    mhalf = sb("mhalf", [P, GC])
    iota_f = sb("iota_f", [P, P])
    part_i = sb("part_i", [P, 1], I32)
    desc8 = sb("desc8", [P, NE])
    tile_f = sb("tile_f", [P, NTILE])

    iota_i, tile_i = iota_f[:].bitcast(I32), tile_f[:].bitcast(I32)
    n = [0]

    def pool_chain(ins):
        n[0] += 1
        done("pool", ins, "const", n[0])
        need("pool", ("const", n[0]))

    for m, v in ((ident, 0.0), (ident16, 0.0), (identb, 0.0), (maskb, 0.0), (ones, 1.0), (onesb, 1.0),
                 (before, 0.0), (from_prev, 0.0), (from_next, 0.0), (edge_prev, 0.0), (edge_next, 0.0),
                 (mhalf, -0.5)):
        ins = pool.memset(m[:], v)
    pool_chain(ins)
    for m, base in ((ident, 0), (ident16, 0), (identb, 0), (from_prev, 1), (from_next, -1),
                    (edge_prev, -(P - 1)), (edge_next, P - 1)):
        ins = pool.affine_select(out=m[:], in_=m[:], compare_op=ALU.not_equal, fill=1.0, base=base,
                                 pattern=[[-1, P]], channel_multiplier=1)
    pool.affine_select(out=maskb[:], in_=maskb[:], compare_op=ALU.is_ge, fill=NEG, base=0,
                       pattern=[[-1, P]], channel_multiplier=1)
    pool.affine_select(out=before[:], in_=before[:], compare_op=ALU.is_ge, fill=1.0, base=0,
                       pattern=[[-1, P]], channel_multiplier=1)
    pool.iota(iota_i, pattern=[[1, P]], base=0, channel_multiplier=0)
    pool.iota(tile_i, pattern=[[1, NTILE]], base=-NTILE, channel_multiplier=0)
    pool_chain(pool.iota(part_i[:], pattern=[[0, 1]], base=0, channel_multiplier=1))
    pool.tensor_copy(iota_f[:], iota_i)
    pool_chain(pool.tensor_copy(tile_f[:], tile_i))
    done("pool", pool.tensor_scalar(desc8[:], iota_f[:, 0:NE], -1.0, float(NE), ALU.mult, ALU.add), "consts")

    wqk = sb("wqk", [P, DC, P])
    bqk = sb("bqk", [P, 1])
    pw = sb("pw", [P, DC, D])
    cw1 = sb("cw1", [P, DC, RED])
    cb1 = sb("cb1", [RED, 1])
    cw2 = sb("cw2", [RED, D])
    cb2 = sb("cb2", [P, DC])
    pb_row = sb("pb_row", [P, D])
    gam = sb("gam", [P, D])
    bet = sb("bet", [P, D])
    cc = sb("cc", [P, 2])
    c1w = sb("c1w", [P, CH * TAPS])
    c2w = sb("c2w", [P, CH * TAPS])
    gng = sb("gng", [P, CH])
    gnb = sb("gnb", [P, CH])
    c2b = sb("c2b", [P, 1])
    rw = sb("rw", [P, DC, NE])

    W0T = sb("W0T", [P, DC, D], F32R)
    sc0 = sb("sc0", [P, 1])
    WCh = sb("WCh", [P, DC, 2 * D], F32R)
    WCl = sb("WCl", [P, DC, 2 * D], F32R)
    WVh = sb("WVh", [P, DC, D], F32R)
    WVl = sb("WVl", [P, DC, D], F32R)
    RW3 = sb("RW3", [P, DC, 3, NE], BF16)
    E1T = sb("E1T", [P, NE + 1, DC, FF], F16)
    E2T = sb("E2T", [P, NE + 1, FC, D], F16)
    e1s = sb("e1s", [P, NE + 1, FC])
    e2s = sb("e2s", [P, NE + 1, D])
    hup = sb("hup", [P, 1])
    hdn = sb("hdn", [P, 1])
    sdn = sb("sdn", [P, 1])
    sup = sb("sup", [P, 1])
    esc = sb("esc", [P, 2, FC])
    esr = sb("esr", [P, 2, FC])
    rne = sb("rne", [P, 1])
    hbound = sb("hbound", [P, 1])
    smax = sb("smax", [P, NE + 2])
    wsum = sb("wsum", [P, 4])
    tmp2 = sb("tmp2", [P, 8])

    NM = ring("NM", 2, [P, NT])
    RS = ring("RS", 2, [P, NT])
    RI = ring("RI", 2, [P, NT])
    bst = sb("bst", [P, NT, 6])
    mv = ring("mv", 4, [P, NT, 2])
    rstd = ring("rstd", 4, [P, NT])
    SUMS = ring("SUMS", 2, [P, DC])
    R1 = sb("R1", [RED, 1])
    CHW = sb("CHW", [P, DC])
    junk_a = sb("junk_a", [P, FF], BF16)
    S2 = ring("S2", 2, [P, GC])
    SQK = ring("SQK", 2, [P, GC])
    WT = ring("WT", 2, [P, GB, NT])
    OH = sb("OH", [P, NTILE, NE], BF16)
    GATE = sb("GATE", [P, NTILE])
    ids = sb("ids", [P, NST], I32)
    q_exi = sb("q_exi", [P, NG], I32)
    group_first = sb("group_first", [P, NG])

    NX2 = FSKEW - 1
    X2 = ring("X2", NX2, [P, NT, D])

    late_start = here[0]
    HT = [sb("HT0", [P, 2, DC, SEQ], F16)]
    HN = sb("HN", [P, NT, D])
    H16 = sb("H16", [P, NT, 2, D], F16)
    S = ring("S", 2, [P, SEQ])
    Sh = sb("Sh", [P, FC, SEQ], F16)
    Sl = sb("Sl", [P, FC, SEQ], F16)
    R = sb("R", [P, NT, D + 2])
    late_end = here[0]

    here[0] = late_start
    w0 = sb("w0", [P, DC, D])
    wall = sb("wall", [P, DC, 3 * D])
    wvT = sb("wvT", [P, DC, D])
    e1n = sb("e1n", [P, FC, D])
    e2n = sb("e2n", [P, DC, FF])
    e1q = sb("e1q", [P, FC, D], F16)
    e2q = sb("e2q", [P, DC, FF], F16)
    dg = sb("dg", [P, DC, P])
    assert here[0] <= late_end

    here[0] = late_end
    U = ring("U", 4, [P, NT, D + 2])
    front_start = here[0]
    X = ring("X", 2, [P, NT, D])
    XT = sb("XT", [P, DC, SEQ])
    Xh = sb("Xh", [P, NT, D], F32R)
    Xl = sb("Xl", [P, NT, D], F32R)
    Qs = sb("Qs", [P, SEQ], F32R)
    KH = sb("KH", [P, SEQ], F32R)
    KL = sb("KL", [P, SEQ], F32R)
    OFF = [P * i * (i + 1) // 2 for i in range(NT + 1)]
    PB = sb("PB", [P, OFF[NT]])
    PTh = sb("PTh", [P, OFF[NT]], F32R)
    PTl = sb("PTl", [P, OFF[NT]], F32R)
    X1 = sb("X1", [P, NT, D])
    TTh = sb("TTh", [P, DC, SEQ], F32R)
    TTl = sb("TTl", [P, DC, SEQ], F32R)
    PSh = sb("PSh", [P, DC, D], F32R)
    PSl = sb("PSl", [P, DC, D], F32R)
    Mh = sb("Mh", [P, DC, D + 2], F32R)
    Ml = sb("Ml", [P, DC, D + 2], F32R)
    DK = sb("DK", [P, D])
    front_end = here[0]

    here[0] = front_start
    HT += [sb(f"HT{k}", [P, 2, DC, SEQ], F16) for k in range(1, HELD)]
    q_C = sb("q_C", [P, NE, NTILE])
    q_tot = sb("q_tot", [P, NE, NTILE])
    q_z = sb("q_z", [P, NTILE])
    q_n = sb("q_n", [P, NE])
    q_ni = sb("q_ni", [P, NE], I32)
    q_end = sb("q_end", [P, NE])
    q_pos = sb("q_pos", [P, NTILE])
    q_i = sb("q_i", [P, NTILE], I32)
    q_lo = sb("q_lo", [P, NTILE])
    q_hi = sb("q_hi", [P, NTILE])
    CHK = 4
    q_A = ring("q_A", 2, [P, CHK, P], BF16)
    q_B = ring("q_B", 2, [P, CHK, 2, NST], BF16)
    part_f = sb("part_f", [P, 1])
    ids_f = sb("ids_f", [P, NST])
    q_ge = sb("q_ge", [P, NE, NG])
    q_ex = sb("q_ex", [P, NG])
    NGT = SLOT // P
    G_rec = ring("G_rec", 3, [P, NGT, REC])
    G_T = ring("G_T", 2, [P, 2, DC, SLOT], F16)
    G_S = ring("G_S", 2, [P, FC, SLOT])
    G_Sh = ring("G_Sh", 2, [P, FC, SLOT], F16)
    G_Sl = ring("G_Sl", 2, [P, FC, SLOT], F16)
    G_y = ring("G_y", 3, [P, NGT, D])
    assert here[0] <= front_end, (here[0], front_end, front_start, late_end, late_start, nc.sbuf_usable_end)
    here[0] = front_end
    small = [
        (wqk[:], t["wqk"].rearrange("(c p) m -> p c m", p=P)), (bqk[:], t["bqk"]),
        (w0[:], t["w0"].rearrange("(c p) i -> p c i", p=P)),
        (wall[:], t["wall"].rearrange("(c p) n -> p c n", p=P)),
        (wvT[:], t["wvT"].rearrange("(c p) n -> p c n", p=P)),
        (pw[:], t["pw"].rearrange("(c p) n -> p c n", p=P)),
        (cw1[:], t["cw1"].rearrange("(c p) n -> p c n", p=P)), (cb1[:], t["cb1"]), (cw2[:], t["cw2"]),
        (cb2[:], t["cb2"]), (pb_row[:], t["pb"].to_broadcast([P, D])), (gam[:], t["gam"].to_broadcast([P, D])),
        (bet[:], t["bet"].to_broadcast([P, D])), (cc[:], t["cc"].to_broadcast([P, 2])),
        (c1w[:], t["c1w"].to_broadcast([P, CH * TAPS])), (c2w[:], t["c2w"].to_broadcast([P, CH * TAPS])),
        (gng[:], t["gng"].to_broadcast([P, CH])), (gnb[:], t["gnb"].to_broadcast([P, CH])),
        (c2b[:], t["c2b"].to_broadcast([P, 1])), (rw[:], t["rw"].rearrange("(c p) e -> p c e", p=P)),
    ]
    for i, (dst, src) in enumerate(small):
        with nc.allow_non_contiguous_dma(reason="small weights, once"):
            moved((sp, act)[i % 2].dma_start(dst, src), "small", "small", i)
    st.at["small"] = st.at["small", len(small) - 1]
    st.at[("small",)] = st.at[("small", len(small) - 1)]

    chain = [0]

    def vstep(ins):
        chain[0] += 1
        done("dve", ins, "v", chain[0])
        need("dve", ("v", chain[0]))

    xv = t["x"].rearrange("(b j p) d -> b p j d", j=NT, p=P)
    xTv = t["xT"].rearrange("(c p) (b n) -> b p c n", p=P, n=SEQ)

    def load_x(b):
        if b >= 2:
            need("sp", ("x1", b - 2, NT - 1), ("Xl", b - 2))
        moved(sp.dma_start(X[b % 2][:], xv[b]), f"x{b % 2}", "X", b)

    def load_xT(b):
        if b >= 1:
            need("sp", ("proj", b - 1))
        moved(sp.dma_start(XT[:], xTv[b]), "xT", "XT", b)

    need("dve", ("small",), ("consts",))
    need("act", ("small",), ("consts",))
    need("pe", ("small",), ("consts",))
    need("pool", ("small",))
    for m in (Qs, KH, KL):
        vstep(dve.memset(m[:].bitcast(F32), 0.0))
    vstep(dve.tensor_scalar(wqk[:, :, 0:64], wqk[:, :, 0:64], QK ** -0.5, None, ALU.mult))
    vstep(dve.tensor_scalar(bqk[0:64, :], bqk[0:64, :], QK ** -0.5, None, ALU.mult))
    zeros = junk_a[:].bitcast(F32)
    done("dve", dve.memset(zeros, 0.0), "zeros")
    vstep(dve.tensor_reduce(wsum[:, 0:1], w0[:], AX.XY, ALU.add, apply_absolute_value=True))
    need("pe", ("v", chain[0]))
    bk, rd = take()
    done("pe", pe.matmul(bk[:, 0:1], ones[:], wsum[:, 0:1], start=True, stop=True), "w0sum")
    need("dve", ("w0sum",))
    vstep(dve.tensor_scalar(sc0[:], bk[:, 0:1], 1.0 / (D * D), 1e-5, ALU.mult, ALU.max))
    rd.append(("v", chain[0]))
    vstep(dve.reciprocal(wsum[:, 1:2], sc0[:]))
    vstep(dve.tensor_scalar(w0[:], w0[:], wsum[:, 1:2], RNE, ALU.mult, ALU.add))
    vstep(dve.tensor_scalar(w0[:], w0[:], RNE + 1.0, RNE - 1.0, ALU.min, ALU.max))
    vstep(dve.tensor_scalar(w0[:], w0[:], RNE, None, ALU.subtract))
    need("pe", ("v", chain[0]))
    bk, rd = take()
    for c in range(DC):
        for o in range(DC):
            last = pe.transpose(bk[:, c * D + o * P:c * D + (o + 1) * P], w0[:, o, c * P:(c + 1) * P], ident[:])
    done("pe", last, "w0T")
    need("act", ("w0T",))
    done("act", act.activation(W0T[:], bk[:].rearrange("p (c o) -> p c o", c=DC), ACT.Copy), "W0T")
    rd.append(("W0T",))
    for c in range(DC):
        for s in range(2):
            part = wall[:, c, s * D:(s + 1) * D]
            vstep(dve.tensor_reduce(tmp2[:, 2 * c + s:2 * c + s + 1], part, AX.X, ALU.add))
            vstep(dve.tensor_scalar(tmp2[:, 2 * c + s:2 * c + s + 1], tmp2[:, 2 * c + s:2 * c + s + 1], 1.0 / D, None, ALU.mult))
            vstep(dve.tensor_scalar(part, part, tmp2[:, 2 * c + s:2 * c + s + 1], None, ALU.subtract))
        vstep(dve.tensor_copy(Mh[:, c, D:D + 2], tmp2[:, 2 * c:2 * c + 2]))
        vstep(dve.tensor_tensor(Ml[:, c, D:D + 2], tmp2[:, 2 * c:2 * c + 2], Mh[:, c, D:D + 2].bitcast(F32), ALU.subtract))
    vstep(dve.tensor_copy(WCh[:], wall[:, :, 0:2 * D]))
    vstep(dve.tensor_tensor(WCl[:], wall[:, :, 0:2 * D], WCh[:].bitcast(F32), ALU.subtract))
    vstep(dve.tensor_copy(WVh[:], wvT[:]))
    vstep(dve.tensor_tensor(WVl[:], wvT[:], WVh[:].bitcast(F32), ALU.subtract))
    rwv = rw
    for k in range(3):
        vstep(dve.tensor_copy(RW3[:, :, k, :], rwv[:]))
        if k < 2:
            vstep(dve.tensor_tensor(rwv[:], rwv[:], RW3[:, :, k, :], ALU.subtract))
    vstep(dve.tensor_reduce(tmp2[:, 0:1], gam[:], AX.X, ALU.max, apply_absolute_value=True))
    vstep(dve.tensor_reduce(tmp2[:, 1:2], bet[:], AX.X, ALU.max, apply_absolute_value=True))
    vstep(dve.tensor_scalar(tmp2[:, 2:3], tmp2[:, 0:1], D ** 0.5, 1e-20, ALU.mult, ALU.add))
    vstep(dve.tensor_tensor(tmp2[:, 2:3], tmp2[:, 2:3], tmp2[:, 1:2], ALU.add))
    vstep(dve.tensor_scalar(hdn[:].bitcast(I32), tmp2[:, 2:3].bitcast(I32), 0x7F800000, None, ALU.bitwise_and))
    H_TOP = 2.0 ** 13
    vstep(dve.tensor_scalar(hdn[:], hdn[:], 1.0 / H_TOP, None, ALU.mult))
    vstep(dve.reciprocal(hup[:], hdn[:]))
    vstep(dve.tensor_scalar(gam[:], gam[:], hup[:], None, ALU.mult))
    vstep(dve.tensor_scalar(bet[:], bet[:], hup[:], None, ALU.mult))
    vstep(dve.tensor_copy(hbound[:], tmp2[:, 2:3]))
    done("dve", dve.memset(smax[:], 0.0), "setup")
    need("dve", ("setup",))

    need("sp", ("zeros",))
    zr = rec[TOK:TOK + 1, :]
    moved(sp.dma_start(zr[:, 0:D], zeros[0:1, :]), "zero", "zero", 0)
    moved(sp.dma_start(zr[:, D:2 * D], zeros[0:1, :]), "zero", "zero", 1)
    moved(sp.dma_start(zr[:, 2 * D:REC], zeros[0:1, 0:REC - 2 * D]), "zero", "zero", 2)


    def expert(e):
        w1 = t["sw1"] if e == NE else t["ew1"][e]
        w2 = t["sw2"] if e == NE else t["ew2"][e]
        key = ("expert", e)
        if ("eq1",) in st.at:
            need("sp", ("eq1",), ("eq2",))
        moved(sp.dma_start(e1n[:], w1.rearrange("(c p) d -> p c d", p=P)), "e1n", "e1n", e)
        moved(sp.dma_start(e2n[:], w2.rearrange("(c p) f -> p c f", p=P)), "e2n", "e2n", e)
        for which, nat, q, nch, width, name in ((0, e1n, e1q, FC, D, "e1n"), (1, e2n, e2q, DC, FF, "e2n")):
            need("dve", (name, e))
            sc = esc[:, which, 0:nch]
            if ("dg",) in st.at:
                need("dve", ("dg",))
            vstep(dve.tensor_reduce(sc, nat[:], AX.X, ALU.add, apply_absolute_value=True))
            vstep(dve.tensor_scalar(sc, sc, 1.0 / width, 1e-5, ALU.mult, ALU.max))
            rs = esr[:, which, 0:nch]
            vstep(dve.reciprocal(rs, sc))
            need("act", ("v", chain[0]))
            for c in range(nch):
                last = act.activation(nat[:, c, :], nat[:, c, :], ACT.Identity, bias=rne[:, 0:1], scale=rs[:, c:c + 1])
            done("act", last, "eround")
            need("dve", ("eround",))
            vstep(dve.tensor_scalar(nat[:], nat[:], RNE + 1.0, RNE - 1.0, ALU.min, ALU.max))
            if (f"et{which}",) in st.at:
                need("dve", (f"et{which}",))
            vstep(dve.tensor_scalar(q[:], nat[:], RNE, None, ALU.subtract))
            st.at[(f"eq{which + 1}",)] = st.at[("v", chain[0])]
            need("pe", ("v", chain[0]))
            bk, rd = take()
            b16 = bk[:].bitcast(F16)
            for c in range(width // P):
                for f in range(nch):
                    o = c * nch * P + f * P
                    last = pe.transpose(b16[:, o:o + P], q[:, f, c * P:(c + 1) * P], ident16[:])
            done("pe", last, f"et{which}")
            need("act", (f"et{which}",))
            dst = (E1T, E2T)[which][:, e, :, :]
            done("act", act.activation(dst, b16[:, 0:width // P * nch * P].rearrange("p (c m) -> p c m", m=nch * P), ACT.Copy), "ET", which, e)
            rd.append(("ET", which, e))
        vstep(dve.tensor_scalar(e1s[:, e, :], esc[:, 0, :], hdn[:], None, ALU.mult))
        vstep(dve.tensor_reduce(smax[:, e:e + 1], esc[:, 0, :], AX.X, ALU.max))
        for c in range(DC):
            vstep(dve.tensor_scalar(dg[:, c, :], ident[:], esc[:, 1, c:c + 1], None, ALU.mult))
        need("pe", ("v", chain[0]))
        bk, rd = take()
        for c in range(DC):
            last = pe.matmul(bk[:, c * P:(c + 1) * P], ones[:], dg[:, c, :], start=True, stop=True)
        done("pe", last, "dg")
        need("act", ("dg",))
        done("act", act.activation(e2s[:, e, :], bk[:, 0:D], ACT.Copy), "e2s", e)
        rd.append(("e2s", e))

    vstep(dve.memset(rne[:], RNE))

    def guards():
        vstep(dve.tensor_reduce(smax[:, NE + 1:NE + 2], smax[:, 0:NE + 1], AX.X, ALU.max))
        need("pe", ("v", chain[0]))
        bk, rd = take()
        done("pe", pe.transpose(bk[0:1, 0:P], smax[:, NE + 1:NE + 2], ident[:]), "smaxT")
        need("dve", ("smaxT",))
        vstep(dve.tensor_reduce(tmp2[0:1, 4:5], bk[0:1, 0:P], AX.X, ALU.max))
        rd.append(("v", chain[0]))
        vstep(dve.tensor_scalar(tmp2[0:1, 4:5], tmp2[0:1, 4:5], hbound[0:1, :], float(D), ALU.mult, ALU.mult))
        need("pe", ("v", chain[0]))
        bk, rd = take()
        done("pe", pe.matmul(bk[:, 0:1], ones[0:1, :], tmp2[0:1, 4:5], start=True, stop=True), "sbound")
        need("dve", ("sbound",))
        vstep(dve.tensor_copy(tmp2[:, 5:6], bk[:, 0:1]))
        rd.append(("v", chain[0]))
        vstep(dve.tensor_scalar(sup[:].bitcast(I32), tmp2[:, 5:6].bitcast(I32), 0x7F800000, None, ALU.bitwise_and))
        vstep(dve.tensor_scalar(sup[:], sup[:], 2.0 ** -13, None, ALU.mult))
        vstep(dve.reciprocal(sdn[:], sup[:]))
        need("dve", ("e2s", 0))
        vstep(dve.tensor_scalar(e2s[:], e2s[:], sup[:], None, ALU.mult))
        st.at[("guards",)] = st.at[("v", chain[0])]

    def ln_stats(x, which, b, j):
        done("dve", dve.bn_stats(bst[:, j, :], x), "bn", which, b, j)
        need("dve", ("bn", which, b, j))
        done("dve", dve.bn_aggr(mv[which][:, j, :], bst[:, j, :]), "mv", which, b, j)

    def ln_root(which, b, j0=0, j1=NT):
        need("pool", ("mv", which, b, j1 - 1))
        r = rstd[which][:, j0:j1]
        done("pool", pool.tensor_scalar(r, mv[which][:, j0:j1, 1], 1.0, LN_EPS, ALU.mult, ALU.add), "veps", which, b)
        need("pool", ("veps", which, b))
        done("pool", pool.tensor_tensor(r, r, mhalf[:, j0:j1], ALU.pow), "rstd", which, b)

    def ln_apply(out, x, which, b, j):
        need("dve", ("rstd", which, b), ("mv", which, b, j))
        return dve.tensor_scalar(out, x, mv[which][:, j, 0:1], rstd[which][:, j:j + 1], ALU.subtract, ALU.mult)

    def a1_split(b):
        need("act", ("X", b))
        if b >= 1:
            need("act", ("pv", b - 1, NT - 1))
        done("act", act.activation(Xh[:], X[b % 2][:], ACT.Copy), "Xh", b)
        need("pool", ("Xh", b))
        done("pool", pool.tensor_tensor(Xl[:], X[b % 2][:], Xh[:].bitcast(F32), ALU.subtract), "Xl", b)

    def a2_project(b):
        need("pe", ("XT", b))
        bk, rd = take()
        for c in range(DC):
            last = pe.matmul(bk[:], wqk[:, c, :], XT[:, c, :], start=c == 0, stop=c == DC - 1)
        done("pe", last, "proj", b)
        need("act", ("proj", b))
        if b >= 1:
            need("act", ("score", b - 1, NT - 1))
        act.activation(Qs[0:64, :], bk[0:64, :], ACT.Identity, bias=bqk[0:64, :])
        done("act", act.activation(KH[0:64, :], bk[64:128, :], ACT.Identity, bias=bqk[64:128, :]), "qkhi", b)
        need("dve", ("qkhi", b))
        dve.scalar_tensor_tensor(Qs[32:64, :], bk[32:64, :], bqk[32:64, :], Qs[32:64, :].bitcast(F32),
                                 ALU.add, ALU.subtract)
        done("dve", dve.scalar_tensor_tensor(KL[0:64, :], bk[64:128, :], bqk[64:128, :],
                                             KH[0:64, :].bitcast(F32), ALU.add, ALU.subtract), "qklo", b)
        rd.append(("qklo", b))

    def b1_scores(b):
        need("pe", ("qklo", b))
        for i in range(NT):
            w = (i + 1) * P
            bk, rd = take()
            q = Qs[:, i * P:(i + 1) * P]
            pe.matmul(bk[:, 0:w], q, KH[:, 0:w], start=True, stop=False)
            pe.matmul(bk[:, 0:w], q, KL[:, 0:w], start=False, stop=False)
            done("pe", pe.matmul(bk[:, i * P:w], identb[:], maskb[:], start=False, stop=True), "score", b, i)
            need("dve", ("score", b, i))
            done("dve", dve.tensor_reduce(NM[b % 2][:, i:i + 1], bk[:, 0:w], AX.X, ALU.max, negate=True), "max", b, i)
            need("act", ("max", b, i))
            if b >= 1 and i == 0:
                need("act", ("pT", b - 1, NT - 1))
            done("act", act.activation(PB[:, OFF[i]:OFF[i + 1]], bk[:, 0:w], ACT.Exp, bias=NM[b % 2][:, i:i + 1],
                                       accum_out=RS[b % 2][:, i:i + 1]), "exp", b, i)
            rd.append(("exp", b, i))

    def b2_transpose(b):
        for i in range(NT):
            need("pe", ("exp", b, i))
            bk, rd = take()
            for k in range(i + 1):
                last = pe.transpose(bk[:, k * P:(k + 1) * P], PB[:, OFF[i] + k * P:OFF[i] + (k + 1) * P], ident[:])
            done("pe", last, "pT", b, i)
            need("act", ("pT", b, i))
            if b >= 1 and i == 0:
                need("act", ("pv", b - 1, NT - 1))
            o = slice(OFF[i], OFF[i + 1])
            done("act", act.activation(PTh[:, o], bk[:, 0:(i + 1) * P], ACT.Copy), "pTh", b, i)
            need("dve", ("pTh", b, i))
            done("dve", dve.tensor_tensor(PTl[:, o], bk[:, 0:(i + 1) * P], PTh[:, o].bitcast(F32), ALU.subtract), "pTl", b, i)
            rd.append(("pTl", b, i))

    def b3_values(b):
        need("dve", ("exp", b, NT - 1))
        done("dve", dve.reciprocal(RI[b % 2][:], RS[b % 2][:]), "rinv", b)
        need("pe", ("Xl", b))
        for i in range(NT):
            need("pe", ("pTl", b, i))
            bk, rd = take()
            for k in range(i + 1):
                o = slice(OFF[i] + k * P, OFF[i] + (k + 1) * P)
                pe.matmul(bk[:, 0:D], PTh[:, o], Xh[:, k, :], start=k == 0, stop=False)
                pe.matmul(bk[:, 0:D], PTh[:, o], Xl[:, k, :], start=False, stop=False)
                last = pe.matmul(bk[:, 0:D], PTl[:, o], Xh[:, k, :], start=False, stop=k == i)
            done("pe", last, "pv", b, i)
            need("dve", ("pv", b, i), ("rinv", b))
            if b >= 1 and i == 0:
                need("dve", ("x1T", b - 1), ("x2", b - 1, NT - 1))
            x1 = X1[:, i, :]
            done("dve", dve.scalar_tensor_tensor(x1, bk[:, 0:D], RI[b % 2][:, i:i + 1], X[b % 2][:, i, :],
                                                 ALU.mult, ALU.add), "x1", b, i)
            rd.append(("x1", b, i))
            need("dve", ("x1", b, i))
            ln_stats(x1, 0, b, i)
        ln_root(0, b)
        for i in range(NT):
            x1 = X1[:, i, :]
            done("dve", ln_apply(x1, x1, 0, b, i), "x1n", b, i)

    def transposed(b, src, name, hi, lo, ready, reread, sums=None):
        for c in range(DC):
            bk, rd = take()
            for j in range(NT):
                if c == 0:
                    need("pe", (ready, b, j))
                last = pe.transpose(bk[:, j * P:(j + 1) * P], src[:, j, c * P:(c + 1) * P], ident[:])
            done("pe", last, name, b, c)
            need("act", (name, b, c))
            if reread in st.at:
                need("act", reread)
            extra = dict(accum_out=sums[:, c:c + 1]) if sums is not None else {}
            done("act", act.activation(hi[:, c, :], bk[:], ACT.Copy, **extra), name + "h", b, c)
            need("dve", (name + "h", b, c))
            done("dve", dve.tensor_tensor(lo[:, c, :], bk[:], hi[:, c, :].bitcast(F32), ALU.subtract), name + "l", b, c)
            rd.append((name + "l", b, c))
        st.at[(name, b)] = st.at[(name, b, DC - 1)]

    def c1_transpose(b):
        transposed(b, X1, "x1T", TTh, TTl, "x1n", ("u", b - 1))

    def c2_linear(b):
        x2 = X2[b % NX2]
        if b == 0:
            need("pe", ("W0T",))
        for j in range(NT):
            need("pe", ("x1Tl", b, DC - 1))
            bk, rd = take()
            for c in range(DC):
                pe.matmul(bk[:, 0:D], TTh[:, c, j * P:(j + 1) * P], W0T[:, c, :], start=c == 0, stop=False)
                last = pe.matmul(bk[:, 0:D], TTl[:, c, j * P:(j + 1) * P], W0T[:, c, :], start=False, stop=c == DC - 1)
            done("pe", last, "ffn", b, j)
            need("dve", ("ffn", b, j))
            if b >= NX2 and j == 0:
                need("dve", ("r", b - NX2))
            done("dve", dve.scalar_tensor_tensor(x2[:, j, :], bk[:, 0:D], sc0[:], X1[:, j, :], ALU.mult, ALU.add),
                 "x2", b, j)
            rd.append(("x2", b, j))
            need("dve", ("x2", b, j))
            ln_stats(x2[:, j, :], 1, b, j)
        st.at[("ffn", b)] = st.at[("ffn", b, NT - 1)]
        ln_root(1, b)
        for j in range(NT):
            done("dve", ln_apply(x2[:, j, :], x2[:, j, :], 1, b, j), "x2n", b, j)

    def d1_transpose(b):
        if b >= 2:
            need("act", ("gate1", b - 2))
        transposed(b, X2[b % NX2], "x2T", TTh, TTl, "x2n", ("ffn", b), sums=SUMS[b % 2])
        need("pool", ("x2T", b))
        done("pool", pool.tensor_tensor(X2[b % NX2][:], X2[b % NX2][:], pb_row[:, None, :].to_broadcast([P, NT, D]), ALU.add),
             "x2b", b)

    def d2_stats(b):
        g, col = b // GB, (b % GB) * NT
        need("pe", ("x2Tl", b, DC - 1), ("x2Th", b, DC - 1))
        bk, rd = take()
        for c in range(DC):
            last = pe.matmul(bk[0:RED, 0:1], cw1[:, c, :], SUMS[b % 2][:, c:c + 1], start=c == 0, stop=c == DC - 1)
        done("pe", last, "gate1", b)
        need("act", ("gate1", b))
        if b >= 1:
            need("act", ("gate2", b - 1))
        done("act", act.activation(R1[:], bk[0:RED, 0:1], ACT.Relu, bias=cb1[:], scale=1.0 / SEQ), "gate_r", b)
        rd.append(("gate_r", b))

        def tile(j):
            bk, rd = take()
            for c in range(DC):
                o = slice(j * P, (j + 1) * P)
                pe.matmul(bk[:], TTh[:, c, o], WCh[:, c, :], start=c == 0, stop=False)
                pe.matmul(bk[:], TTh[:, c, o], WCl[:, c, :], start=False, stop=False)
                last = pe.matmul(bk[:], TTl[:, c, o], WCh[:, c, :], start=False, stop=c == DC - 1)
            done("pe", last, "dqk", b, j)
            need("act", ("dqk", b, j))
            if last_qk[0]:
                need("act", last_qk[0])
            act.activation(DK[:], bk[:, D:2 * D], ACT.Copy)
            if g >= 2 and b % GB == 0 and j == 0:
                need("act", ("ode", g - 2))
            need("act", last_sq[0] or ("zero", 2))
            done("act", act.activation(junk_a[:], bk[:], ACT.Square, accum_out=S2[g % 2][:, col + j:col + j + 1]), "sq", b, j)
            last_sq[0] = ("sq", b, j)
            need("dve", ("sq", b, j))
            if last_qk[0]:
                need("dve", last_qk[0])
            done("dve", dve.tensor_tensor_reduce(out=bk[:, 0:D], in0=bk[:, 0:D], in1=DK[:], scale=1.0, scalar=0.0,
                                                 op0=ALU.mult, op1=ALU.add,
                                                 accum_out=SQK[g % 2][:, col + j:col + j + 1]), "sqk", b, j)
            last_qk[0] = ("sqk", b, j)
            rd.append(("sqk", b, j))

        tile(0)
        need("pe", ("gate_r", b))
        bk, rd = take()
        for c in range(DC):
            last = pe.matmul(bk[:, c:c + 1], cw2[:, c * P:(c + 1) * P], R1[:], start=True, stop=True)
        done("pe", last, "gate2", b)
        need("dve", ("gate2", b))
        if b >= 1:
            need("dve", ("psh", b - 1))
        vstep(dve.tensor_tensor(CHW[:], bk[:, 0:DC], cb2[:], ALU.add))
        rd.append(("v", chain[0]))
        vstep(dve.tensor_scalar(CHW[:], CHW[:], -80.0, None, ALU.max))
        need("act", ("v", chain[0]))
        done("act", act.activation(CHW[:], CHW[:], ACT.Exp, scale=-1.0), "gexp", b)
        tile(1)
        need("dve", ("gexp", b))
        vstep(dve.tensor_scalar(CHW[:], CHW[:], 1.0, None, ALU.add))
        vstep(dve.reciprocal(CHW[:], CHW[:]))
        need("act", ("v", chain[0]))
        if b >= 1:
            need("act", ("fuse", b - 1))
        for c in range(DC):
            last = act.activation(PSh[:, c, :], pw[:, c, :], ACT.Copy, scale=CHW[:, c:c + 1])
        done("act", last, "psh", b)
        tile(2)
        need("dve", ("psh", b))
        for c in range(DC):
            last = dve.scalar_tensor_tensor(PSl[:, c, :], pw[:, c, :], CHW[:, c:c + 1], PSh[:, c, :].bitcast(F32),
                                            ALU.mult, ALU.subtract)
        done("dve", last, "psl", b)
        st.at[("psh", b)] = st.at[("psl", b)]
        tile(3)
        need("pe", ("psl", b))
        bk, rd = take()
        for m in range(DC):
            for c in range(DC):
                o = slice(m * P, (m + 1) * P)
                pe.matmul(bk[:, m * D:(m + 1) * D], WVh[:, c, o], PSh[:, c, :], start=c == 0, stop=False)
                pe.matmul(bk[:, m * D:(m + 1) * D], WVh[:, c, o], PSl[:, c, :], start=False, stop=False)
                last = pe.matmul(bk[:, m * D:(m + 1) * D], WVl[:, c, o], PSh[:, c, :], start=False, stop=c == DC - 1)
        done("pe", last, "fuse", b)
        need("act", ("fuse", b))
        if b >= 1:
            need("act", ("u", b - 1))
        fused = bk[:].rearrange("p (m n) -> p m n", m=DC)
        done("act", act.activation(Mh[:, :, 0:D], fused, ACT.Copy), "Mh", b)
        need("dve", ("Mh", b))
        done("dve", dve.tensor_tensor(Ml[:, :, 0:D], fused, Mh[:, :, 0:D].bitcast(F32), ALU.subtract), "Ml", b)
        rd.append(("Ml", b))

    last_sq, last_qk = [None], [None]

    def d3_values(b):
        need("pe", ("Ml", b))
        for j in range(NT):
            bk, rd = take()
            for c in range(DC):
                o = slice(j * P, (j + 1) * P)
                pe.matmul(bk[:, 0:D + 2], TTh[:, c, o], Mh[:, c, :], start=c == 0, stop=False)
                pe.matmul(bk[:, 0:D + 2], TTh[:, c, o], Ml[:, c, :], start=False, stop=False)
                last = pe.matmul(bk[:, 0:D + 2], TTl[:, c, o], Mh[:, c, :], start=False, stop=c == DC - 1)
            done("pe", last, "u", b, j)
            need("act", ("u", b, j))
            if b >= 4 and j == 0:
                need("act", ("x3", b - 4, NT - 1))
            done("act", act.activation(U[b % 4][:, j, :], bk[:, 0:D + 2], ACT.Copy), "U", b, j)
            rd.append(("U", b, j))
        st.at[("u", b)] = st.at[("u", b, NT - 1)]

    o_mm = sb("o_mm", [P, GC])
    o_d1 = sb("o_d1", [P, GC])
    o_kk = sb("o_kk", [P, GC])
    o_n2 = sb("o_n2", [P, GC])
    o_A = sb("o_A", [P, GB, NT])
    o_h = sb("o_h", [P, 2, GB, 2, NT])
    o_sq = sb("o_sq", [P, 2, GB, 2, NT])
    o_mean = sb("o_mean", [P, 2 * GB])
    o_rs = sb("o_rs", [P, 2 * GB])
    o_t = sb("o_t", [P, TAPS, GB, NT])
    o_e = sb("o_e", [P, GB, NT])
    o_s = sb("o_s", [P, GB])

    def neighbours(out, prev, nxt, extra=None):
        o1, o2 = out
        pe.matmul(o1, from_prev[:], prev, start=True, stop=False)
        pe.matmul(o1[:, :, 1:NT], edge_prev[:], prev[:, :, 0:NT - 1], start=False, stop=extra is None)
        if extra is not None:
            pe.matmul(o1, ident[:], extra, start=False, stop=False)
        pe.matmul(o2, from_next[:], nxt, start=extra is None, stop=False)
        return pe.matmul(o2[:, :, 0:NT - 1], edge_next[:], nxt[:, :, 1:NT], start=False, stop=True)

    def ode(g):
        last_b = GB * g + GB - 1
        need("dve", *[("U", b, NT - 1) for b in range(GB * g, last_b + 1)], ("sqk", last_b, NT - 1), ("sq", last_b, NT - 1))
        for i in range(GB):
            b = GB * g + i
            mq, mk = U[b % 4][:, :, D], U[b % 4][:, :, D + 1]
            c = slice(i * NT, (i + 1) * NT)
            dve.tensor_tensor(o_mm[:, c], mq, mk, ALU.mult)
            dve.tensor_tensor(o_d1[:, c], mq, mq, ALU.mult)
            last = dve.tensor_tensor(o_kk[:, c], mk, mk, ALU.mult)
        vstep(last)
        c1, c2 = cc[:, 0:1], cc[:, 1:2]
        s2, sqk = S2[g % 2][:], SQK[g % 2][:]
        dve.tensor_scalar(o_mm[:], o_mm[:], 2.0, c1, ALU.mult, ALU.add)
        dve.scalar_tensor_tensor(o_d1[:], o_d1[:], c1, o_kk[:], ALU.add, ALU.add)
        dve.tensor_scalar(o_n2[:], sqk, 2.0 / (D - 1), c2, ALU.mult, ALU.add)
        vstep(dve.tensor_scalar(s2, s2, 1.0 / (D - 1), c2, ALU.mult, ALU.add))
        dve.tensor_tensor(o_mm[:], o_mm[:], o_n2[:], ALU.mult)
        vstep(dve.tensor_tensor(o_d1[:], o_d1[:], s2, ALU.mult))
        vstep(dve.tensor_scalar(o_d1[:], o_d1[:], 1e-7, None, ALU.add))
        vstep(dve.reciprocal(o_d1[:], o_d1[:]))
        vstep(dve.tensor_tensor(o_mm[:], o_mm[:], o_d1[:], ALU.mult))
        A = o_A[:].rearrange("p b j -> p (b j)")
        vstep(dve.tensor_tensor(A, o_mm[:], o_mm[:], ALU.mult))
        st.at[("ode", g)] = st.at[("v", chain[0])]
        need("pe", ("v", chain[0]))
        bk, rd = take()
        left = bk[:, 0:GC].rearrange("p (b j) -> p b j", b=GB)
        right = bk[:, GC:2 * GC].rearrange("p (b j) -> p b j", b=GB)
        done("pe", neighbours((left, right), o_A[:], o_A[:]), "nb", g)
        need("dve", ("nb", g))
        h = [o_h[:, ch // 2, :, ch % 2, :] for ch in range(CH)]
        for tap, src in enumerate((left, o_A[:], right)):
            for ch in range(CH):
                w = c1w[:, ch * TAPS + tap:ch * TAPS + tap + 1]
                if tap == 0:
                    last = dve.tensor_scalar(h[ch], src, w, None, ALU.mult)
                else:
                    last = dve.scalar_tensor_tensor(h[ch], src, w, h[ch], ALU.mult, ALU.add)
            vstep(last)
        rd.append(("v", chain[0]))
        hf = o_h[:].rearrange("p g b c j -> p (g b) (c j)")
        sqf = o_sq[:].rearrange("p g b c j -> p (g b) (c j)")
        flat = o_h[:].rearrange("p g b c j -> p (g b c j)")

        def over_tokens(src, key):
            need("pe", ("v", chain[0]))
            bk, rd = take()
            done("pe", pe.matmul(bk[:, 0:src.shape[-1]], ones[:], src, start=True, stop=True), key, g)
            need("dve", (key, g))
            return bk, rd

        bk, rd = over_tokens(flat, "gn1")
        vstep(dve.tensor_reduce(o_mean[:], bk[:, 0:2 * GB * 2 * NT].rearrange("p (k m) -> p k m", k=2 * GB), AX.X, ALU.add))
        rd.append(("v", chain[0]))
        vstep(dve.tensor_scalar(o_mean[:], o_mean[:], 1.0 / (2 * SEQ), None, ALU.mult))
        vstep(dve.tensor_tensor(hf, hf, o_mean[:, :, None].to_broadcast([P, 2 * GB, 2 * NT]), ALU.subtract))
        vstep(dve.tensor_tensor(sqf, hf, hf, ALU.mult))
        bk, rd = over_tokens(o_sq[:].rearrange("p g b c j -> p (g b c j)"), "gn2")
        vstep(dve.tensor_reduce(o_rs[:], bk[:, 0:2 * GB * 2 * NT].rearrange("p (k m) -> p k m", k=2 * GB), AX.X, ALU.add))
        rd.append(("v", chain[0]))
        vstep(dve.tensor_scalar(o_rs[:], o_rs[:], 1.0 / (2 * SEQ), 1e-5, ALU.mult, ALU.add))
        need("pool", ("v", chain[0]))
        done("pool", pool.tensor_tensor(o_rs[:], o_rs[:], mhalf[:, 0:2 * GB], ALU.pow), "gnr", g)
        need("dve", ("gnr", g))
        vstep(dve.tensor_tensor(hf, hf, o_rs[:, :, None].to_broadcast([P, 2 * GB, 2 * NT]), ALU.mult))
        for ch in range(CH):
            last = dve.tensor_scalar(h[ch], h[ch], gng[:, ch:ch + 1], gnb[:, ch:ch + 1], ALU.mult, ALU.add)
        vstep(last)
        vstep(dve.tensor_scalar(flat, flat, 0.0, None, ALU.max))
        for ch in range(CH):
            for tap in range(TAPS):
                w = c2w[:, ch * TAPS + tap:ch * TAPS + tap + 1]
                if ch == 0:
                    last = dve.tensor_scalar(o_t[:, tap], h[ch], w, None, ALU.mult)
                else:
                    last = dve.scalar_tensor_tensor(o_t[:, tap], h[ch], w, o_t[:, tap], ALU.mult, ALU.add)
            vstep(last)
        need("pe", ("v", chain[0]))
        bk, rd = take()
        y = bk[:, 0:GC].rearrange("p (b j) -> p b j", b=GB)
        done("pe", neighbours((y, y), o_t[:, 0], o_t[:, 2], extra=o_t[:, 1]), "nb2", g)
        need("dve", ("nb2", g))
        vstep(dve.scalar_tensor_tensor(o_e[:], y, c2b[:], o_A[:], ALU.add, ALU.add))
        rd.append(("v", chain[0]))
        vstep(dve.tensor_scalar(o_e[:], o_e[:], -80.0, None, ALU.max))
        need("act", ("v", chain[0]))
        done("act", act.activation(o_e[:], o_e[:], ACT.Exp, scale=-1.0), "oexp", g)
        need("dve", ("oexp", g))
        vstep(dve.tensor_scalar(o_e[:], o_e[:], 1.0, None, ALU.add))
        vstep(dve.reciprocal(o_e[:], o_e[:]))
        need("act", ("v", chain[0]))
        done("act", act.activation(o_e[:], o_e[:], ACT.Exp), "oexp2", g)
        need("dve", ("oexp2", g))
        vstep(dve.tensor_reduce(o_s[:], o_e[:], AX.X, ALU.add))
        bk, rd = over_tokens(o_s[:], "osum")
        vstep(dve.reciprocal(o_s[:], bk[:, 0:GB]))
        rd.append(("v", chain[0]))
        vstep(dve.tensor_tensor(WT[g % 2][:], o_e[:], o_s[:, :, None].to_broadcast([P, GB, NT]), ALU.mult))
        st.at[("weights", g)] = st.at[("v", chain[0])]

    recv = rec[0:TOK, :].rearrange("(b j p) c -> b p j c", j=NT, p=P)

    def f1_norms(b):
        g = b // GB
        x3 = X2[b % NX2]
        need("dve", ("weights", g), ("x2b", b), ("U", b, NT - 1))
        for j in range(NT):
            done("dve", dve.scalar_tensor_tensor(x3[:, j, :], U[b % 4][:, j, 0:D], WT[g % 2][:, b % GB, j:j + 1],
                                                 x3[:, j, :], ALU.mult, ALU.add), "x3", b, j)
            need("dve", ("x3", b, j))
            ln_stats(x3[:, j, :], 2, b, j)
        ln_root(2, b)
        for j in range(NT):
            done("dve", ln_apply(x3[:, j, :], x3[:, j, :], 2, b, j), "x3n", b, j)
            need("dve", ("x3n", b, j))
            ln_stats(x3[:, j, :], 3, b, j)
        ln_root(3, b)
        if b >= 1:
            need("dve", ("h16", b - 1))
        for j in range(NT):
            done("dve", ln_apply(HN[:, j, :], x3[:, j, :], 3, b, j), "hn", b, j)
        need("pool", ("hn", b, NT - 1))
        done("pool", pool.tensor_tensor(HN[:], HN[:], gam[:, None, :].to_broadcast([P, NT, D]), ALU.mult), "hg", b)
        need("pool", ("hg", b))
        done("pool", pool.tensor_tensor(HN[:], HN[:], bet[:, None, :].to_broadcast([P, NT, D]), ALU.add), "h", b)

    def ht_of(b):
        return HT[b - (B - HELD) + 1] if B - HELD <= b < B - 1 else HT[0]

    def f2_router(b):
        h16 = H16
        need("act", ("h", b))
        if b >= 1:
            need("act", ("hrec", b - 1), ("hT", b - 1))
        done("act", act.activation(h16[:, :, 0, :], HN[:], ACT.Copy), "hhi", b)
        need("dve", ("hhi", b))
        done("dve", dve.tensor_tensor(h16[:, :, 1, :], HN[:], h16[:, :, 0, :], ALU.subtract), "h16", b)
        need("sp", ("h16", b))
        moved(sp.dma_start(recv[b][:, :, 0:D], h16[:].rearrange("p j s d -> p j (s d)").bitcast(F32)),
              "hrec", "hrec", b)
        ht = ht_of(b)
        need("pe", ("h16", b))
        for s in range(2):
            bk, rd = take()
            b16 = bk[:].bitcast(F16)
            for c in range(DC):
                for j in range(NT):
                    o = c * SEQ + j * P
                    last = pe.transpose(b16[:, o:o + P], h16[:, j, s, c * P:(c + 1) * P], ident16[:])
            done("pe", last, "hT", b, s)
            if b > 0:
                need("act", ("up", min(b, B - HELD) - 1, FC - 1))
            if b == B - HELD and s == 0:
                need("act", ("u", B - 1), ("Ml", B - 1), ("Xl", B - 1))
            need("act", ("hT", b, s))
            done("act", act.activation(ht[:, s].rearrange("p c n -> p (c n)"), b16, ACT.Copy), "HT", b, s)
            rd.append(("HT", b, s))
        st.at[("hT", b)] = st.at[("hT", b, 1)]
        need("pe", ("HT", b, 1))
        bk, rd = take()
        W3 = 3 * NE
        for j in range(NT):
            for k, (s, c) in enumerate([(s, c) for s in range(2) for c in range(DC)]):
                last = pe.matmul(bk[:, j * W3:(j + 1) * W3], ht[:, s, c, j * P:(j + 1) * P],
                                 RW3[:, c].rearrange("p k e -> p (k e)"), start=k == 0, stop=k == 3)
        done("pe", last, "logits", b)
        need("dve", ("logits", b))
        lg = r_lg
        vstep(dve.tensor_reduce(lg[:], bk[:, 0:NT * W3].rearrange("p (j k e) -> p j e k", j=NT, k=3), AX.X, ALU.add))
        rd.append(("v", chain[0]))
        T = slice(b * NT, (b + 1) * NT)

        def wide(x):
            return x[:, :, None].to_broadcast([P, NT, NE])

        vstep(dve.tensor_reduce(r_mx[:], lg[:], AX.X, ALU.max))
        dve.tensor_tensor(r_eq[:], lg[:], wide(r_mx), ALU.is_equal)
        vstep(dve.tensor_tensor(lg[:], lg[:], wide(r_mx), ALU.subtract))
        need("act", ("v", chain[0]))
        done("act", act.activation(lg[:], lg[:], ACT.Exp, scale=hdn[:]), "rexp", b)
        vstep(dve.tensor_tensor(r_eq[:], r_eq[:], desc8[:, None, :].to_broadcast([P, NT, NE]), ALU.mult))
        vstep(dve.tensor_reduce(r_mx[:], r_eq[:], AX.X, ALU.max))
        vstep(dve.tensor_tensor(OH[:, T, :], r_eq[:], wide(r_mx), ALU.is_equal))
        need("dve", ("rexp", b))
        vstep(dve.tensor_reduce(r_mx[:], lg[:], AX.X, ALU.add))
        vstep(dve.reciprocal(GATE[:, T], r_mx[:]))
        st.at[("gate", b)] = st.at[("v", chain[0])]

    r_lg = sb("r_lg", [P, NT, NE])
    r_mx = sb("r_mx", [P, NT])
    r_eq = sb("r_eq", [P, NT, NE])
    sn = [0]

    def g1_shared(b):
        ht = ht_of(b)
        for f in range(FC):
            bk, rd = take()
            for k, (s, c) in enumerate([(s, c) for s in range(2) for c in range(DC)]):
                last = pe.matmul(bk[:], E1T[:, NE, c, f * P:(f + 1) * P], ht[:, s, c, :], start=k == 0, stop=k == 3)
            done("pe", last, "up", b, f)
            need("act", ("up", b, f))
            s = S[sn[0] % 2]
            if sn[0] >= 2:
                need("act", ("Sl", sn[0] - 2))
            done("act", act.activation(s[:], bk[:], ACT.Silu, scale=e1s[:, NE, f:f + 1]), "silu", sn[0])
            rd.append(("silu", sn[0]))
            need("dve", ("silu", sn[0]))
            if f == 0 and b >= 1:
                need("dve", ("down", b - 1, NT - 1))
            done("dve", dve.tensor_scalar(Sh[:, f, :], s[:], sdn[:], None, ALU.mult), "Sh", sn[0])
            need("dve", ("Sh", sn[0]))
            done("dve", dve.scalar_tensor_tensor(Sl[:, f, :], s[:], sdn[:], Sh[:, f, :], ALU.mult, ALU.subtract), "Sl", sn[0])
            sn[0] += 1

    def g2_shared(b):
        need("pe", ("Sl", sn[0] - 1))
        r = R
        for j in range(NT):
            bk, rd = take()
            for k, (f, s) in enumerate([(f, s) for f in range(FC) for s in (Sh, Sl)]):
                last = pe.matmul(bk[:, 0:D], s[:, f, j * P:(j + 1) * P], E2T[:, NE, f, :], start=k == 0, stop=k == 2 * FC - 1)
            done("pe", last, "down", b, j)
            need("dve", ("down", b, j))
            if b >= 1 and j == 0:
                need("dve", ("rrec", b - 1))
            done("dve", dve.tensor_tensor(r[:, j, 0:D], bk[:, 0:D], e2s[:, NE, :], ALU.mult), "y", b, j)
            rd.append(("y", b, j))
        need("dve", ("gate", b))
        done("dve", dve.tensor_copy(r[:, :, D:D + 2], GATE[:, b * NT:(b + 1) * NT, None].to_broadcast([P, NT, 2])), "rg", b)
        need("pool", ("y", b, NT - 1), ("x3n", b, NT - 1))
        done("pool", pool.tensor_tensor(r[:, :, 0:D], r[:, :, 0:D], X2[b % NX2][:], ALU.add), "r", b)
        need("sp", ("r", b), ("rg", b))
        moved(sp.dma_start(recv[b][:, :, D:REC], r[:]), "rrec", "rrec", b)

    sort_bank = []

    def sort_places():
        need("pe", ("gate", B - 1))
        ohv = OH[:].rearrange("p t e -> p e t")
        bk1, rd1 = take()
        bk2, rd2 = take()
        pe.matmul(bk1[:], before[:], ohv, start=True, stop=True)
        done("pe", pe.matmul(bk2[:], onesb[:], ohv, start=True, stop=True), "counts")
        need("dve", ("counts",))
        dve.memset(q_z[:], 0.0)
        dve.tensor_copy(part_f[:], part_i[:])
        dve.tensor_copy(q_C[:], bk1[:].rearrange("p (e t) -> p e t", e=NE))
        vstep(dve.tensor_copy(q_tot[:], bk2[:].rearrange("p (e t) -> p e t", e=NE)))
        rd1.append(("v", chain[0]))
        rd2.append(("v", chain[0]))
        dve.tensor_tensor(q_C[:], q_C[:], q_tot[:], ALU.subtract)
        vstep(dve.tensor_reduce(q_n[:], q_tot[:], AX.X, ALU.add))
        vstep(dve.tensor_scalar(q_ni[:], q_n[:], float(SLOT - 1), None, ALU.add))
        vstep(dve.tensor_scalar(q_ni[:], q_ni[:], SLOT.bit_length() - 1, SLOT.bit_length() - 1,
                                ALU.logical_shift_right, ALU.logical_shift_left))
        vstep(dve.tensor_copy(q_n[:], q_ni[:]))
        vstep(dve.tensor_tensor_scan(q_end[:], q_n[:], q_z[:, 0:NE], 0.0, ALU.add, ALU.add))
        vstep(dve.tensor_tensor(q_n[:], q_end[:], q_n[:], ALU.subtract))
        for e in range(NE):
            last = dve.tensor_tensor_scan(q_tot[:, e, :], q_tot[:, e, :], q_z[:], q_n[:, e:e + 1], ALU.add, ALU.add)
        vstep(last)
        vstep(dve.tensor_tensor(q_C[:], q_C[:], q_tot[:], ALU.add))
        vstep(dve.tensor_tensor(q_C[:], q_C[:], ohv, ALU.mult))
        vstep(dve.tensor_reduce(q_pos[:], q_C[:].rearrange("p e t -> p t e"), AX.X, ALU.add))
        vstep(dve.tensor_copy(q_i[:], q_pos[:]))
        vstep(dve.tensor_scalar(q_i[:], q_i[:], 7, None, ALU.logical_shift_right))
        vstep(dve.tensor_copy(q_hi[:], q_i[:]))
        vstep(dve.scalar_tensor_tensor(q_lo[:], q_hi[:], -float(P), q_pos[:], ALU.mult, ALU.add))
        vstep(dve.tensor_tensor(q_ge[:], q_end[:, :, None].to_broadcast([P, NE, NG]), group_first[:, None, :].to_broadcast([P, NE, NG]), ALU.is_le))
        vstep(dve.tensor_reduce(q_ex[:], q_ge[:].rearrange("p e g -> p g e"), AX.X, ALU.add))
        vstep(dve.tensor_scalar(q_exi[:], q_ex[:], float(NE - 1), None, ALU.min))
        st.at[("experts",)] = st.at[("v", chain[0])]

    def sort_invert(k):
        if k == 0:
            sort_bank.extend(take())
            kept.append((turn[0] - 1) % len(banks))
        bk, _ = sort_bank
        a, bb = q_A[k % 2], q_B[k % 2]
        T = slice(k * CHK, (k + 1) * CHK)
        if k >= 2:
            need("dve", ("inv", k - 2))
        dve.tensor_tensor(a[:], q_lo[:, T, None].to_broadcast([P, CHK, P]), iota_f[:, None, :].to_broadcast([P, CHK, P]), ALU.is_equal)
        vstep(dve.tensor_tensor(bb[:, :, 1, :], q_hi[:, T, None].to_broadcast([P, CHK, NST]),
                                iota_f[:, None, 0:NST].to_broadcast([P, CHK, NST]), ALU.is_equal))
        vstep(dve.tensor_tensor(bb[:, :, 0, :], bb[:, :, 1, :], tile_f[:, T, None].to_broadcast([P, CHK, NST]), ALU.mult))
        vstep(dve.tensor_scalar(bb[:, :, 1, :], bb[:, :, 1, :], part_f[:], None, ALU.mult))
        need("pe", ("v", chain[0]))
        for i in range(CHK):
            tt = k * CHK + i
            last = pe.matmul(bk[:, 0:2 * NST], a[:, i, :], bb[:, i].rearrange("p s h -> p (s h)"),
                             start=tt == 0, stop=tt == NTILE - 1)
        done("pe", last, "inv", k)

    def sort_ids():
        bk, rd = sort_bank
        need("dve", ("inv", NTILE // CHK - 1))
        vstep(dve.tensor_scalar(ids_f[:], bk[:, 0:NST], float(P), float(TOK), ALU.mult, ALU.add))
        vstep(dve.tensor_tensor(ids_f[:], ids_f[:], bk[:, NST:2 * NST], ALU.add))
        rd.append(("v", chain[0]))
        kept.clear()
        vstep(dve.tensor_copy(ids[:], ids_f[:]))
        st.at[("ids",)] = st.at[("v", chain[0])]

    pool_chain(pool.iota(group_first[:].bitcast(I32), pattern=[[SLOT, NG]], base=0, channel_multiplier=0))
    done("pool", pool.tensor_copy(group_first[:], group_first[:].bitcast(I32)), "gfirst")
    need("dve", ("gfirst",))

    regs = {}
    front_free = []

    def r0_gather(s):
        if s >= 3:
            need("pool", ("gx", s - 3, NGT - 1), ("gTr", s - 3))
        if s == 0:
            need("pool", ("ids",), ("hrec", B - 1), ("rrec", B - 1), ("zero", 2), *front_free)
        for j in range(NGT):
            tt = s * NGT + j
            moved(pool.indirect_dma_start(G_rec[s % 3][:, j, :], None, rec[:],
                                          bass.IndirectOffsetOnAxis(ids[:, tt:tt + 1], 0)), f"gat{s % 3}", "gat", s, j)

    def r1_transpose(s):
        g = G_rec[s % 3]
        need("pe", ("gat", s, NGT - 1))
        bk, rd = take()
        b16 = bk[:].bitcast(F16)
        for j in range(NGT):
            h16 = g[:, j, 0:D].bitcast(F16)
            for s2 in range(2):
                for c in range(DC):
                    o = (s2 * DC + c) * SLOT + j * P
                    last = pe.transpose(b16[:, o:o + P], h16[:, s2 * D + c * P:s2 * D + (c + 1) * P], ident16[:])
        done("pe", last, "gTr", s)
        need("act", ("gTr", s))
        if s >= 2:
            need("act", ("gup", s - 2, FC - 1))
        done("act", act.activation(G_T[s % 2][:].rearrange("p s c n -> p (s c n)"), b16, ACT.Copy), "gT", s)
        rd.append(("gT", s))

    def r2_up(s):
        for eng in ("pe", "act"):
            need(eng, ("experts",))
            regs[eng, s] = st.engines[eng].value_load(q_exi[0:1, s:s + 1], min_val=0, max_val=NE - 1)
        ep, ea = regs["pe", s], regs["act", s]
        need("pe", ("gT", s))
        gt = G_T[s % 2]
        for f in range(FC):
            if f % 2 == 0:
                bk, rd = take()
            o = (f % 2) * SLOT
            for k, (s2, c) in enumerate([(s2, c) for s2 in range(2) for c in range(DC)]):
                last = pe.matmul(bk[:, o:o + SLOT], E1T[:, bass.DynSlice(ep, 1), c, f * P:(f + 1) * P], gt[:, s2, c, :],
                                 start=k == 0, stop=k == 3)
            done("pe", last, "gup", s, f)
            if f % 2 == 1:
                for ff in (f - 1, f):
                    need("act", ("gup", s, f))
                    if s >= 2 and ff == 0:
                        need("act", ("gSl", s - 2))
                    done("act", act.activation(G_S[s % 2][:, ff, :], bk[:, (ff % 2) * SLOT:(ff % 2 + 1) * SLOT], ACT.Silu,
                                               scale=e1s[:, bass.DynSlice(ea, 1), ff]), "gsilu", s, ff)
                rd.append(("gsilu", s, f))
        need("dve", ("gsilu", s, FC - 1))
        if s >= 2:
            need("dve", ("gdown", s - 2, NGT - 1))
        done("dve", dve.tensor_scalar(G_Sh[s % 2][:], G_S[s % 2][:], sdn[:], None, ALU.mult), "gSh", s)
        need("dve", ("gSh", s))
        done("dve", dve.scalar_tensor_tensor(G_Sl[s % 2][:], G_S[s % 2][:], sdn[:], G_Sh[s % 2][:], ALU.mult, ALU.subtract),
             "gSl", s)

    def r3_down(s):
        need("dve", ("experts",))
        ev = dve.value_load(q_exi[0:1, s:s + 1], min_val=0, max_val=NE - 1)
        ep = regs["pe", s]
        need("pe", ("gSl", s))
        g, y = G_rec[s % 3], G_y[s % 3]
        for j in range(NGT):
            bk, rd = take()
            for k, (f, sx) in enumerate([(f, sx) for f in range(FC) for sx in (G_Sh, G_Sl)]):
                last = pe.matmul(bk[:, 0:D], sx[s % 2][:, f, j * P:(j + 1) * P], E2T[:, bass.DynSlice(ep, 1), f, :],
                                 start=k == 0, stop=k == 2 * FC - 1)
            done("pe", last, "gdown", s, j)
            need("dve", ("gdown", s, j), ("gat", s, NGT - 1))
            if s >= 3 and j == 0:
                need("dve", ("gout", s - 3, NGT - 1))
            done("dve", dve.scalar_tensor_tensor(y[:, j, :], bk[:, 0:D], g[:, j, 2 * D:2 * D + 1],
                                                 e2s[:, bass.DynSlice(ev, 1), :].rearrange("p o d -> p (o d)"), ALU.mult, ALU.mult), "gy", s, j)
            rd.append(("gy", s, j))
            need("dve", ("gy", s, j))
            done("dve", dve.tensor_tensor(y[:, j, :], y[:, j, :], g[:, j, D:2 * D], ALU.add), "gx", s, j)
            need("dve", ("gx", s, j))
            ln_stats(y[:, j, :], 0, ("g", s), j)
        ln_root(0, ("g", s), 0, NGT)

    def r4_out(s):
        y = G_y[s % 3]
        for j in range(NGT):
            done("dve", ln_apply(y[:, j, :], y[:, j, :], 0, ("g", s), j), "gn", s, j)
            need("pool", ("gn", s, j))
            tt = s * NGT + j
            moved(pool.indirect_dma_start(t["out"], bass.IndirectOffsetOnAxis(ids[:, tt:tt + 1], 0), y[:, j, :], None,
                                          bounds_check=TOK - 1, oob_is_err=False), f"out{s % 3}", "gout", s, j)

    todo = list(range(NE, -1, -1))
    load_x(0)
    load_xT(0)

    for i in range(B + FSKEW):
        def at(stage, skew, last=B):
            if 0 <= i - skew < last:
                stage(i - skew)
        at(b3_values, 1)
        if i + 1 < B:
            load_x(i + 1)
        at(a1_split, 0)
        at(d2_stats, 2)
        at(f1_norms, FSKEW)
        at(a2_project, 0)
        if i + 1 < B:
            load_xT(i + 1)
        at(d3_values, 2)
        at(c1_transpose, 1)
        at(f2_router, FSKEW)
        at(b1_scores, 0)
        at(g1_shared, FSKEW, B - HELD)
        at(b2_transpose, 0)
        at(g2_shared, FSKEW, B - HELD)
        at(c2_linear, 1)
        if i >= 2 and (i - 2) % GB == GB - 1 and (i - 2) // GB < B // GB:
            ode((i - 2) // GB)
        for _ in range(2):
            if todo:
                expert(todo.pop(0))
                if not todo:
                    guards()
                    for eng in ("act", "dve", "pool"):
                        need(eng, ("guards",))
        at(d1_transpose, 1)
    front_free.extend([("u", B - 1), ("x3", B - 1, NT - 1), ("U", B - 1, NT - 1), ("Ml", B - 1), ("Xl", B - 1)])
    for eng in ("dve", "act"):
        need(eng, *front_free)
    sort_places()
    chunks = list(range(NTILE // CHK))
    for b in range(B - HELD, B):
        for _ in range(2):
            if chunks:
                sort_invert(chunks.pop(0))
        g1_shared(b)
        if chunks:
            sort_invert(chunks.pop(0))
        g2_shared(b)
    for k in chunks:
        sort_invert(k)
    sort_ids()
    for s in range(NG + 3):
        if s < NG:
            r0_gather(s)
        if 0 <= s - 3 < NG:
            r4_out(s - 3)
        if 0 <= s - 1 < NG:
            r1_transpose(s - 1)
        if 0 <= s - 2 < NG:
            r3_down(s - 2)
        if 0 <= s - 1 < NG:
            r2_up(s - 1)
    for s in range(NG - 3, NG):
        need("sp", ("gout", s, NGT - 1))
    for lane in ("small", "zero"):
        sp.wait_ge(st.sems["d_" + lane], st.count["d_" + lane])


def kernel(**inputs):
    import concourse.bacc as bacc
    from concourse.bass_utils import run_bass_kernel_spmd

    a = {k: np.ascontiguousarray(v) for k, v in inputs.items()}
    x = a["L0_attn_x"].reshape(TOK, D)
    wqk = np.zeros((D, 4, 32), x.dtype)
    bqk = np.zeros((4, 32, 1), x.dtype)
    for s, (w, b) in enumerate([("w_q", "b_q")] * 2 + [("w_k", "b_k")] * 2):
        wqk[:, s, :QK] = a["L0_attn_" + w].T
        bqk[s, :QK, 0] = a["L0_attn_" + b]
    wall = a["L1_attn_qkv_w"]
    arrays = {
        "x": x, "xT": np.ascontiguousarray(x.T), "wqk": wqk.reshape(D, P), "bqk": bqk.reshape(P, 1),
        "w0": a["L0_ffn_weight"], "wall": wall, "wvT": np.ascontiguousarray(wall[:, 2 * D:].T),
        "pw": a["L1_attn_proj_w"], "cw1": a["L1_attn_ch_w1"], "cb1": a["L1_attn_ch_b1"].reshape(RED, 1),
        "cw2": a["L1_attn_ch_w2"], "cb2": np.ascontiguousarray(a["L1_attn_ch_b2"].reshape(DC, P).T),
        "pb": a["L1_attn_proj_b"].reshape(1, D), "gam": a["L1_ffn_ln_gamma"].reshape(1, D),
        "bet": a["L1_ffn_ln_beta"].reshape(1, D),
        "cc": np.stack([a["L1_attn_c1"].reshape(()), a["L1_attn_c2"].reshape(())]).reshape(1, 2),
        "c1w": a["L1_attn_conv1_w"].reshape(1, CH * TAPS), "c2w": a["L1_attn_conv2_w"].reshape(1, CH * TAPS),
        "gng": a["L1_attn_gn_g"].reshape(1, CH), "gnb": a["L1_attn_gn_b"].reshape(1, CH),
        "c2b": a["L1_attn_conv2_b"].reshape(1, 1), "rw": np.ascontiguousarray(a["L1_ffn_router_w"].T),
        "sw1": a["L1_ffn_shared_w1"], "sw2": a["L1_ffn_shared_w2"],
        "ew1": a["L1_ffn_expert_w1"], "ew2": a["L1_ffn_expert_w2"],
    }
    nc = bacc.Bacc("TRN2", target_bir_lowering=False, num_devices=1)
    t = {k: nc.dram_tensor("in_" + k, v.shape, mybir.dt.from_np(v.dtype), kind="ExternalInput").ap() for k, v in arrays.items()}
    t["out"] = nc.dram_tensor("out", (TOK, D), F32, kind="ExternalOutput").ap()
    build_program(nc, t)
    r = run_bass_kernel_spmd(nc, [{"in_" + k: v for k, v in arrays.items()}], core_ids=[0])
    return r.results[0]["out"].reshape(B, SEQ, D)
```

```python
import numpy as np

import concourse.bass as bass
from concourse import mybir
from collections import deque
from contextlib import ExitStack

F32 = mybir.dt.float32
F32R = mybir.dt.float32r
F16 = mybir.dt.float16
BF16 = mybir.dt.bfloat16
I32 = mybir.dt.int32
ALU = mybir.AluOpType
ACT = mybir.ActivationFunctionType
AX = mybir.AxisListType

P = 128
B, SEQ, D = 16, 512, 256
TOK = B * SEQ
NT = SEQ // P
NTILE = TOK // P
DC = D // P
QK = 16
RED = D // 4
FF = 512
FC = FF // P
NE = 8
CH = 4
TAPS = 3
GB = 4
GC = GB * NT
SLOT = 256
NG = (TOK + NE * (SLOT - 1)) // SLOT
NST = NG * SLOT // P
REC = 2 * D + 2
LN_EPS = 1e-5
HELD = 3
FSKEW = GB + 2
RNE = 12582912.0
NEG = -1e30
BANK = 512


COST = {"pe": 0.5, "act": 0.4, "dve": 0.35, "pool": 1.0,
        "dqk": 1.84, "gdown": 1.5, "gup": 0.66, "pv": 1.23, "down": 1.06, "up": 1.03, "u": 0.67, "proj": 2.4,
        "gTr": 0.86, "hT": 0.86, "x2T": 0.55, "fuse": 1.7, "et0": 0.6, "et1": 0.6,
        "eround": 1.7, "ET": 0.9, "silu": 0.85, "gT": 0.9, "HT": 0.9, "gSh": 0.6, "qkhi": 1.14, "Xh": 1.0, "hhi": 0.95,
        "ps": 0.8, "v": 0.27, "gSl": 0.66, "Sl": 0.66, "qklo": 1.3, "x1Tl": 0.6, "x2Tl": 0.6, "h16": 1.14,
        "mv": 0.08, "veps": 1.0, "rstd": 1.0, "Xl": 2.3, "x2b": 2.3, "hg": 2.3, "h": 2.3, "r": 2.3, "gnr": 1.2}
HANDOVER = 0.15
DMA_TIME = 3.0


class Steps:

    def __init__(self, nc, ctx):
        self.nc, self.ctx = nc, ctx
        self.engines = {"pe": nc.tensor, "act": nc.scalar, "dve": nc.vector, "pool": nc.gpsimd, "sp": nc.sync}
        self.sems, self.count, self.at, self.seen = {}, {}, {}, {}
        self.clock, self.ended, self.latest = dict.fromkeys(self.engines, 0.0), {}, 0.0

    def sem(self, name):
        if name not in self.sems:
            self.sems[name] = self.ctx.enter_context(self.nc.semaphore(name))
            self.count[name] = 0
        return self.sems[name]

    def done(self, eng, ins, *key):
        ins.then_inc(self.sem("s_" + eng), 1)
        self.count["s_" + eng] += 1
        self.at[key] = ("s_" + eng, self.count["s_" + eng])
        self.clock[eng] += COST.get(key[0], COST[eng])
        self.ended[self.at[key]] = self.latest = self.clock[eng] + HANDOVER

    def moved(self, ins, lane, *key):
        ins.then_inc(self.sem("d_" + lane), 16)
        self.count["d_" + lane] += 16
        self.at[key] = ("d_" + lane, self.count["d_" + lane])
        if lane[:3] in ("gat", "out"):
            self.clock["pool"] += COST["pool"]
            self.latest = self.clock["pool"]
        self.ended[self.at[key]] = self.latest + DMA_TIME

    def need(self, eng, *keys):
        for key in keys:
            name, value = self.at[key]
            if self.seen.get((eng, name), 0) < value:
                self.engines[eng].wait_ge(self.sems[name], value)
                self.seen[eng, name] = value
            self.clock[eng] = max(self.clock[eng], self.ended[name, value])


def build_program(nc, t):
    ctx = ExitStack()
    with ctx:
        program(nc, t, ctx)


def program(nc, t, ctx):
    pe, act, dve, pool, sp = nc.tensor, nc.scalar, nc.vector, nc.gpsimd, nc.sync
    st = Steps(nc, ctx)
    done, need, moved = st.done, st.need, st.moved

    start = -(-nc.sbuf_base // 64) * 64
    here = [start]

    def sb(name, shape, dt=F32):
        size = 4 if dt in (F32, F32R, I32) else 2
        for d in shape[1:]:
            size *= d
        at = here[0]
        here[0] = -(-(at + size) // 64) * 64
        assert here[0] <= nc.sbuf_usable_end, (name, here[0])
        return nc.alloc_sbuf_tensor_at(name, list(shape), dt, offset=at, align_bytes=32)

    def ring(name, n, shape, dt=F32):
        return [sb(f"{name}{i}", shape, dt) for i in range(n)]

    free_banks = deque((ctx.enter_context(nc.psum_tensor(f"bank{i}", [P, BANK], F32)), None) for i in range(8))

    class Lease:

        def __init__(self, bank):
            self.bank = bank

        def append(self, key):
            free_banks.append((self.bank, key))

    def take():
        while not free_banks:
            yield
        bank, key = free_banks.popleft()
        if key is not None:
            need("pe", key)
        return bank, Lease(bank)

    rec = nc.dram_tensor("rec", [TOK + 1, REC], F32)

    ident = sb("ident", [P, P])
    ident16 = sb("ident16", [P, P], F16)
    identb = sb("identb", [P, P], BF16)
    maskb = sb("maskb", [P, P], BF16)
    ones = sb("ones", [P, P])
    onesb = sb("onesb", [P, P], BF16)
    before = sb("before", [P, P], BF16)
    from_prev = sb("from_prev", [P, P])
    from_next = sb("from_next", [P, P])
    edge_prev = sb("edge_prev", [P, P])
    edge_next = sb("edge_next", [P, P])
    mhalf = sb("mhalf", [P, GC])
    iota_f = sb("iota_f", [P, P])
    part_i = sb("part_i", [P, 1], I32)
    desc8 = sb("desc8", [P, NE])
    tile_f = sb("tile_f", [P, NTILE])

    iota_i, tile_i = iota_f[:].bitcast(I32), tile_f[:].bitcast(I32)
    n = [0]

    def pool_chain(ins):
        n[0] += 1
        done("pool", ins, "const", n[0])
        need("pool", ("const", n[0]))

    for m, v in ((ident, 0.0), (ident16, 0.0), (identb, 0.0), (maskb, 0.0), (ones, 1.0), (onesb, 1.0),
                 (before, 0.0), (from_prev, 0.0), (from_next, 0.0), (edge_prev, 0.0), (edge_next, 0.0),
                 (mhalf, -0.5)):
        ins = pool.memset(m[:], v)
    pool_chain(ins)
    for m, base in ((ident, 0), (ident16, 0), (identb, 0), (from_prev, 1), (from_next, -1),
                    (edge_prev, -(P - 1)), (edge_next, P - 1)):
        ins = pool.affine_select(out=m[:], in_=m[:], compare_op=ALU.not_equal, fill=1.0, base=base,
                                 pattern=[[-1, P]], channel_multiplier=1)
    pool.affine_select(out=maskb[:], in_=maskb[:], compare_op=ALU.is_ge, fill=NEG, base=0,
                       pattern=[[-1, P]], channel_multiplier=1)
    pool.affine_select(out=before[:], in_=before[:], compare_op=ALU.is_ge, fill=1.0, base=0,
                       pattern=[[-1, P]], channel_multiplier=1)
    pool.iota(iota_i, pattern=[[1, P]], base=0, channel_multiplier=0)
    pool.iota(tile_i, pattern=[[1, NTILE]], base=-NTILE, channel_multiplier=0)
    pool_chain(pool.iota(part_i[:], pattern=[[0, 1]], base=0, channel_multiplier=1))
    pool.tensor_copy(iota_f[:], iota_i)
    pool_chain(pool.tensor_copy(tile_f[:], tile_i))
    done("pool", pool.tensor_scalar(desc8[:], iota_f[:, 0:NE], -1.0, float(NE), ALU.mult, ALU.add), "consts")

    wqk = sb("wqk", [P, DC, P])
    bqk = sb("bqk", [P, 1])
    pw = sb("pw", [P, DC, D])
    cw1 = sb("cw1", [P, DC, RED])
    cb1 = sb("cb1", [RED, 1])
    cw2 = sb("cw2", [RED, D])
    cb2 = sb("cb2", [P, DC])
    pb_row = sb("pb_row", [P, D])
    gam = sb("gam", [P, D])
    bet = sb("bet", [P, D])
    cc = sb("cc", [P, 2])
    c1w = sb("c1w", [P, CH * TAPS])
    c2w = sb("c2w", [P, CH * TAPS])
    gng = sb("gng", [P, CH])
    gnb = sb("gnb", [P, CH])
    c2b = sb("c2b", [P, 1])
    rw = sb("rw", [P, DC, NE])

    W0T = sb("W0T", [P, DC, D], F16)
    sc0 = sb("sc0", [P, 1])
    WCh = sb("WCh", [P, DC, 2 * D], F32R)
    WCl = sb("WCl", [P, DC, 2 * D], F32R)
    wvT = sb("wvT", [P, DC, D])
    RW3 = sb("RW3", [P, DC, 3, NE], BF16)
    E1T = sb("E1T", [P, NE + 1, DC, FF], F16)
    E2T = sb("E2T", [P, NE + 1, FC, D], F16)
    e1s = sb("e1s", [P, NE + 1, FC])
    e2s = sb("e2s", [P, NE + 1, D])
    hup = sb("hup", [P, 1])
    hdn = sb("hdn", [P, 1])
    sdn = sb("sdn", [P, 1])
    sup = sb("sup", [P, 1])
    esc = sb("esc", [P, 2, FC])
    esr = sb("esr", [P, 2, FC])
    rne = sb("rne", [P, 1])
    hbound = sb("hbound", [P, 1])
    smax = sb("smax", [P, NE + 2])
    wsum = sb("wsum", [P, 4])
    tmp2 = sb("tmp2", [P, 8])

    NM = ring("NM", 2, [P, NT])
    RS = ring("RS", 2, [P, NT])
    RI = ring("RI", 2, [P, NT])
    bst = ring("bst", 4, [P, NT, 6])
    mv = ring("mv", 4, [P, NT, 2])
    rstd = ring("rstd", 4, [P, NT])
    SUMS = ring("SUMS", 2, [P, DC])
    R1 = sb("R1", [RED, 1])
    CHW = sb("CHW", [P, DC])
    junk_a = sb("junk_a", [P, FF], BF16)
    S2 = ring("S2", 2, [P, GC])
    SQK = ring("SQK", 2, [P, GC])
    WT = ring("WT", 2, [P, GB, NT])
    OH = sb("OH", [P, NTILE, NE], BF16)
    GATE = sb("GATE", [P, NTILE])
    ids = sb("ids", [P, NST], I32)
    q_exi = sb("q_exi", [P, NG], I32)
    group_first = sb("group_first", [P, NG])

    NX2 = FSKEW - 1
    X2 = ring("X2", NX2, [P, NT, D])

    late_start = here[0]
    HT = [sb("HT0", [P, 2, DC, SEQ], F16)]
    HN = sb("HN", [P, NT, D])
    H16 = sb("H16", [P, NT, 2, D], F16)
    S = ring("S", 2, [P, SEQ])
    Sh = sb("Sh", [P, FC, SEQ], F16)
    Sl = sb("Sl", [P, FC, SEQ], F16)
    R = sb("R", [P, NT, D + 2])
    late_end = here[0]

    here[0] = late_start
    w0 = sb("w0", [P, DC, D])
    wall = sb("wall", [P, DC, 3 * D])
    e1n = sb("e1n", [P, FC, D])
    e2n = sb("e2n", [P, DC, FF])
    e1q = sb("e1q", [P, FC, D], F16)
    e2q = sb("e2q", [P, DC, FF], F16)
    dg = sb("dg", [P, DC, P])
    assert here[0] <= late_end

    here[0] = late_end
    U = ring("U", 4, [P, NT, D + 2])
    front_start = here[0]
    X = ring("X", 2, [P, NT, D])
    XT = sb("XT", [P, DC, SEQ])
    Xh = sb("Xh", [P, NT, D], F32R)
    Xl = sb("Xl", [P, NT, D], F32R)
    Qs = sb("Qs", [P, SEQ], F32R)
    KH = sb("KH", [P, SEQ], F32R)
    KL = sb("KL", [P, SEQ], F32R)
    OFF = [P * i * (i + 1) // 2 for i in range(NT + 1)]
    PB = sb("PB", [P, OFF[NT]])
    PTh = sb("PTh", [P, OFF[NT]], F32R)
    PTl = sb("PTl", [P, OFF[NT]], F32R)
    X1 = sb("X1", [P, NT, D])
    T1h = sb("T1h", [P, DC, SEQ], F16)
    T1l = sb("T1l", [P, DC, SEQ], F16)
    TTh = sb("TTh", [P, DC, SEQ], F32R)
    TTl = sb("TTl", [P, DC, SEQ], F32R)
    PS = sb("PS", [P, DC, D])
    Mh = sb("Mh", [P, DC, D + 2], F32R)
    Ml = sb("Ml", [P, DC, D + 2], F32R)
    DK = sb("DK", [P, D])
    front_end = here[0]

    here[0] = front_start
    HT += [sb(f"HT{k}", [P, 2, DC, SEQ], F16) for k in range(1, HELD)]
    q_C = sb("q_C", [P, NE, NTILE])
    q_tot = sb("q_tot", [P, NE, NTILE])
    q_z = sb("q_z", [P, NTILE])
    q_n = sb("q_n", [P, NE])
    q_ni = sb("q_ni", [P, NE], I32)
    q_end = sb("q_end", [P, NE])
    q_pos = sb("q_pos", [P, NTILE])
    q_i = sb("q_i", [P, NTILE], I32)
    q_lo = sb("q_lo", [P, NTILE])
    q_hi = sb("q_hi", [P, NTILE])
    CHK = 4
    q_A = ring("q_A", 2, [P, CHK, P], BF16)
    q_B = ring("q_B", 2, [P, CHK, 2, NST], BF16)
    part_f = sb("part_f", [P, 1])
    ids_f = sb("ids_f", [P, NST])
    q_ge = sb("q_ge", [P, NE, NG])
    q_ex = sb("q_ex", [P, NG])
    NGT = SLOT // P
    G_rec = ring("G_rec", 3, [P, NGT, REC])
    G_T = ring("G_T", 2, [P, 2, DC, SLOT], F16)
    G_S = ring("G_S", 2, [P, FC, SLOT])
    G_Sh = ring("G_Sh", 2, [P, FC, SLOT], F16)
    G_Sl = ring("G_Sl", 2, [P, FC, SLOT], F16)
    G_y = ring("G_y", 3, [P, NGT, D])
    assert here[0] <= front_end, (here[0], front_end, front_start, late_end, late_start, nc.sbuf_usable_end)
    here[0] = front_end
    small = [
        (wqk[:], t["wqk"].rearrange("(c p) m -> p c m", p=P)), (bqk[:], t["bqk"]),
        (w0[:], t["w0"].rearrange("(c p) i -> p c i", p=P)),
        (wall[:], t["wall"].rearrange("(c p) n -> p c n", p=P)),
        (wvT[:], t["wvT"].rearrange("(c p) n -> p c n", p=P)),
        (pw[:], t["pw"].rearrange("(c p) n -> p c n", p=P)),
        (cw1[:], t["cw1"].rearrange("(c p) n -> p c n", p=P)), (cb1[:], t["cb1"]), (cw2[:], t["cw2"]),
        (cb2[:], t["cb2"]), (pb_row[:], t["pb"].to_broadcast([P, D])), (gam[:], t["gam"].to_broadcast([P, D])),
        (bet[:], t["bet"].to_broadcast([P, D])), (cc[:], t["cc"].to_broadcast([P, 2])),
        (c1w[:], t["c1w"].to_broadcast([P, CH * TAPS])), (c2w[:], t["c2w"].to_broadcast([P, CH * TAPS])),
        (gng[:], t["gng"].to_broadcast([P, CH])), (gnb[:], t["gnb"].to_broadcast([P, CH])),
        (c2b[:], t["c2b"].to_broadcast([P, 1])), (rw[:], t["rw"].rearrange("(c p) e -> p c e", p=P)),
    ]
    for i, (dst, src) in enumerate(small):
        with nc.allow_non_contiguous_dma(reason="small weights, once"):
            moved((sp, act)[i % 2].dma_start(dst, src), "small", "small", i)
    st.at["small"] = st.at["small", len(small) - 1]
    st.at[("small",)] = st.at[("small", len(small) - 1)]

    chain = [0]
    mine = [None]

    def vstep(ins):
        chain[0] += 1
        n = chain[0]
        done("dve", ins, "v", n)
        yield
        need("dve", ("v", n))
        mine[0] = ("v", n)

    xv = t["x"].rearrange("(b j p) d -> b p j d", j=NT, p=P)
    xTv = t["xT"].rearrange("(c p) (b n) -> b p c n", p=P, n=SEQ)

    def load_x(b):
        if b >= 2:
            need("sp", ("x1", b - 2, NT - 1), ("Xl", b - 2))
        moved(sp.dma_start(X[b % 2][:], xv[b]), f"x{b % 2}", "X", b)

    def load_xT(b):
        if b >= 1:
            need("sp", ("proj", b - 1))
        moved(sp.dma_start(XT[:], xTv[b]), "xT", "XT", b)

    need("dve", ("small",), ("consts",))
    need("act", ("small",), ("consts",))
    need("pe", ("small",), ("consts",))
    need("pool", ("small",))
    def setup_first():
        for m in (Qs, KH, KL):
            dve.memset(m[:].bitcast(F32), 0.0)
        dve.memset(smax[:], 0.0)
        yield from vstep(dve.memset(rne[:], RNE))
        yield from vstep(dve.tensor_scalar(wqk[:, :, 0:64], wqk[:, :, 0:64], QK ** -0.5, None, ALU.mult))
        yield from vstep(dve.tensor_scalar(bqk[0:64, :], bqk[0:64, :], QK ** -0.5, None, ALU.mult))
        zeros = junk_a[:].bitcast(F32)
        done("dve", dve.memset(zeros, 0.0), "zeros")
        need("sp", ("zeros",))
        zr = rec[TOK:TOK + 1, :]
        moved(sp.dma_start(zr[:, 0:D], zeros[0:1, :]), "zero", "zero", 0)
        moved(sp.dma_start(zr[:, D:2 * D], zeros[0:1, :]), "zero", "zero", 1)
        moved(sp.dma_start(zr[:, 2 * D:REC], zeros[0:1, 0:REC - 2 * D]), "zero", "zero", 2)

    def setup_rest():
        yield from vstep(dve.tensor_reduce(wsum[:, 0:1], w0[:], AX.XY, ALU.add, apply_absolute_value=True))
        need("pe", mine[0])
        bk, rd = yield from take()
        done("pe", pe.matmul(bk[:, 0:1], ones[:], wsum[:, 0:1], start=True, stop=True), "w0sum")
        yield
        need("dve", ("w0sum",))
        yield from vstep(dve.tensor_scalar(sc0[:], bk[:, 0:1], 1.0 / (D * D), 1e-5, ALU.mult, ALU.max))
        rd.append(mine[0])
        yield from vstep(dve.reciprocal(wsum[:, 1:2], sc0[:]))
        yield from vstep(dve.tensor_scalar(w0[:], w0[:], wsum[:, 1:2], RNE, ALU.mult, ALU.add))
        yield from vstep(dve.tensor_scalar(w0[:], w0[:], RNE + 1.0, RNE - 1.0, ALU.min, ALU.max))
        yield from vstep(dve.tensor_scalar(w0[:], w0[:], RNE, None, ALU.subtract))
        need("pe", mine[0])
        bk, rd = yield from take()
        for c in range(DC):
            for o in range(DC):
                last = pe.transpose(bk[:, c * D + o * P:c * D + (o + 1) * P], w0[:, o, c * P:(c + 1) * P], ident[:])
        done("pe", last, "w0T")
        yield
        need("act", ("w0T",))
        done("act", act.activation(W0T[:], bk[:].rearrange("p (c o) -> p c o", c=DC), ACT.Copy), "W0T")
        rd.append(("W0T",))
        for c in range(DC):
            for s in range(2):
                part = wall[:, c, s * D:(s + 1) * D]
                yield from vstep(dve.tensor_reduce(tmp2[:, 2 * c + s:2 * c + s + 1], part, AX.X, ALU.add))
                yield from vstep(dve.tensor_scalar(tmp2[:, 2 * c + s:2 * c + s + 1], tmp2[:, 2 * c + s:2 * c + s + 1], 1.0 / D, None, ALU.mult))
                yield from vstep(dve.tensor_scalar(part, part, tmp2[:, 2 * c + s:2 * c + s + 1], None, ALU.subtract))
            yield from vstep(dve.tensor_copy(Mh[:, c, D:D + 2], tmp2[:, 2 * c:2 * c + 2]))
            yield from vstep(dve.tensor_tensor(Ml[:, c, D:D + 2], tmp2[:, 2 * c:2 * c + 2], Mh[:, c, D:D + 2].bitcast(F32), ALU.subtract))
        yield from vstep(dve.tensor_copy(WCh[:], wall[:, :, 0:2 * D]))
        yield from vstep(dve.tensor_tensor(WCl[:], wall[:, :, 0:2 * D], WCh[:].bitcast(F32), ALU.subtract))
        rwv = rw
        for k in range(3):
            yield from vstep(dve.tensor_copy(RW3[:, :, k, :], rwv[:]))
            if k < 2:
                yield from vstep(dve.tensor_tensor(rwv[:], rwv[:], RW3[:, :, k, :], ALU.subtract))
        yield from vstep(dve.tensor_reduce(tmp2[:, 0:1], gam[:], AX.X, ALU.max, apply_absolute_value=True))
        yield from vstep(dve.tensor_reduce(tmp2[:, 1:2], bet[:], AX.X, ALU.max, apply_absolute_value=True))
        yield from vstep(dve.tensor_scalar(tmp2[:, 2:3], tmp2[:, 0:1], D ** 0.5, 1e-20, ALU.mult, ALU.add))
        yield from vstep(dve.tensor_tensor(tmp2[:, 2:3], tmp2[:, 2:3], tmp2[:, 1:2], ALU.add))
        yield from vstep(dve.tensor_scalar(hdn[:].bitcast(I32), tmp2[:, 2:3].bitcast(I32), 0x7F800000, None, ALU.bitwise_and))
        H_TOP = 2.0 ** 13
        yield from vstep(dve.tensor_scalar(hdn[:], hdn[:], 1.0 / H_TOP, None, ALU.mult))
        yield from vstep(dve.reciprocal(hup[:], hdn[:]))
        yield from vstep(dve.tensor_scalar(gam[:], gam[:], hup[:], None, ALU.mult))
        yield from vstep(dve.tensor_scalar(bet[:], bet[:], hup[:], None, ALU.mult))
        yield from vstep(dve.tensor_copy(hbound[:], tmp2[:, 2:3]))


    def expert(e):
        w1 = t["sw1"] if e == NE else t["ew1"][e]
        w2 = t["sw2"] if e == NE else t["ew2"][e]
        key = ("expert", e)
        if ("eq1",) in st.at:
            need("sp", ("eq1",), ("eq2",))
        moved(sp.dma_start(e1n[:], w1.rearrange("(c p) d -> p c d", p=P)), "e1n", "e1n", e)
        moved(sp.dma_start(e2n[:], w2.rearrange("(c p) f -> p c f", p=P)), "e2n", "e2n", e)
        for which, nat, q, nch, width, name in ((0, e1n, e1q, FC, D, "e1n"), (1, e2n, e2q, DC, FF, "e2n")):
            yield
            need("dve", (name, e))
            sc = esc[:, which, 0:nch]
            if ("dg",) in st.at:
                need("dve", ("dg",))
            yield from vstep(dve.tensor_reduce(sc, nat[:], AX.X, ALU.add, apply_absolute_value=True))
            yield from vstep(dve.tensor_scalar(sc, sc, 1.0 / width, 1e-5, ALU.mult, ALU.max))
            rs = esr[:, which, 0:nch]
            yield from vstep(dve.reciprocal(rs, sc))
            need("act", mine[0])
            for c in range(nch):
                last = act.activation(nat[:, c, :], nat[:, c, :], ACT.Identity, bias=rne[:, 0:1], scale=rs[:, c:c + 1])
            done("act", last, "eround")
            yield
            need("dve", ("eround",))
            yield from vstep(dve.tensor_scalar(nat[:], nat[:], RNE + 1.0, RNE - 1.0, ALU.min, ALU.max))
            if (f"et{which}",) in st.at:
                need("dve", (f"et{which}",))
            yield from vstep(dve.tensor_scalar(q[:], nat[:], RNE, None, ALU.subtract))
            st.at[(f"eq{which + 1}",)] = st.at[mine[0]]
            need("pe", mine[0])
            bk, rd = yield from take()
            b16 = bk[:].bitcast(F16)
            for c in range(width // P):
                for f in range(nch):
                    o = c * nch * P + f * P
                    last = pe.transpose(b16[:, o:o + P], q[:, f, c * P:(c + 1) * P], ident16[:])
            done("pe", last, f"et{which}")
            yield
            need("act", (f"et{which}",))
            dst = (E1T, E2T)[which][:, e, :, :]
            done("act", act.activation(dst, b16[:, 0:width // P * nch * P].rearrange("p (c m) -> p c m", m=nch * P), ACT.Copy), "ET", which, e)
            rd.append(("ET", which, e))
        yield from vstep(dve.tensor_scalar(e1s[:, e, :], esc[:, 0, :], hdn[:], None, ALU.mult))
        yield from vstep(dve.tensor_reduce(smax[:, e:e + 1], esc[:, 0, :], AX.X, ALU.max))
        for c in range(DC):
            yield from vstep(dve.tensor_scalar(dg[:, c, :], ident[:], esc[:, 1, c:c + 1], None, ALU.mult))
        need("pe", mine[0])
        bk, rd = yield from take()
        for c in range(DC):
            last = pe.matmul(bk[:, c * P:(c + 1) * P], ones[:], dg[:, c, :], start=True, stop=True)
        done("pe", last, "dg")
        yield
        need("act", ("dg",))
        done("act", act.activation(e2s[:, e, :], bk[:, 0:D], ACT.Copy), "e2s", e)
        rd.append(("e2s", e))


    def guards():
        yield from vstep(dve.tensor_reduce(smax[:, NE + 1:NE + 2], smax[:, 0:NE + 1], AX.X, ALU.max))
        need("pe", mine[0])
        bk, rd = yield from take()
        done("pe", pe.transpose(bk[0:1, 0:P], smax[:, NE + 1:NE + 2], ident[:]), "smaxT")
        yield
        need("dve", ("smaxT",))
        yield from vstep(dve.tensor_reduce(tmp2[0:1, 4:5], bk[0:1, 0:P], AX.X, ALU.max))
        rd.append(mine[0])
        yield from vstep(dve.tensor_scalar(tmp2[0:1, 4:5], tmp2[0:1, 4:5], hbound[0:1, :], float(D), ALU.mult, ALU.mult))
        need("pe", mine[0])
        bk, rd = yield from take()
        done("pe", pe.matmul(bk[:, 0:1], ones[0:1, :], tmp2[0:1, 4:5], start=True, stop=True), "sbound")
        yield
        need("dve", ("sbound",))
        yield from vstep(dve.tensor_copy(tmp2[:, 5:6], bk[:, 0:1]))
        rd.append(mine[0])
        yield from vstep(dve.tensor_scalar(sup[:].bitcast(I32), tmp2[:, 5:6].bitcast(I32), 0x7F800000, None, ALU.bitwise_and))
        yield from vstep(dve.tensor_scalar(sup[:], sup[:], 2.0 ** -13, None, ALU.mult))
        yield from vstep(dve.reciprocal(sdn[:], sup[:]))
        need("dve", ("e2s", 0))
        yield from vstep(dve.tensor_scalar(e2s[:], e2s[:], sup[:], None, ALU.mult))
        st.at[("guards",)] = st.at[mine[0]]

    def bn(x, which, b, j):
        done("dve", dve.bn_stats(bst[which][:, j, :], x), "bn", which, b, j)

    def aggregate(which, b, j):
        need("dve", ("bn", which, b, j))
        done("dve", dve.bn_aggr(mv[which][:, j, :], bst[which][:, j, :]), "mv", which, b, j)

    def root(which, b, n=NT):
        need("pool", ("mv", which, b, n - 1))
        r = rstd[which][:, 0:n]
        done("pool", pool.tensor_scalar(r, mv[which][:, 0:n, 1], 1.0, LN_EPS, ALU.mult, ALU.add), "veps", which, b)
        yield
        need("pool", ("veps", which, b))
        done("pool", pool.tensor_tensor(r, r, mhalf[:, 0:n], ALU.pow), "rstd", which, b)
        yield

    def normalise(out, x, which, b, j):
        need("dve", ("rstd", which, b), ("mv", which, b, j))
        return dve.tensor_scalar(out, x, mv[which][:, j, 0:1], rstd[which][:, j:j + 1], ALU.subtract, ALU.mult)

    def until(*key):
        while key not in st.at:
            yield

    def once(eng, *keys):
        for key in keys:
            yield from until(*key)
            need(eng, key)

    def a1_split(b):
        if b >= 1:
            yield from once("act", ("pv", b - 1, NT - 1))
        need("act", ("X", b))
        done("act", act.activation(Xh[:], X[b % 2][:], ACT.Copy), "Xh", b)
        yield
        need("pool", ("Xh", b))
        done("pool", pool.tensor_tensor(Xl[:], X[b % 2][:], Xh[:].bitcast(F32), ALU.subtract), "Xl", b)
        yield

    def a2_project(b):
        need("pe", ("XT", b))
        bk, rd = yield from take()
        for c in range(DC):
            last = pe.matmul(bk[:], wqk[:, c, :], XT[:, c, :], start=c == 0, stop=c == DC - 1)
        done("pe", last, "proj", b)
        yield
        need("act", ("proj", b))
        if b >= 1:
            need("act", ("score", b - 1, NT - 1))
        act.activation(Qs[0:64, :], bk[0:64, :], ACT.Identity, bias=bqk[0:64, :])
        done("act", act.activation(KH[0:64, :], bk[64:128, :], ACT.Identity, bias=bqk[64:128, :]), "qkhi", b)
        yield
        need("dve", ("qkhi", b))
        dve.scalar_tensor_tensor(Qs[32:64, :], bk[32:64, :], bqk[32:64, :], Qs[32:64, :].bitcast(F32),
                                 ALU.add, ALU.subtract)
        done("dve", dve.scalar_tensor_tensor(KL[0:64, :], bk[64:128, :], bqk[64:128, :],
                                             KH[0:64, :].bitcast(F32), ALU.add, ALU.subtract), "qklo", b)
        rd.append(("qklo", b))
        yield

    def b1_scores(b):
        need("pe", ("qklo", b))
        for i in range(NT):
            w = (i + 1) * P
            bk, rd = yield from take()
            q = Qs[:, i * P:(i + 1) * P]
            pe.matmul(bk[:, 0:w], q, KH[:, 0:w], start=True, stop=False)
            pe.matmul(bk[:, 0:w], q, KL[:, 0:w], start=False, stop=False)
            done("pe", pe.matmul(bk[:, i * P:w], identb[:], maskb[:], start=False, stop=True), "score", b, i)
            yield
            need("dve", ("score", b, i))
            done("dve", dve.tensor_reduce(NM[b % 2][:, i:i + 1], bk[:, 0:w], AX.X, ALU.max, negate=True), "max", b, i)
            yield
            need("act", ("max", b, i))
            if b >= 1 and i == 0:
                need("act", ("pT", b - 1, NT - 1))
            done("act", act.activation(PB[:, OFF[i]:OFF[i + 1]], bk[:, 0:w], ACT.Exp, bias=NM[b % 2][:, i:i + 1],
                                       accum_out=RS[b % 2][:, i:i + 1]), "exp", b, i)
            rd.append(("exp", b, i))
            yield

    def b2_transpose(b):
        for i in range(NT):
            need("pe", ("exp", b, i))
            bk, rd = yield from take()
            for k in range(i + 1):
                last = pe.transpose(bk[:, k * P:(k + 1) * P], PB[:, OFF[i] + k * P:OFF[i] + (k + 1) * P], ident[:])
            done("pe", last, "pT", b, i)
            yield
            need("act", ("pT", b, i))
            if b >= 1 and i == 0:
                yield from once("act", ("pv", b - 1, NT - 1))
            o = slice(OFF[i], OFF[i + 1])
            done("act", act.activation(PTh[:, o], bk[:, 0:(i + 1) * P], ACT.Copy), "pTh", b, i)
            yield
            need("dve", ("pTh", b, i))
            done("dve", dve.tensor_tensor(PTl[:, o], bk[:, 0:(i + 1) * P], PTh[:, o].bitcast(F32), ALU.subtract), "pTl", b, i)
            rd.append(("pTl", b, i))
            yield

    def b3_values(b):
        need("dve", ("exp", b, NT - 1))
        done("dve", dve.reciprocal(RI[b % 2][:], RS[b % 2][:]), "rinv", b)
        need("pe", ("Xl", b))
        for i in range(NT):
            need("pe", ("pTl", b, i))
            bk, rd = yield from take()
            for k in range(i + 1):
                o = slice(OFF[i] + k * P, OFF[i] + (k + 1) * P)
                pe.matmul(bk[:, 0:D], PTh[:, o], Xh[:, k, :], start=k == 0, stop=False)
                pe.matmul(bk[:, 0:D], PTh[:, o], Xl[:, k, :], start=False, stop=False)
                last = pe.matmul(bk[:, 0:D], PTl[:, o], Xh[:, k, :], start=False, stop=k == i)
            done("pe", last, "pv", b, i)
            yield
            need("dve", ("pv", b, i), ("rinv", b))
            if b >= 1 and i == 0:
                yield from once("dve", ("x1T", b - 1), ("x2", b - 1, NT - 1))
            done("dve", dve.scalar_tensor_tensor(X1[:, i, :], bk[:, 0:D], RI[b % 2][:, i:i + 1], X[b % 2][:, i, :],
                                                 ALU.mult, ALU.add), "x1", b, i)
            rd.append(("x1", b, i))
            yield
            need("dve", ("x1", b, i))
            bn(X1[:, i, :], 0, b, i)
            yield
            aggregate(0, b, i)
        yield
        yield from root(0, b)
        for i in range(NT):
            done("dve", normalise(X1[:, i, :], X1[:, i, :], 0, b, i), "x1n", b, i)
            yield

    def transposed(b, src, hi, lo, name, ready, reread, sums=None):
        for c in range(DC):
            bk, rd = yield from take()
            for j in range(NT):
                if c == 0:
                    need("pe", (ready, b, j))
                last = pe.transpose(bk[:, j * P:(j + 1) * P], src[:, j, c * P:(c + 1) * P], ident[:])
            done("pe", last, name, b, c)
            yield
            need("act", (name, b, c))
            if reread is not None:
                yield from once("act", reread)
            extra = dict(accum_out=sums[:, c:c + 1]) if sums is not None else {}
            done("act", act.activation(hi[:, c, :], bk[:], ACT.Copy, **extra), name + "h", b, c)
            yield
            need("dve", (name + "h", b, c))
            h = hi[:, c, :].bitcast(F32) if hi.dtype == F32R else hi[:, c, :]
            done("dve", dve.tensor_tensor(lo[:, c, :], bk[:], h, ALU.subtract), name + "l", b, c)
            rd.append((name + "l", b, c))
            yield
        st.at[(name, b)] = st.at[(name, b, DC - 1)]

    def c1_transpose(b):
        yield from transposed(b, X1, T1h, T1l, "x1T", "x1n", ("ffn", b - 1) if b >= 1 else None)

    def c2_linear(b):
        x2 = X2[b % NX2]
        if b == 0:
            need("pe", ("W0T",))
        for j in range(NT):
            need("pe", ("x1Tl", b, DC - 1))
            bk, rd = yield from take()
            for c in range(DC):
                pe.matmul(bk[:, 0:D], T1h[:, c, j * P:(j + 1) * P], W0T[:, c, :], start=c == 0, stop=False)
                last = pe.matmul(bk[:, 0:D], T1l[:, c, j * P:(j + 1) * P], W0T[:, c, :], start=False, stop=c == DC - 1)
            done("pe", last, "ffn", b, j)
            yield
            need("dve", ("ffn", b, j))
            if b >= NX2 and j == 0:
                yield from once("dve", ("r", b - NX2))
            done("dve", dve.scalar_tensor_tensor(x2[:, j, :], bk[:, 0:D], sc0[:], X1[:, j, :], ALU.mult, ALU.add),
                 "x2", b, j)
            rd.append(("x2", b, j))
            yield
            need("dve", ("x2", b, j))
            bn(x2[:, j, :], 1, b, j)
            yield
            aggregate(1, b, j)
        st.at[("ffn", b)] = st.at[("ffn", b, NT - 1)]
        yield
        yield from root(1, b)
        for j in range(NT):
            done("dve", normalise(x2[:, j, :], x2[:, j, :], 1, b, j), "x2n", b, j)
            yield

    def d1_transpose(b):
        if b >= 2:
            need("act", ("gate1", b - 2))
        yield from transposed(b, X2[b % NX2], TTh, TTl, "x2T", "x2n", ("u", b - 1) if b >= 1 else None, sums=SUMS[b % 2])
        need("pool", ("x2T", b))
        done("pool", pool.tensor_tensor(X2[b % NX2][:], X2[b % NX2][:], pb_row[:, None, :].to_broadcast([P, NT, D]), ALU.add),
             "x2b", b)
        yield

    last_of = {}

    def d2_stats(b):
        g, col = b // GB, (b % GB) * NT
        need("pe", ("x2Tl", b, DC - 1), ("x2Th", b, DC - 1))
        bk, rd = yield from take()
        for c in range(DC):
            last = pe.matmul(bk[0:RED, 0:1], cw1[:, c, :], SUMS[b % 2][:, c:c + 1], start=c == 0, stop=c == DC - 1)
        done("pe", last, "gate1", b)
        yield
        need("act", ("gate1", b))
        if b >= 1:
            need("act", ("gate2", b - 1))
        done("act", act.activation(R1[:], bk[0:RED, 0:1], ACT.Relu, bias=cb1[:], scale=1.0 / SEQ), "gate_r", b)
        rd.append(("gate_r", b))

        def tile(j):
            bk, rd = yield from take()
            for c in range(DC):
                o = slice(j * P, (j + 1) * P)
                pe.matmul(bk[:], TTh[:, c, o], WCh[:, c, :], start=c == 0, stop=False)
                pe.matmul(bk[:], TTh[:, c, o], WCl[:, c, :], start=False, stop=False)
                last = pe.matmul(bk[:], TTl[:, c, o], WCh[:, c, :], start=False, stop=c == DC - 1)
            done("pe", last, "dqk", b, j)
            yield
            need("act", ("dqk", b, j))
            if "qk" in last_of:
                need("act", last_of["qk"])
            act.activation(DK[:], bk[:, D:2 * D], ACT.Copy)
            if g >= 2 and b % GB == 0 and j == 0:
                need("act", ("ode", g - 2))
            need("act", last_of.get("sq", ("zero", 2)))
            done("act", act.activation(junk_a[:], bk[:], ACT.Square, accum_out=S2[g % 2][:, col + j:col + j + 1]), "sq", b, j)
            last_of["sq"] = ("sq", b, j)
            yield
            need("dve", ("sq", b, j))
            done("dve", dve.tensor_tensor_reduce(out=bk[:, 0:D], in0=bk[:, 0:D], in1=DK[:], scale=1.0, scalar=0.0,
                                                 op0=ALU.mult, op1=ALU.add,
                                                 accum_out=SQK[g % 2][:, col + j:col + j + 1]), "sqk", b, j)
            last_of["qk"] = ("sqk", b, j)
            rd.append(("sqk", b, j))

        yield from tile(0)
        need("pe", ("gate_r", b))
        bk, rd = yield from take()
        for c in range(DC):
            last = pe.matmul(bk[:, c:c + 1], cw2[:, c * P:(c + 1) * P], R1[:], start=True, stop=True)
        done("pe", last, "gate2", b)
        yield
        need("dve", ("gate2", b))
        if b >= 1:
            need("dve", ("ps", b - 1))
        yield from vstep(dve.tensor_tensor(CHW[:], bk[:, 0:DC], cb2[:], ALU.add))
        rd.append(mine[0])
        yield from vstep(dve.tensor_scalar(CHW[:], CHW[:], -80.0, None, ALU.max))
        need("act", mine[0])
        done("act", act.activation(CHW[:], CHW[:], ACT.Exp, scale=-1.0), "gexp", b)
        yield from tile(1)
        need("dve", ("gexp", b))
        yield from vstep(dve.tensor_scalar(CHW[:], CHW[:], 1.0, None, ALU.add))
        yield from vstep(dve.reciprocal(CHW[:], CHW[:]))
        need("act", mine[0])
        if b >= 1:
            need("act", ("fuse", b - 1))
        for c in range(DC):
            last = act.activation(PS[:, c, :], pw[:, c, :], ACT.Copy, scale=CHW[:, c:c + 1])
        done("act", last, "ps", b)
        yield from tile(2)
        yield from tile(3)
        need("pe", ("ps", b))
        bk, rd = yield from take()
        for m in range(DC):
            for c in range(DC):
                last = pe.matmul(bk[:, m * D:(m + 1) * D], wvT[:, c, m * P:(m + 1) * P], PS[:, c, :], start=c == 0,
                                 stop=c == DC - 1)
        done("pe", last, "fuse", b)
        yield
        need("act", ("fuse", b))
        if b >= 1:
            need("act", ("u", b - 1))
        fused = bk[:].rearrange("p (m n) -> p m n", m=DC)
        done("act", act.activation(Mh[:, :, 0:D], fused, ACT.Copy), "Mh", b)
        yield
        need("dve", ("Mh", b))
        done("dve", dve.tensor_tensor(Ml[:, :, 0:D], fused, Mh[:, :, 0:D].bitcast(F32), ALU.subtract), "Ml", b)
        rd.append(("Ml", b))
        yield

    def d3_values(b):
        need("pe", ("Ml", b))
        if b >= 4:
            yield from until("x3", b - 4, NT - 1)
        for j in range(NT):
            bk, rd = yield from take()
            for c in range(DC):
                o = slice(j * P, (j + 1) * P)
                pe.matmul(bk[:, 0:D + 2], TTh[:, c, o], Mh[:, c, :], start=c == 0, stop=False)
                pe.matmul(bk[:, 0:D + 2], TTh[:, c, o], Ml[:, c, :], start=False, stop=False)
                last = pe.matmul(bk[:, 0:D + 2], TTl[:, c, o], Mh[:, c, :], start=False, stop=c == DC - 1)
            done("pe", last, "u", b, j)
            yield
            need("act", ("u", b, j))
            if b >= 4:
                need("act", ("x3", b - 4, NT - 1))
            done("act", act.activation(U[b % 4][:, j, :], bk[:, 0:D + 2], ACT.Copy), "U", b, j)
            rd.append(("U", b, j))
        st.at[("u", b)] = st.at[("u", b, NT - 1)]
        yield

    o_mm = sb("o_mm", [P, GC])
    o_d1 = sb("o_d1", [P, GC])
    o_kk = sb("o_kk", [P, GC])
    o_n2 = sb("o_n2", [P, GC])
    o_A = sb("o_A", [P, GB, NT])
    o_h = sb("o_h", [P, 2, GB, 2, NT])
    o_sq = sb("o_sq", [P, 2, GB, 2, NT])
    o_mean = sb("o_mean", [P, 2 * GB])
    o_rs = sb("o_rs", [P, 2 * GB])
    o_t = sb("o_t", [P, TAPS, GB, NT])
    o_e = sb("o_e", [P, GB, NT])
    o_s = sb("o_s", [P, GB])

    def neighbours(out, prev, nxt, extra=None):
        o1, o2 = out
        pe.matmul(o1, from_prev[:], prev, start=True, stop=False)
        pe.matmul(o1[:, :, 1:NT], edge_prev[:], prev[:, :, 0:NT - 1], start=False, stop=extra is None)
        if extra is not None:
            pe.matmul(o1, ident[:], extra, start=False, stop=False)
        pe.matmul(o2, from_next[:], nxt, start=extra is None, stop=False)
        return pe.matmul(o2[:, :, 0:NT - 1], edge_next[:], nxt[:, :, 1:NT], start=False, stop=True)

    def ode(g):
        last_b = GB * g + GB - 1
        need("dve", *[("U", b, NT - 1) for b in range(GB * g, last_b + 1)], ("sqk", last_b, NT - 1), ("sq", last_b, NT - 1))
        for i in range(GB):
            b = GB * g + i
            mq, mk = U[b % 4][:, :, D], U[b % 4][:, :, D + 1]
            c = slice(i * NT, (i + 1) * NT)
            dve.tensor_tensor(o_mm[:, c], mq, mk, ALU.mult)
            dve.tensor_tensor(o_d1[:, c], mq, mq, ALU.mult)
            last = dve.tensor_tensor(o_kk[:, c], mk, mk, ALU.mult)
        yield from vstep(last)
        c1, c2 = cc[:, 0:1], cc[:, 1:2]
        s2, sqk = S2[g % 2][:], SQK[g % 2][:]
        dve.tensor_scalar(o_mm[:], o_mm[:], 2.0, c1, ALU.mult, ALU.add)
        dve.scalar_tensor_tensor(o_d1[:], o_d1[:], c1, o_kk[:], ALU.add, ALU.add)
        dve.tensor_scalar(o_n2[:], sqk, 2.0 / (D - 1), c2, ALU.mult, ALU.add)
        yield from vstep(dve.tensor_scalar(s2, s2, 1.0 / (D - 1), c2, ALU.mult, ALU.add))
        dve.tensor_tensor(o_mm[:], o_mm[:], o_n2[:], ALU.mult)
        yield from vstep(dve.tensor_tensor(o_d1[:], o_d1[:], s2, ALU.mult))
        yield from vstep(dve.tensor_scalar(o_d1[:], o_d1[:], 1e-7, None, ALU.add))
        yield from vstep(dve.reciprocal(o_d1[:], o_d1[:]))
        yield from vstep(dve.tensor_tensor(o_mm[:], o_mm[:], o_d1[:], ALU.mult))
        A = o_A[:].rearrange("p b j -> p (b j)")
        yield from vstep(dve.tensor_tensor(A, o_mm[:], o_mm[:], ALU.mult))
        st.at[("ode", g)] = st.at[mine[0]]
        need("pe", mine[0])
        bk, rd = yield from take()
        left = bk[:, 0:GC].rearrange("p (b j) -> p b j", b=GB)
        right = bk[:, GC:2 * GC].rearrange("p (b j) -> p b j", b=GB)
        done("pe", neighbours((left, right), o_A[:], o_A[:]), "nb", g)
        yield
        need("dve", ("nb", g))
        h = [o_h[:, ch // 2, :, ch % 2, :] for ch in range(CH)]
        for tap, src in enumerate((left, o_A[:], right)):
            for ch in range(CH):
                w = c1w[:, ch * TAPS + tap:ch * TAPS + tap + 1]
                if tap == 0:
                    last = dve.tensor_scalar(h[ch], src, w, None, ALU.mult)
                else:
                    last = dve.scalar_tensor_tensor(h[ch], src, w, h[ch], ALU.mult, ALU.add)
            yield from vstep(last)
        rd.append(mine[0])
        hf = o_h[:].rearrange("p g b c j -> p (g b) (c j)")
        sqf = o_sq[:].rearrange("p g b c j -> p (g b) (c j)")
        flat = o_h[:].rearrange("p g b c j -> p (g b c j)")

        def over_tokens(src, key):
            need("pe", mine[0])
            bk, rd = yield from take()
            done("pe", pe.matmul(bk[:, 0:src.shape[-1]], ones[:], src, start=True, stop=True), key, g)
            yield
            need("dve", (key, g))
            return bk, rd

        bk, rd = yield from over_tokens(flat, "gn1")
        yield from vstep(dve.tensor_reduce(o_mean[:], bk[:, 0:2 * GB * 2 * NT].rearrange("p (k m) -> p k m", k=2 * GB), AX.X, ALU.add))
        rd.append(mine[0])
        yield from vstep(dve.tensor_scalar(o_mean[:], o_mean[:], 1.0 / (2 * SEQ), None, ALU.mult))
        yield from vstep(dve.tensor_tensor(hf, hf, o_mean[:, :, None].to_broadcast([P, 2 * GB, 2 * NT]), ALU.subtract))
        yield from vstep(dve.tensor_tensor(sqf, hf, hf, ALU.mult))
        bk, rd = yield from over_tokens(o_sq[:].rearrange("p g b c j -> p (g b c j)"), "gn2")
        yield from vstep(dve.tensor_reduce(o_rs[:], bk[:, 0:2 * GB * 2 * NT].rearrange("p (k m) -> p k m", k=2 * GB), AX.X, ALU.add))
        rd.append(mine[0])
        yield from vstep(dve.tensor_scalar(o_rs[:], o_rs[:], 1.0 / (2 * SEQ), 1e-5, ALU.mult, ALU.add))
        need("pool", mine[0])
        done("pool", pool.tensor_tensor(o_rs[:], o_rs[:], mhalf[:, 0:2 * GB], ALU.pow), "gnr", g)
        yield
        need("dve", ("gnr", g))
        yield from vstep(dve.tensor_tensor(hf, hf, o_rs[:, :, None].to_broadcast([P, 2 * GB, 2 * NT]), ALU.mult))
        for ch in range(CH):
            last = dve.tensor_scalar(h[ch], h[ch], gng[:, ch:ch + 1], gnb[:, ch:ch + 1], ALU.mult, ALU.add)
        yield from vstep(last)
        yield from vstep(dve.tensor_scalar(flat, flat, 0.0, None, ALU.max))
        for ch in range(CH):
            for tap in range(TAPS):
                w = c2w[:, ch * TAPS + tap:ch * TAPS + tap + 1]
                if ch == 0:
                    last = dve.tensor_scalar(o_t[:, tap], h[ch], w, None, ALU.mult)
                else:
                    last = dve.scalar_tensor_tensor(o_t[:, tap], h[ch], w, o_t[:, tap], ALU.mult, ALU.add)
            yield from vstep(last)
        need("pe", mine[0])
        bk, rd = yield from take()
        y = bk[:, 0:GC].rearrange("p (b j) -> p b j", b=GB)
        done("pe", neighbours((y, y), o_t[:, 0], o_t[:, 2], extra=o_t[:, 1]), "nb2", g)
        yield
        need("dve", ("nb2", g))
        yield from vstep(dve.scalar_tensor_tensor(o_e[:], y, c2b[:], o_A[:], ALU.add, ALU.add))
        rd.append(mine[0])
        yield from vstep(dve.tensor_scalar(o_e[:], o_e[:], -80.0, None, ALU.max))
        need("act", mine[0])
        done("act", act.activation(o_e[:], o_e[:], ACT.Exp, scale=-1.0), "oexp", g)
        yield
        need("dve", ("oexp", g))
        yield from vstep(dve.tensor_scalar(o_e[:], o_e[:], 1.0, None, ALU.add))
        yield from vstep(dve.reciprocal(o_e[:], o_e[:]))
        need("act", mine[0])
        done("act", act.activation(o_e[:], o_e[:], ACT.Exp), "oexp2", g)
        yield
        need("dve", ("oexp2", g))
        yield from vstep(dve.tensor_reduce(o_s[:], o_e[:], AX.X, ALU.add))
        bk, rd = yield from over_tokens(o_s[:], "osum")
        yield from vstep(dve.reciprocal(o_s[:], bk[:, 0:GB]))
        rd.append(mine[0])
        yield from vstep(dve.tensor_tensor(WT[g % 2][:], o_e[:], o_s[:, :, None].to_broadcast([P, GB, NT]), ALU.mult))
        st.at[("weights", g)] = st.at[mine[0]]

    recv = rec[0:TOK, :].rearrange("(b j p) c -> b p j c", j=NT, p=P)

    def f1_norms(b):
        g = b // GB
        x3 = X2[b % NX2]
        need("dve", ("weights", g), ("x2b", b), ("U", b, NT - 1))
        for j in range(NT):
            done("dve", dve.scalar_tensor_tensor(x3[:, j, :], U[b % 4][:, j, 0:D], WT[g % 2][:, b % GB, j:j + 1],
                                                 x3[:, j, :], ALU.mult, ALU.add), "x3", b, j)
            yield
            need("dve", ("x3", b, j))
            bn(x3[:, j, :], 2, b, j)
            yield
            aggregate(2, b, j)
        yield
        yield from root(2, b)
        for j in range(NT):
            done("dve", normalise(x3[:, j, :], x3[:, j, :], 2, b, j), "x3n", b, j)
            yield
            need("dve", ("x3n", b, j))
            bn(x3[:, j, :], 3, b, j)
            yield
            aggregate(3, b, j)
        yield
        yield from root(3, b)
        if b >= 1:
            need("dve", ("h16", b - 1))
        for j in range(NT):
            done("dve", normalise(HN[:, j, :], x3[:, j, :], 3, b, j), "hn", b, j)
            yield
        need("pool", ("hn", b, NT - 1))
        done("pool", pool.tensor_tensor(HN[:], HN[:], gam[:, None, :].to_broadcast([P, NT, D]), ALU.mult), "hg", b)
        yield
        need("pool", ("hg", b))
        done("pool", pool.tensor_tensor(HN[:], HN[:], bet[:, None, :].to_broadcast([P, NT, D]), ALU.add), "h", b)
        yield

    def ht_of(b):
        return HT[b - (B - HELD) + 1] if B - HELD <= b < B - 1 else HT[0]

    def f2_router(b):
        h16 = H16
        need("act", ("h", b))
        if b >= 1:
            need("act", ("hrec", b - 1), ("hT", b - 1))
        done("act", act.activation(h16[:, :, 0, :], HN[:], ACT.Copy), "hhi", b)
        yield
        need("dve", ("hhi", b))
        done("dve", dve.tensor_tensor(h16[:, :, 1, :], HN[:], h16[:, :, 0, :], ALU.subtract), "h16", b)
        yield
        need("sp", ("h16", b))
        moved(sp.dma_start(recv[b][:, :, 0:D], h16[:].rearrange("p j s d -> p j (s d)").bitcast(F32)),
              "hrec", "hrec", b)
        ht = ht_of(b)
        need("pe", ("h16", b))
        for s in range(2):
            bk, rd = yield from take()
            b16 = bk[:].bitcast(F16)
            for c in range(DC):
                for j in range(NT):
                    o = c * SEQ + j * P
                    last = pe.transpose(b16[:, o:o + P], h16[:, j, s, c * P:(c + 1) * P], ident16[:])
            done("pe", last, "hT", b, s)
            yield
            if b > 0:
                need("act", ("up", min(b, B - HELD) - 1, FC - 1))
            if b == B - HELD and s == 0:
                need("act", ("u", B - 1), ("Ml", B - 1), ("Xl", B - 1))
            need("act", ("hT", b, s))
            done("act", act.activation(ht[:, s].rearrange("p c n -> p (c n)"), b16, ACT.Copy), "HT", b, s)
            rd.append(("HT", b, s))
        st.at[("hT", b)] = st.at[("hT", b, 1)]
        yield
        need("pe", ("HT", b, 1))
        bk, rd = yield from take()
        W3 = 3 * NE
        for j in range(NT):
            for k, (s, c) in enumerate([(s, c) for s in range(2) for c in range(DC)]):
                last = pe.matmul(bk[:, j * W3:(j + 1) * W3], ht[:, s, c, j * P:(j + 1) * P],
                                 RW3[:, c].rearrange("p k e -> p (k e)"), start=k == 0, stop=k == 3)
        done("pe", last, "logits", b)
        yield
        need("dve", ("logits", b))
        lg = r_lg
        yield from vstep(dve.tensor_reduce(lg[:], bk[:, 0:NT * W3].rearrange("p (j k e) -> p j e k", j=NT, k=3), AX.X, ALU.add))
        rd.append(mine[0])
        T = slice(b * NT, (b + 1) * NT)

        def wide(x):
            return x[:, :, None].to_broadcast([P, NT, NE])

        yield from vstep(dve.tensor_reduce(r_mx[:], lg[:], AX.X, ALU.max))
        dve.tensor_tensor(r_eq[:], lg[:], wide(r_mx), ALU.is_equal)
        yield from vstep(dve.tensor_tensor(lg[:], lg[:], wide(r_mx), ALU.subtract))
        need("act", mine[0])
        done("act", act.activation(lg[:], lg[:], ACT.Exp, scale=hdn[:]), "rexp", b)
        yield from vstep(dve.tensor_tensor(r_eq[:], r_eq[:], desc8[:, None, :].to_broadcast([P, NT, NE]), ALU.mult))
        yield from vstep(dve.tensor_reduce(r_mx[:], r_eq[:], AX.X, ALU.max))
        yield from vstep(dve.tensor_tensor(OH[:, T, :], r_eq[:], wide(r_mx), ALU.is_equal))
        need("dve", ("rexp", b))
        yield from vstep(dve.tensor_reduce(r_mx[:], lg[:], AX.X, ALU.add))
        yield from vstep(dve.reciprocal(GATE[:, T], r_mx[:]))
        st.at[("gate", b)] = st.at[mine[0]]

    r_lg = sb("r_lg", [P, NT, NE])
    r_mx = sb("r_mx", [P, NT])
    r_eq = sb("r_eq", [P, NT, NE])

    def g1_shared(b):
        ht = ht_of(b)
        for f in range(FC):
            bk, rd = yield from take()
            for k, (s, c) in enumerate([(s, c) for s in range(2) for c in range(DC)]):
                last = pe.matmul(bk[:], E1T[:, NE, c, f * P:(f + 1) * P], ht[:, s, c, :], start=k == 0, stop=k == 3)
            done("pe", last, "up", b, f)
            yield
            n = b * FC + f
            need("act", ("up", b, f))
            s = S[n % 2]
            if n >= 2:
                need("act", ("Sl", n - 2))
            done("act", act.activation(s[:], bk[:], ACT.Silu, scale=e1s[:, NE, f:f + 1]), "silu", n)
            rd.append(("silu", n))
            yield
            need("dve", ("silu", n))
            if f == 0 and b >= 1:
                need("dve", ("down", b - 1, NT - 1))
            done("dve", dve.tensor_scalar(Sh[:, f, :], s[:], sdn[:], None, ALU.mult), "Sh", n)
            yield
            need("dve", ("Sh", n))
            done("dve", dve.scalar_tensor_tensor(Sl[:, f, :], s[:], sdn[:], Sh[:, f, :], ALU.mult, ALU.subtract), "Sl", n)
            yield

    def g2_shared(b):
        need("pe", ("Sl", b * FC + FC - 1))
        r = R
        for j in range(NT):
            bk, rd = yield from take()
            for k, (f, s) in enumerate([(f, s) for f in range(FC) for s in (Sh, Sl)]):
                last = pe.matmul(bk[:, 0:D], s[:, f, j * P:(j + 1) * P], E2T[:, NE, f, :], start=k == 0, stop=k == 2 * FC - 1)
            done("pe", last, "down", b, j)
            yield
            need("dve", ("down", b, j))
            if b >= 1 and j == 0:
                need("dve", ("rrec", b - 1))
            done("dve", dve.tensor_tensor(r[:, j, 0:D], bk[:, 0:D], e2s[:, NE, :], ALU.mult), "y", b, j)
            rd.append(("y", b, j))
            yield
        need("dve", ("gate", b))
        done("dve", dve.tensor_copy(r[:, :, D:D + 2], GATE[:, b * NT:(b + 1) * NT, None].to_broadcast([P, NT, 2])), "rg", b)
        yield
        need("pool", ("y", b, NT - 1), ("x3n", b, NT - 1))
        done("pool", pool.tensor_tensor(r[:, :, 0:D], r[:, :, 0:D], X2[b % NX2][:], ALU.add), "r", b)
        yield
        need("sp", ("r", b), ("rg", b))
        moved(sp.dma_start(recv[b][:, :, D:REC], r[:]), "rrec", "rrec", b)

    sort_bank = []

    def sort_places():
        need("pe", ("gate", B - 1))
        ohv = OH[:].rearrange("p t e -> p e t")
        bk1, rd1 = yield from take()
        bk2, rd2 = yield from take()
        pe.matmul(bk1[:], before[:], ohv, start=True, stop=True)
        done("pe", pe.matmul(bk2[:], onesb[:], ohv, start=True, stop=True), "counts")
        yield
        need("dve", ("counts",))
        dve.memset(q_z[:], 0.0)
        dve.tensor_copy(part_f[:], part_i[:])
        dve.tensor_copy(q_C[:], bk1[:].rearrange("p (e t) -> p e t", e=NE))
        yield from vstep(dve.tensor_copy(q_tot[:], bk2[:].rearrange("p (e t) -> p e t", e=NE)))
        rd1.append(mine[0])
        rd2.append(mine[0])
        dve.tensor_tensor(q_C[:], q_C[:], q_tot[:], ALU.subtract)
        yield from vstep(dve.tensor_reduce(q_n[:], q_tot[:], AX.X, ALU.add))
        yield from vstep(dve.tensor_scalar(q_ni[:], q_n[:], float(SLOT - 1), None, ALU.add))
        yield from vstep(dve.tensor_scalar(q_ni[:], q_ni[:], SLOT.bit_length() - 1, SLOT.bit_length() - 1,
                                ALU.logical_shift_right, ALU.logical_shift_left))
        yield from vstep(dve.tensor_copy(q_n[:], q_ni[:]))
        yield from vstep(dve.tensor_tensor_scan(q_end[:], q_n[:], q_z[:, 0:NE], 0.0, ALU.add, ALU.add))
        yield from vstep(dve.tensor_tensor(q_n[:], q_end[:], q_n[:], ALU.subtract))
        for e in range(NE):
            last = dve.tensor_tensor_scan(q_tot[:, e, :], q_tot[:, e, :], q_z[:], q_n[:, e:e + 1], ALU.add, ALU.add)
        yield from vstep(last)
        yield from vstep(dve.tensor_tensor(q_C[:], q_C[:], q_tot[:], ALU.add))
        yield from vstep(dve.tensor_tensor(q_C[:], q_C[:], ohv, ALU.mult))
        yield from vstep(dve.tensor_reduce(q_pos[:], q_C[:].rearrange("p e t -> p t e"), AX.X, ALU.add))
        yield from vstep(dve.tensor_copy(q_i[:], q_pos[:]))
        yield from vstep(dve.tensor_scalar(q_i[:], q_i[:], 7, None, ALU.logical_shift_right))
        yield from vstep(dve.tensor_copy(q_hi[:], q_i[:]))
        yield from vstep(dve.scalar_tensor_tensor(q_lo[:], q_hi[:], -float(P), q_pos[:], ALU.mult, ALU.add))
        yield from vstep(dve.tensor_tensor(q_ge[:], q_end[:, :, None].to_broadcast([P, NE, NG]), group_first[:, None, :].to_broadcast([P, NE, NG]), ALU.is_le))
        yield from vstep(dve.tensor_reduce(q_ex[:], q_ge[:].rearrange("p e g -> p g e"), AX.X, ALU.add))
        yield from vstep(dve.tensor_scalar(q_exi[:], q_ex[:], float(NE - 1), None, ALU.min))
        st.at[("experts",)] = st.at[mine[0]]

    def sort_invert(k):
        if k == 0:
            sort_bank.extend((yield from take()))
        bk, _ = sort_bank
        a, bb = q_A[k % 2], q_B[k % 2]
        T = slice(k * CHK, (k + 1) * CHK)
        if k >= 2:
            need("dve", ("inv", k - 2))
        dve.tensor_tensor(a[:], q_lo[:, T, None].to_broadcast([P, CHK, P]), iota_f[:, None, :].to_broadcast([P, CHK, P]), ALU.is_equal)
        yield from vstep(dve.tensor_tensor(bb[:, :, 1, :], q_hi[:, T, None].to_broadcast([P, CHK, NST]),
                                iota_f[:, None, 0:NST].to_broadcast([P, CHK, NST]), ALU.is_equal))
        yield from vstep(dve.tensor_tensor(bb[:, :, 0, :], bb[:, :, 1, :], tile_f[:, T, None].to_broadcast([P, CHK, NST]), ALU.mult))
        yield from vstep(dve.tensor_scalar(bb[:, :, 1, :], bb[:, :, 1, :], part_f[:], None, ALU.mult))
        need("pe", mine[0])
        for i in range(CHK):
            tt = k * CHK + i
            last = pe.matmul(bk[:, 0:2 * NST], a[:, i, :], bb[:, i].rearrange("p s h -> p (s h)"),
                             start=tt == 0, stop=tt == NTILE - 1)
        done("pe", last, "inv", k)
        yield

    def sort_ids():
        bk, rd = sort_bank
        need("dve", ("inv", NTILE // CHK - 1))
        yield from vstep(dve.tensor_scalar(ids_f[:], bk[:, 0:NST], float(P), float(TOK), ALU.mult, ALU.add))
        yield from vstep(dve.tensor_tensor(ids_f[:], ids_f[:], bk[:, NST:2 * NST], ALU.add))
        rd.append(mine[0])
        yield from vstep(dve.tensor_copy(ids[:], ids_f[:]))
        st.at[("ids",)] = st.at[mine[0]]

    pool_chain(pool.iota(group_first[:].bitcast(I32), pattern=[[SLOT, NG]], base=0, channel_multiplier=0))
    done("pool", pool.tensor_copy(group_first[:], group_first[:].bitcast(I32)), "gfirst")
    need("dve", ("gfirst",))

    expert_of = {}

    def gather(s):
        if s >= 3:
            yield from until("gx", s - 3, NGT - 1)
            need("pool", ("gx", s - 3, NGT - 1), ("gTr", s - 3))
        if s == 0:
            need("pool", ("ids",), ("hrec", B - 1), ("rrec", B - 1), ("zero", 2), *front_free)
        for j in range(NGT):
            tt = s * NGT + j
            moved(pool.indirect_dma_start(G_rec[s % 3][:, j, :], None, rec[:],
                                          bass.IndirectOffsetOnAxis(ids[:, tt:tt + 1], 0)), f"gat{s % 3}", "gat", s, j)
            yield

    def routed_up(s):
        g = G_rec[s % 3]
        for eng in ("pe", "act"):
            need(eng, ("experts",))
            expert_of[eng, s] = st.engines[eng].value_load(q_exi[0:1, s:s + 1], min_val=0, max_val=NE - 1)
        ep, ea = expert_of["pe", s], expert_of["act", s]
        need("pe", ("gat", s, NGT - 1))
        bk, rd = yield from take()
        b16 = bk[:].bitcast(F16)
        for j in range(NGT):
            h16 = g[:, j, 0:D].bitcast(F16)
            for s2 in range(2):
                for c in range(DC):
                    o = (s2 * DC + c) * SLOT + j * P
                    last = pe.transpose(b16[:, o:o + P], h16[:, s2 * D + c * P:s2 * D + (c + 1) * P], ident16[:])
        done("pe", last, "gTr", s)
        yield
        need("act", ("gTr", s))
        if s >= 2:
            need("act", ("gup", s - 2, FC - 1))
        done("act", act.activation(G_T[s % 2][:].rearrange("p s c n -> p (s c n)"), b16, ACT.Copy), "gT", s)
        rd.append(("gT", s))
        yield
        need("pe", ("gT", s))
        gt = G_T[s % 2]
        for f in range(0, FC, 2):
            bk, rd = yield from take()
            for ff in (f, f + 1):
                o = (ff - f) * SLOT
                for k, (s2, c) in enumerate([(s2, c) for s2 in range(2) for c in range(DC)]):
                    last = pe.matmul(bk[:, o:o + SLOT], E1T[:, bass.DynSlice(ep, 1), c, ff * P:(ff + 1) * P], gt[:, s2, c, :],
                                     start=k == 0, stop=k == 3)
                done("pe", last, "gup", s, ff)
            yield
            need("act", ("gup", s, f + 1))
            if s >= 2 and f == 0:
                need("act", ("gSl", s - 2, FC - 2))
            for ff in (f, f + 1):
                done("act", act.activation(G_S[s % 2][:, ff, :], bk[:, (ff - f) * SLOT:(ff - f + 1) * SLOT], ACT.Silu,
                                           scale=e1s[:, bass.DynSlice(ea, 1), ff]), "gsilu", s, ff)
            rd.append(("gsilu", s, f + 1))
            yield
            if s >= 2 and f == 0:
                need("act", ("gdown", s - 2, NGT - 1))
            o = slice(f, f + 2)
            need("act", ("gsilu", s, f + 1))
            done("act", act.activation(G_Sh[s % 2][:, o], G_S[s % 2][:, o], ACT.Copy, scale=sdn[:]), "gSh", s, f)
            yield
            need("dve", ("gSh", s, f))
            done("dve", dve.scalar_tensor_tensor(G_Sl[s % 2][:, o], G_S[s % 2][:, o], sdn[:], G_Sh[s % 2][:, o],
                                                 ALU.mult, ALU.subtract), "gSl", s, f)
            yield

    def routed_down(s):
        need("dve", ("experts",))
        ev = dve.value_load(q_exi[0:1, s:s + 1], min_val=0, max_val=NE - 1)
        ep = expert_of["pe", s]
        need("pe", ("gSl", s, FC - 2))
        g, y = G_rec[s % 3], G_y[s % 3]
        key = ("g", s)
        w = s % 4
        for j in range(NGT):
            bk, rd = yield from take()
            for k, (f, sx) in enumerate([(f, sx) for f in range(FC) for sx in (G_Sh, G_Sl)]):
                last = pe.matmul(bk[:, 0:D], sx[s % 2][:, f, j * P:(j + 1) * P], E2T[:, bass.DynSlice(ep, 1), f, :],
                                 start=k == 0, stop=k == 2 * FC - 1)
            done("pe", last, "gdown", s, j)
            yield
            need("dve", ("gdown", s, j), ("gat", s, NGT - 1))
            if s >= 3 and j == 0:
                need("dve", ("gout", s - 3, NGT - 1))
            done("dve", dve.scalar_tensor_tensor(y[:, j, :], bk[:, 0:D], g[:, j, 2 * D:2 * D + 1],
                                                 e2s[:, bass.DynSlice(ev, 1), :].rearrange("p o d -> p (o d)"),
                                                 ALU.mult, ALU.mult), "gy", s, j)
            rd.append(("gy", s, j))
            yield
            need("dve", ("gy", s, j))
            done("dve", dve.tensor_tensor(y[:, j, :], y[:, j, :], g[:, j, D:2 * D], ALU.add), "gx", s, j)
            yield
            need("dve", ("gx", s, j))
            bn(y[:, j, :], w, key, j)
            yield
            aggregate(w, key, j)
        yield
        yield from root(w, key, NGT)
        for j in range(NGT):
            done("dve", normalise(y[:, j, :], y[:, j, :], w, key, j), "gn", s, j)
            yield
            need("pool", ("gn", s, j))
            tt = s * NGT + j
            moved(pool.indirect_dma_start(t["out"], bass.IndirectOffsetOnAxis(ids[:, tt:tt + 1], 0), y[:, j, :], None,
                                          bounds_check=TOK - 1, oob_is_err=False), f"out{s % 3}", "gout", s, j)

    def together(*threads):
        live = [[0.0, n, thread] for n, thread in enumerate(threads)]
        while live:
            x = min(live)
            before = st.latest, len(st.at)
            ended = next(x[2], "end") == "end"
            if ended:
                live.remove(x)
            elif len(st.at) == before[1]:
                x[0] = max(x[0], min((y[0] for y in live if y is not x), default=x[0])) + 0.2
            else:
                x[0] = st.latest

    over = set()

    def after(*parts):
        while not over.issuperset(parts):
            yield

    def series(name, part, count, *before):
        for i in range(count):
            yield from after(*(x for x in before[0](i) if x[1] >= 0))
            yield from part(i)
            over.add((name, i))

    def scores(b):
        yield from until("X", b)
        yield from until("XT", b)
        yield from a1_split(b)
        yield from a2_project(b)
        if b + 1 < B:
            load_xT(b + 1)
        yield from b1_scores(b)
        yield from b2_transpose(b)

    def values(b):
        yield from b3_values(b)
        if b + 2 < B:
            load_x(b + 2)

    def linear(b):
        yield from c1_transpose(b)
        yield from c2_linear(b)
        yield from d1_transpose(b)

    def projections(b):
        yield from d2_stats(b)
        yield from d3_values(b)

    def norms(b):
        yield from f1_norms(b)
        yield from f2_router(b)

    def shared(b):
        yield from g1_shared(b)
        yield from g2_shared(b)

    def prepare(i):
        if i == 0:
            yield from setup_rest()
        else:
            for e in reversed(range(NE + 1)):
                yield from expert(e)
            yield from guards()
            for eng in ("act", "dve", "pool"):
                need(eng, ("guards",))

    def sorting():
        yield from after(("norms", B - 1))
        for eng in ("dve", "act"):
            need(eng, *front_free)
        yield from sort_places()
        for k in range(NTILE // CHK):
            yield from sort_invert(k)
        yield from sort_ids()

    front_free = [("u", B - 1), ("x3", B - 1, NT - 1), ("U", B - 1, NT - 1), ("Ml", B - 1), ("Xl", B - 1)]
    load_x(0)
    load_xT(0)
    load_x(1)
    together(setup_first())
    together(
        series("norms", norms, B, lambda b: [("ode", b // GB), ("prepare", 1)]),
        series("shared", shared, B, lambda b: [("norms", b)]),
        series("ode", ode, B // GB, lambda g: [("projections", g * GB + GB - 1)]),
        series("projections", projections, B, lambda b: [("linear", b), ("prepare", 0)]),
        series("linear", linear, B, lambda b: [("values", b), ("prepare", 0)]),
        series("values", values, B, lambda b: [("scores", b)]),
        series("scores", scores, B, lambda b: [("values", b - 2)]),
        series("prepare", prepare, 2, lambda i: []),
        sorting())
    together(
        series("down", routed_down, NG, lambda s: [("up", s)]),
        series("up", routed_up, NG, lambda s: [("gather", s), ("down", s - 2)]),
        series("gather", gather, NG, lambda s: [("down", s - 3)]))
    for s in range(NG - 3, NG):
        need("sp", ("gout", s, NGT - 1))
    for lane in ("small", "zero"):
        sp.wait_ge(st.sems["d_" + lane], st.count["d_" + lane])


def kernel(**inputs):
    import concourse.bacc as bacc
    from concourse.bass_utils import run_bass_kernel_spmd

    a = {k: np.ascontiguousarray(v) for k, v in inputs.items()}
    x = a["L0_attn_x"].reshape(TOK, D)
    wqk = np.zeros((D, 4, 32), x.dtype)
    bqk = np.zeros((4, 32, 1), x.dtype)
    for s, (w, b) in enumerate([("w_q", "b_q")] * 2 + [("w_k", "b_k")] * 2):
        wqk[:, s, :QK] = a["L0_attn_" + w].T
        bqk[s, :QK, 0] = a["L0_attn_" + b]
    wall = a["L1_attn_qkv_w"]
    arrays = {
        "x": x, "xT": np.ascontiguousarray(x.T), "wqk": wqk.reshape(D, P), "bqk": bqk.reshape(P, 1),
        "w0": a["L0_ffn_weight"], "wall": wall, "wvT": np.ascontiguousarray(wall[:, 2 * D:].T),
        "pw": a["L1_attn_proj_w"], "cw1": a["L1_attn_ch_w1"], "cb1": a["L1_attn_ch_b1"].reshape(RED, 1),
        "cw2": a["L1_attn_ch_w2"], "cb2": np.ascontiguousarray(a["L1_attn_ch_b2"].reshape(DC, P).T),
        "pb": a["L1_attn_proj_b"].reshape(1, D), "gam": a["L1_ffn_ln_gamma"].reshape(1, D),
        "bet": a["L1_ffn_ln_beta"].reshape(1, D),
        "cc": np.stack([a["L1_attn_c1"].reshape(()), a["L1_attn_c2"].reshape(())]).reshape(1, 2),
        "c1w": a["L1_attn_conv1_w"].reshape(1, CH * TAPS), "c2w": a["L1_attn_conv2_w"].reshape(1, CH * TAPS),
        "gng": a["L1_attn_gn_g"].reshape(1, CH), "gnb": a["L1_attn_gn_b"].reshape(1, CH),
        "c2b": a["L1_attn_conv2_b"].reshape(1, 1), "rw": np.ascontiguousarray(a["L1_ffn_router_w"].T),
        "sw1": a["L1_ffn_shared_w1"], "sw2": a["L1_ffn_shared_w2"],
        "ew1": a["L1_ffn_expert_w1"], "ew2": a["L1_ffn_expert_w2"],
    }
    nc = bacc.Bacc("TRN2", target_bir_lowering=False, num_devices=1)
    t = {k: nc.dram_tensor("in_" + k, v.shape, mybir.dt.from_np(v.dtype), kind="ExternalInput").ap() for k, v in arrays.items()}
    t["out"] = nc.dram_tensor("out", (TOK, D), F32, kind="ExternalOutput").ap()
    build_program(nc, t)
    r = run_bass_kernel_spmd(nc, [{"in_" + k: v for k, v in arrays.items()}], core_ids=[0])
    return r.results[0]["out"].reshape(B, SEQ, D)
```

```python
import numpy as np

import concourse.bass as bass
from concourse import mybir
from collections import deque
from contextlib import ExitStack

F32 = mybir.dt.float32
F32R = mybir.dt.float32r
F16 = mybir.dt.float16
BF16 = mybir.dt.bfloat16
I32 = mybir.dt.int32
ALU = mybir.AluOpType
ACT = mybir.ActivationFunctionType
AX = mybir.AxisListType

P = 128
B, SEQ, D = 16, 512, 256
TOK = B * SEQ
NT = SEQ // P
NTILE = TOK // P
DC = D // P
QK = 16
RED = D // 4
FF = 512
FC = FF // P
NE = 8
CH = 4
TAPS = 3
GB = 2
GC = GB * NT
SLOT = 256
NG = (TOK + NE * (SLOT - 1)) // SLOT
NST = NG * SLOT // P
REC = 2 * D + 2
LN_EPS = 1e-5
HELD = 2
NU = 4
NX2 = 5
RNE = 12582912.0
NEG = -1e30
BANK = 512


COST = {"pe": 0.5, "act": 0.4, "dve": 0.35, "pool": 1.0,
        "dqk": 1.84, "gdown": 1.5, "gup": 0.66, "pv": 1.23, "down": 1.06, "up": 1.03, "u": 0.67, "proj": 2.4,
        "gTr": 0.86, "hT": 0.86, "x2T": 0.55, "fuse": 1.7, "et": 0.8,
        "eround": 1.7, "ET": 0.9, "silu": 0.85, "gT": 0.9, "HT": 0.9, "gSh": 0.6, "qkhi": 1.14, "Xh": 1.0, "hhi": 0.95,
        "ps": 0.8, "v": 0.27, "gSl": 0.66, "Sl": 0.66, "qklo": 1.3, "x1Tl": 0.6, "x2Tl": 0.6, "h16": 2.3, "hn": 0.35, "Sh": 0.5,
        "mv": 0.08, "veps": 0.1, "rstd": 1.0, "Xl": 2.3, "x2b": 2.3, "hg": 2.3, "h": 2.3, "r": 2.3, "gnr": 1.2}
HANDOVER = 0.15
DMA_TIME = 3.0
STUCK = 0.2


class Steps:

    def __init__(self, nc, ctx):
        self.nc, self.ctx = nc, ctx
        self.engines = {"pe": nc.tensor, "act": nc.scalar, "dve": nc.vector, "pool": nc.gpsimd, "sp": nc.sync}
        self.sems, self.count, self.at, self.seen = {}, {}, {}, {}
        self.clock, self.ended, self.latest = dict.fromkeys(self.engines, 0.0), {}, 0.0

    def sem(self, name):
        if name not in self.sems:
            self.sems[name] = self.ctx.enter_context(self.nc.semaphore(name))
            self.count[name] = 0
        return self.sems[name]

    def done(self, eng, ins, *key):
        ins.then_inc(self.sem("s_" + eng), 1)
        self.count["s_" + eng] += 1
        self.at[key] = ("s_" + eng, self.count["s_" + eng])
        self.clock[eng] += COST.get(key[0], COST[eng])
        self.ended[self.at[key]] = self.latest = self.clock[eng] + HANDOVER

    def moved(self, ins, lane, *key):
        ins.then_inc(self.sem("d_" + lane), 16)
        self.count["d_" + lane] += 16
        self.at[key] = ("d_" + lane, self.count["d_" + lane])
        if lane[:3] in ("gat", "out"):
            self.clock["pool"] += COST["pool"]
            self.latest = self.clock["pool"]
        self.ended[self.at[key]] = self.latest + DMA_TIME

    def need(self, eng, *keys):
        for key in keys:
            name, value = self.at[key]
            if self.seen.get((eng, name), 0) < value:
                self.engines[eng].wait_ge(self.sems[name], value)
                self.seen[eng, name] = value
            self.clock[eng] = max(self.clock[eng], self.ended[name, value])


def build_program(nc, t):
    ctx = ExitStack()
    with ctx:
        program(nc, t, ctx)


def program(nc, t, ctx):
    pe, act, dve, pool, sp = nc.tensor, nc.scalar, nc.vector, nc.gpsimd, nc.sync
    st = Steps(nc, ctx)
    done, need, moved = st.done, st.need, st.moved

    start = -(-nc.sbuf_base // 64) * 64
    here = [start]

    def sb(name, shape, dt=F32):
        size = 4 if dt in (F32, F32R, I32) else 2
        for d in shape[1:]:
            size *= d
        at = here[0]
        here[0] = -(-(at + size) // 64) * 64
        assert here[0] <= nc.sbuf_usable_end, (name, here[0])
        return nc.alloc_sbuf_tensor_at(name, list(shape), dt, offset=at, align_bytes=32)

    def ring(name, n, shape, dt=F32):
        return [sb(f"{name}{i}", shape, dt) for i in range(n)]

    free_banks = deque((ctx.enter_context(nc.psum_tensor(f"bank{i}", [P, BANK], F32)), None) for i in range(8))

    class Lease:

        def __init__(self, bank):
            self.bank = bank

        def append(self, key):
            free_banks.append((self.bank, key))

    def take():
        while not free_banks:
            yield
        bank, key = free_banks.popleft()
        if key is not None:
            need("pe", key)
        return bank, Lease(bank)

    rec = nc.dram_tensor("rec", [TOK + 1, REC], F32)

    ident = sb("ident", [P, P])
    ident16 = sb("ident16", [P, P], F16)
    identb = sb("identb", [P, P], BF16)
    maskb = sb("maskb", [P, P], BF16)
    ones = sb("ones", [P, P])
    onesb = sb("onesb", [P, P], BF16)
    before = sb("before", [P, P], BF16)
    from_prev = sb("from_prev", [P, P])
    from_next = sb("from_next", [P, P])
    edge_prev = sb("edge_prev", [P, P])
    edge_next = sb("edge_next", [P, P])
    mhalf = sb("mhalf", [P, GC])
    iota_f = sb("iota_f", [P, P])
    part_i = sb("part_i", [P, 1], I32)
    desc8 = sb("desc8", [P, NE])

    iota_i = iota_f[:].bitcast(I32)
    n = [0]

    def pool_chain(ins):
        n[0] += 1
        done("pool", ins, "const", n[0])
        need("pool", ("const", n[0]))

    for m, v in ((ident, 0.0), (ident16, 0.0), (identb, 0.0), (maskb, 0.0), (ones, 1.0), (onesb, 1.0),
                 (before, 0.0), (from_prev, 0.0), (from_next, 0.0), (edge_prev, 0.0), (edge_next, 0.0),
                 (mhalf, -0.5)):
        ins = pool.memset(m[:], v)
    pool_chain(ins)
    for m, base in ((ident, 0), (ident16, 0), (identb, 0), (from_prev, 1), (from_next, -1),
                    (edge_prev, -(P - 1)), (edge_next, P - 1)):
        ins = pool.affine_select(out=m[:], in_=m[:], compare_op=ALU.not_equal, fill=1.0, base=base,
                                 pattern=[[-1, P]], channel_multiplier=1)
    pool.affine_select(out=maskb[:], in_=maskb[:], compare_op=ALU.is_ge, fill=NEG, base=0,
                       pattern=[[-1, P]], channel_multiplier=1)
    pool.affine_select(out=before[:], in_=before[:], compare_op=ALU.is_ge, fill=1.0, base=0,
                       pattern=[[-1, P]], channel_multiplier=1)
    pool.iota(iota_i, pattern=[[1, P]], base=0, channel_multiplier=0)
    pool_chain(pool.iota(part_i[:], pattern=[[0, 1]], base=0, channel_multiplier=1))
    pool_chain(pool.tensor_copy(iota_f[:], iota_i))
    done("pool", pool.tensor_scalar(desc8[:], iota_f[:, 0:NE], -1.0, float(NE), ALU.mult, ALU.add), "consts")

    wqk = sb("wqk", [P, DC, P])
    bqk = sb("bqk", [P, 1])
    pw = sb("pw", [P, DC, D])
    cw1 = sb("cw1", [P, DC, RED])
    cb1 = sb("cb1", [RED, 1])
    cw2 = sb("cw2", [RED, D])
    cb2 = sb("cb2", [P, DC])
    pb_row = sb("pb_row", [P, D])
    gam = sb("gam", [P, D])
    bet = sb("bet", [P, D])
    cc = sb("cc", [P, 2])
    c1w = sb("c1w", [P, CH * TAPS])
    c2w = sb("c2w", [P, CH * TAPS])
    gng = sb("gng", [P, CH])
    gnb = sb("gnb", [P, CH])
    c2b = sb("c2b", [P, 1])
    rw = sb("rw", [P, DC, NE])

    W0T = sb("W0T", [P, DC, D], F16)
    sc0 = sb("sc0", [P, 1])
    WCh = sb("WCh", [P, DC, 2 * D], F32R)
    WCl = sb("WCl", [P, DC, 2 * D], F32R)
    wvT = sb("wvT", [P, DC, D])
    RW3 = sb("RW3", [P, DC, 3, NE], BF16)
    E1T = sb("E1T", [P, NE + 1, DC, FF], F16)
    E2T = sb("E2T", [P, NE + 1, FC, D], F16)
    e1s = sb("e1s", [P, NE + 1, FC])
    e2s = sb("e2s", [P, NE + 1, D])
    hup = sb("hup", [P, 1])
    hdn = sb("hdn", [P, 1])
    sdn = sb("sdn", [P, 1])
    sup = sb("sup", [P, 1])
    esc = sb("esc", [P, 2, FC])
    esr = sb("esr", [P, 2, FC])
    rne = sb("rne", [P, 1])
    hbound = sb("hbound", [P, 1])
    smax = sb("smax", [P, NE + 2])
    wsum = sb("wsum", [P, 4])
    tmp2 = sb("tmp2", [P, 8])

    NM = ring("NM", 2, [P, NT])
    RS = ring("RS", 2, [P, NT])
    RI = ring("RI", 2, [P, NT])
    bst = ring("bst", 4, [P, NT, 6])
    mv = ring("mv", 4, [P, NT, 2])
    rstd = ring("rstd", 4, [P, NT])
    SUMS = ring("SUMS", 2, [P, DC])
    R1 = sb("R1", [RED, 1])
    CHW = sb("CHW", [P, DC])
    junk_a = sb("junk_a", [P, FF], BF16)
    S2 = ring("S2", 2, [P, GC])
    SQK = ring("SQK", 2, [P, GC])
    WT = ring("WT", 2, [P, GB, NT])
    OH = sb("OH", [P, NTILE, NE], BF16)
    GATE = sb("GATE", [P, NTILE])
    ids = sb("ids", [P, NST], I32)
    q_exi = sb("q_exi", [P, NG], I32)
    group_first = sb("group_first", [P, NG])

    X2 = ring("X2", NX2, [P, NT, D])

    late_start = here[0]
    HT = [sb("HT0", [P, 2, DC, SEQ], F16)]
    HN = sb("HN", [P, NT, D])
    H16 = sb("H16", [P, NT, 2, D], F16)
    S = ring("S", 2, [P, SEQ])
    Sh = sb("Sh", [P, FC, SEQ], F16)
    Sl = sb("Sl", [P, FC, SEQ], F16)
    R = sb("R", [P, NT, D + 2])
    late_end = here[0]

    here[0] = late_start
    w0 = sb("w0", [P, DC, D])
    wall = sb("wall", [P, DC, 3 * D])
    e1n = sb("e1n", [P, FC, D])
    e2n = sb("e2n", [P, DC, FF])
    e1q = sb("e1q", [P, FC, D], F16)
    e2q = sb("e2q", [P, DC, FF], F16)
    dg = sb("dg", [P, DC, P])
    assert here[0] <= late_end

    here[0] = late_end
    U = ring("U", NU, [P, NT, D + 2])
    front_start = here[0]
    X = ring("X", 2, [P, NT, D])
    XT = sb("XT", [P, DC, SEQ])
    Xh = sb("Xh", [P, NT, D], F32R)
    Xl = sb("Xl", [P, NT, D], F32R)
    Qs = sb("Qs", [P, SEQ], F32R)
    KH = sb("KH", [P, SEQ], F32R)
    KL = sb("KL", [P, SEQ], F32R)
    OFF = [P * i * (i + 1) // 2 for i in range(NT + 1)]
    PB = sb("PB", [P, OFF[NT]])
    PTh = sb("PTh", [P, OFF[NT]], F32R)
    PTl = sb("PTl", [P, OFF[NT]], F32R)
    X1 = sb("X1", [P, NT, D])
    T1h = sb("T1h", [P, DC, SEQ], F16)
    T1l = sb("T1l", [P, DC, SEQ], F16)
    TTh = sb("TTh", [P, DC, SEQ], F32R)
    TTl = sb("TTl", [P, DC, SEQ], F32R)
    PS = sb("PS", [P, DC, D])
    Mh = sb("Mh", [P, DC, D + 2], F32R)
    Ml = sb("Ml", [P, DC, D + 2], F32R)
    DK = sb("DK", [P, D])
    front_end = here[0]

    here[0] = front_start
    HT += [sb(f"HT{k}", [P, 2, DC, SEQ], F16) for k in range(1, HELD)]
    q_C = sb("q_C", [P, NE, NTILE])
    q_tot = sb("q_tot", [P, NE, NTILE])
    q_z = sb("q_z", [P, NTILE])
    q_n = sb("q_n", [P, NE])
    q_ni = sb("q_ni", [P, NE], I32)
    q_end = sb("q_end", [P, NE])
    q_pos = sb("q_pos", [P, NTILE])
    q_i = sb("q_i", [P, NTILE], I32)
    q_lo = sb("q_lo", [P, NTILE])
    q_hi = sb("q_hi", [P, NTILE])
    CHK = 4
    q_A = ring("q_A", 2, [P, CHK, P], BF16)
    q_B = ring("q_B", 2, [P, CHK, 2, NST], BF16)
    part_f = sb("part_f", [P, 1])
    ids_f = sb("ids_f", [P, NST])
    q_ge = sb("q_ge", [P, NE, NG])
    q_ex = sb("q_ex", [P, NG])
    NGT = SLOT // P
    NGR, NGB = 4, 3
    G_rec = ring("G_rec", NGR, [P, NGT, REC])
    G_T = ring("G_T", NGB, [P, 2, DC, SLOT], F16)
    G_S = ring("G_S", 2, [P, FC, SLOT])
    G_Sh = ring("G_Sh", NGB, [P, FC, SLOT], F16)
    G_Sl = ring("G_Sl", NGB, [P, FC, SLOT], F16)
    G_y = ring("G_y", 3, [P, NGT, D])
    assert here[0] <= front_end
    here[0] = front_end
    xv = t["x"].rearrange("(b j p) d -> b p j d", j=NT, p=P)
    xTv = t["xT"].rearrange("(c p) (b n) -> b p c n", p=P, n=SEQ)

    def load_x(b):
        if b >= 2:
            need("sp", ("x1", b - 2, NT - 1), ("Xl", b - 2))
        moved(sp.dma_start(X[b % 2][:], xv[b]), f"x{b % 2}", "X", b)

    def load_xT(b):
        if b >= 1:
            need("sp", ("proj", b - 1))
        moved(sp.dma_start(XT[:], xTv[b]), "xT", "XT", b)

    load_x(0)
    load_xT(0)
    small = [
        (wqk[:], t["wqk"].rearrange("(c p) m -> p c m", p=P)), (bqk[:], t["bqk"]),
        (w0[:], t["w0"].rearrange("(c p) i -> p c i", p=P)),
        (wall[:], t["wall"].rearrange("(c p) n -> p c n", p=P)),
        (wvT[:], t["wvT"].rearrange("(c p) n -> p c n", p=P)),
        (pw[:], t["pw"].rearrange("(c p) n -> p c n", p=P)),
        (cw1[:], t["cw1"].rearrange("(c p) n -> p c n", p=P)), (cb1[:], t["cb1"]), (cw2[:], t["cw2"]),
        (cb2[:], t["cb2"]), (pb_row[:], t["pb"].to_broadcast([P, D])), (gam[:], t["gam"].to_broadcast([P, D])),
        (bet[:], t["bet"].to_broadcast([P, D])), (cc[:], t["cc"].to_broadcast([P, 2])),
        (c1w[:], t["c1w"].to_broadcast([P, CH * TAPS])), (c2w[:], t["c2w"].to_broadcast([P, CH * TAPS])),
        (gng[:], t["gng"].to_broadcast([P, CH])), (gnb[:], t["gnb"].to_broadcast([P, CH])),
        (c2b[:], t["c2b"].to_broadcast([P, 1])), (rw[:], t["rw"].rearrange("(c p) e -> p c e", p=P)),
    ]
    for i, (dst, src) in enumerate(small):
        with nc.allow_non_contiguous_dma(reason="small weights, once"):
            moved((sp, act)[i % 2].dma_start(dst, src), "small", "small", i)
    st.at["small"] = st.at["small", len(small) - 1]
    st.at[("small",)] = st.at[("small", len(small) - 1)]

    chain = [0]
    mine = [None]

    def vstep(ins):
        chain[0] += 1
        n = chain[0]
        done("dve", ins, "v", n)
        yield
        need("dve", ("v", n))
        mine[0] = ("v", n)

    need("dve", ("small",), ("consts",))
    need("act", ("small",), ("consts",))
    need("pe", ("small",), ("consts",))
    need("pool", ("small",))
    def setup_first():
        for m in (Qs, KH, KL):
            dve.memset(m[:].bitcast(F32), 0.0)
        dve.memset(smax[:], 0.0)
        yield from vstep(dve.memset(rne[:], RNE))
        yield from vstep(dve.tensor_scalar(wqk[:, :, 0:64], wqk[:, :, 0:64], QK ** -0.5, None, ALU.mult))
        yield from vstep(dve.tensor_scalar(bqk[0:64, :], bqk[0:64, :], QK ** -0.5, None, ALU.mult))
        zeros = junk_a[:].bitcast(F32)
        done("dve", dve.memset(zeros, 0.0), "zeros")
        for eng in ("pe", "act"):
            need(eng, mine[0])
        need("sp", ("zeros",))
        zr = rec[TOK:TOK + 1, :]
        moved(sp.dma_start(zr[:, 0:D], zeros[0:1, :]), "zero", "zero", 0)
        moved(sp.dma_start(zr[:, D:2 * D], zeros[0:1, :]), "zero", "zero", 1)
        moved(sp.dma_start(zr[:, 2 * D:REC], zeros[0:1, 0:REC - 2 * D]), "zero", "zero", 2)

    def setup_rest():
        yield from vstep(dve.tensor_reduce(wsum[:, 0:1], w0[:], AX.XY, ALU.add, apply_absolute_value=True))
        need("pe", mine[0])
        bk, rd = yield from take()
        done("pe", pe.matmul(bk[:, 0:1], ones[:], wsum[:, 0:1], start=True, stop=True), "w0sum")
        yield
        need("dve", ("w0sum",))
        yield from vstep(dve.tensor_scalar(sc0[:], bk[:, 0:1], 1.0 / (D * D), 1e-5, ALU.mult, ALU.max))
        rd.append(mine[0])
        yield from vstep(dve.reciprocal(wsum[:, 1:2], sc0[:]))
        yield from vstep(dve.tensor_scalar(w0[:], w0[:], wsum[:, 1:2], RNE, ALU.mult, ALU.add))
        yield from vstep(dve.tensor_scalar(w0[:], w0[:], RNE + 1.0, RNE - 1.0, ALU.min, ALU.max))
        yield from vstep(dve.tensor_scalar(w0[:], w0[:], RNE, None, ALU.subtract))
        need("pe", mine[0])
        bk, rd = yield from take()
        for c in range(DC):
            for o in range(DC):
                last = pe.transpose(bk[:, c * D + o * P:c * D + (o + 1) * P], w0[:, o, c * P:(c + 1) * P], ident[:])
        done("pe", last, "w0T")
        yield
        need("act", ("w0T",))
        done("act", act.activation(W0T[:], bk[:].rearrange("p (c o) -> p c o", c=DC), ACT.Copy), "W0T")
        rd.append(("W0T",))
        for c in range(DC):
            for s in range(2):
                part = wall[:, c, s * D:(s + 1) * D]
                yield from vstep(dve.tensor_reduce(tmp2[:, 2 * c + s:2 * c + s + 1], part, AX.X, ALU.add))
                yield from vstep(dve.tensor_scalar(tmp2[:, 2 * c + s:2 * c + s + 1], tmp2[:, 2 * c + s:2 * c + s + 1], 1.0 / D, None, ALU.mult))
                yield from vstep(dve.tensor_scalar(part, part, tmp2[:, 2 * c + s:2 * c + s + 1], None, ALU.subtract))
            yield from vstep(dve.tensor_copy(Mh[:, c, D:D + 2], tmp2[:, 2 * c:2 * c + 2]))
            yield from vstep(dve.tensor_tensor(Ml[:, c, D:D + 2], tmp2[:, 2 * c:2 * c + 2], Mh[:, c, D:D + 2].bitcast(F32), ALU.subtract))
        yield from vstep(dve.tensor_copy(WCh[:], wall[:, :, 0:2 * D]))
        yield from vstep(dve.tensor_tensor(WCl[:], wall[:, :, 0:2 * D], WCh[:].bitcast(F32), ALU.subtract))
        rwv = rw
        for k in range(3):
            yield from vstep(dve.tensor_copy(RW3[:, :, k, :], rwv[:]))
            if k < 2:
                yield from vstep(dve.tensor_tensor(rwv[:], rwv[:], RW3[:, :, k, :], ALU.subtract))
        yield from vstep(dve.tensor_reduce(tmp2[:, 0:1], gam[:], AX.X, ALU.max, apply_absolute_value=True))
        yield from vstep(dve.tensor_reduce(tmp2[:, 1:2], bet[:], AX.X, ALU.max, apply_absolute_value=True))
        yield from vstep(dve.tensor_scalar(tmp2[:, 2:3], tmp2[:, 0:1], D ** 0.5, 1e-20, ALU.mult, ALU.add))
        yield from vstep(dve.tensor_tensor(tmp2[:, 2:3], tmp2[:, 2:3], tmp2[:, 1:2], ALU.add))
        yield from vstep(dve.tensor_scalar(hdn[:].bitcast(I32), tmp2[:, 2:3].bitcast(I32), 0x7F800000, None, ALU.bitwise_and))
        H_TOP = 2.0 ** 13
        yield from vstep(dve.tensor_scalar(hdn[:], hdn[:], 1.0 / H_TOP, None, ALU.mult))
        yield from vstep(dve.reciprocal(hup[:], hdn[:]))
        yield from vstep(dve.tensor_scalar(gam[:], gam[:], hup[:], None, ALU.mult))
        yield from vstep(dve.tensor_scalar(bet[:], bet[:], hup[:], None, ALU.mult))
        yield from vstep(dve.tensor_copy(hbound[:], tmp2[:, 2:3]))
        st.at[("hscale",)] = st.at[mine[0]]


    def expert_map(which, e):
        w = ((t["sw1"], t["sw2"]) if e == NE else (t["ew1"][e], t["ew2"][e]))[which]
        nat, q, nch, width = ((e1n, e1q, FC, D), (e2n, e2q, DC, FF))[which]
        lane = f"e{which}n"
        if e < NE:
            need("sp", ("eq", which, e + 1))
        moved(sp.dma_start(nat[:], w.rearrange("(c p) n -> p c n", p=P)), lane, lane, e)
        yield
        need("dve", (lane, e))
        sc = esc[:, which, 0:nch]
        yield from vstep(dve.tensor_reduce(sc, nat[:], AX.X, ALU.add, apply_absolute_value=True))
        yield from vstep(dve.tensor_scalar(sc, sc, 1.0 / width, 1e-5, ALU.mult, ALU.max))
        rs = esr[:, which, 0:nch]
        yield from vstep(dve.reciprocal(rs, sc))
        need("act", mine[0])
        for c in range(nch):
            last = act.activation(nat[:, c, :], nat[:, c, :], ACT.Identity, bias=rne[:, 0:1], scale=rs[:, c:c + 1])
        done("act", last, "eround", which, e)
        yield
        need("dve", ("eround", which, e))
        yield from vstep(dve.tensor_scalar(nat[:], nat[:], RNE + 1.0, RNE, ALU.min, ALU.subtract))
        if e < NE:
            need("dve", ("et", which, e + 1))
        yield from vstep(dve.tensor_scalar(q[:], nat[:], -1.0, None, ALU.max))
        st.at[("eq", which, e)] = st.at[mine[0]]
        need("pe", mine[0])
        bk, rd = yield from take()
        b16 = bk[:].bitcast(F16)
        for c in range(width // P):
            for f in range(nch):
                o = c * nch * P + f * P
                last = pe.transpose(b16[:, o:o + P], q[:, f, c * P:(c + 1) * P], ident16[:])
        done("pe", last, "et", which, e)
        yield
        need("act", ("et", which, e))
        dst = (E1T, E2T)[which][:, e, :, :]
        done("act", act.activation(dst, b16[:, 0:width // P * nch * P].rearrange("p (c m) -> p c m", m=nch * P), ACT.Copy), "ET", which, e)
        rd.append(("ET", which, e))
        if which == 0:
            yield from once("dve", ("hscale",))
            yield from vstep(dve.tensor_scalar(e1s[:, e, :], sc, hdn[:], None, ALU.mult))
            yield from vstep(dve.tensor_reduce(smax[:, e:e + 1], sc, AX.X, ALU.max))
        else:
            if e < NE:
                need("dve", ("dg", e + 1))
            for c in range(DC):
                last = dve.tensor_scalar(dg[:, c, :], ident[:], sc[:, c:c + 1], None, ALU.mult)
            yield from vstep(last)
            need("pe", mine[0])
            bk, rd = yield from take()
            for c in range(DC):
                last = pe.matmul(bk[:, c * P:(c + 1) * P], ones[:], dg[:, c, :], start=True, stop=True)
            done("pe", last, "dg", e)
            yield
            need("act", ("dg", e))
            done("act", act.activation(e2s[:, e, :], bk[:, 0:D], ACT.Copy), "e2s", e)
            rd.append(("e2s", e))

    def guards():
        yield from vstep(dve.tensor_reduce(smax[:, NE + 1:NE + 2], smax[:, 0:NE + 1], AX.X, ALU.max))
        need("pe", mine[0])
        bk, rd = yield from take()
        done("pe", pe.transpose(bk[0:1, 0:P], smax[:, NE + 1:NE + 2], ident[:]), "smaxT")
        yield
        need("dve", ("smaxT",))
        yield from vstep(dve.tensor_reduce(tmp2[0:1, 4:5], bk[0:1, 0:P], AX.X, ALU.max))
        rd.append(mine[0])
        yield from vstep(dve.tensor_scalar(tmp2[0:1, 4:5], tmp2[0:1, 4:5], hbound[0:1, :], float(D), ALU.mult, ALU.mult))
        need("pe", mine[0])
        bk, rd = yield from take()
        done("pe", pe.matmul(bk[:, 0:1], ones[0:1, :], tmp2[0:1, 4:5], start=True, stop=True), "sbound")
        yield
        need("dve", ("sbound",))
        yield from vstep(dve.tensor_copy(tmp2[:, 5:6], bk[:, 0:1]))
        rd.append(mine[0])
        yield from vstep(dve.tensor_scalar(sup[:].bitcast(I32), tmp2[:, 5:6].bitcast(I32), 0x7F800000, None, ALU.bitwise_and))
        yield from vstep(dve.tensor_scalar(sup[:], sup[:], 2.0 ** -13, None, ALU.mult))
        yield from vstep(dve.reciprocal(sdn[:], sup[:]))
        need("dve", ("e2s", 0))
        yield from vstep(dve.tensor_scalar(e2s[:], e2s[:], sup[:], None, ALU.mult))
        st.at[("guards",)] = st.at[mine[0]]

    def bn(x, which, b, j):
        done("dve", dve.bn_stats(bst[which][:, j, :], x), "bn", which, b, j)

    def aggregate(which, b, j):
        need("dve", ("bn", which, b, j))
        done("dve", dve.bn_aggr(mv[which][:, j, :], bst[which][:, j, :]), "mv", which, b, j)

    def root(which, b, n=NT):
        need("dve", ("mv", which, b, n - 1))
        r = rstd[which][:, 0:n]
        done("dve", dve.tensor_scalar(r, mv[which][:, 0:n, 1], LN_EPS, None, ALU.add), "veps", which, b)
        yield
        need("pool", ("veps", which, b))
        done("pool", pool.tensor_tensor(r, r, mhalf[:, 0:n], ALU.pow), "rstd", which, b)
        yield

    def normalise(out, x, which, b, j):
        need("dve", ("rstd", which, b), ("mv", which, b, j))
        return dve.tensor_scalar(out, x, mv[which][:, j, 0:1], rstd[which][:, j:j + 1], ALU.subtract, ALU.mult)

    def until(*key):
        while key not in st.at:
            yield

    def once(eng, *keys):
        for key in keys:
            yield from until(*key)
            need(eng, key)

    def a1_split(b):
        if b >= 1:
            yield from once("act", ("pv", b - 1, NT - 1))
        need("act", ("X", b))
        done("act", act.activation(Xh[:], X[b % 2][:], ACT.Copy), "Xh", b)
        yield
        need("pool", ("Xh", b))
        done("pool", pool.tensor_tensor(Xl[:], X[b % 2][:], Xh[:].bitcast(F32), ALU.subtract), "Xl", b)
        yield

    def a2_project(b):
        need("pe", ("XT", b))
        bk, rd = yield from take()
        for c in range(DC):
            last = pe.matmul(bk[:], wqk[:, c, :], XT[:, c, :], start=c == 0, stop=c == DC - 1)
        done("pe", last, "proj", b)
        yield
        need("act", ("proj", b))
        if b >= 1:
            yield from once("act", ("score", b - 1, NT - 1))
        act.activation(Qs[0:64, :], bk[0:64, :], ACT.Identity, bias=bqk[0:64, :])
        done("act", act.activation(KH[0:64, :], bk[64:128, :], ACT.Identity, bias=bqk[64:128, :]), "qkhi", b)
        yield
        need("dve", ("qkhi", b))
        dve.scalar_tensor_tensor(Qs[32:64, :], bk[32:64, :], bqk[32:64, :], Qs[32:64, :].bitcast(F32),
                                 ALU.add, ALU.subtract)
        done("dve", dve.scalar_tensor_tensor(KL[0:64, :], bk[64:128, :], bqk[64:128, :],
                                             KH[0:64, :].bitcast(F32), ALU.add, ALU.subtract), "qklo", b)
        rd.append(("qklo", b))
        yield

    def b1_scores(b):
        need("pe", ("qklo", b))
        held = []
        for i in range(NT):
            w = (i + 1) * P
            bk, rd = yield from take()
            held.append((bk, rd))
            q = Qs[:, i * P:(i + 1) * P]
            pe.matmul(bk[:, 0:w], q, KH[:, 0:w], start=True, stop=False)
            pe.matmul(bk[:, 0:w], q, KL[:, 0:w], start=False, stop=False)
            done("pe", pe.matmul(bk[:, i * P:w], identb[:], maskb[:], start=False, stop=True), "score", b, i)
            yield
            need("dve", ("score", b, i))
            done("dve", dve.tensor_reduce(NM[b % 2][:, i:i + 1], bk[:, 0:w], AX.X, ALU.max, negate=True), "max", b, i)
            yield
        if b >= 1:
            need("act", ("pT", b - 1, NT - 1))
        for i, (bk, rd) in enumerate(held):
            need("act", ("max", b, i))
            done("act", act.activation(PB[:, OFF[i]:OFF[i + 1]], bk[:, 0:(i + 1) * P], ACT.Exp, bias=NM[b % 2][:, i:i + 1],
                                       accum_out=RS[b % 2][:, i:i + 1]), "exp", b, i)
            rd.append(("exp", b, i))
        yield

    def b2_transpose(b):
        for i in range(NT):
            need("pe", ("exp", b, i))
            bk, rd = yield from take()
            for k in range(i + 1):
                last = pe.transpose(bk[:, k * P:(k + 1) * P], PB[:, OFF[i] + k * P:OFF[i] + (k + 1) * P], ident[:])
            done("pe", last, "pT", b, i)
            yield
            need("act", ("pT", b, i))
            if b >= 1 and i == 0:
                yield from once("act", ("pv", b - 1, NT - 1))
            o = slice(OFF[i], OFF[i + 1])
            done("act", act.activation(PTh[:, o], bk[:, 0:(i + 1) * P], ACT.Copy), "pTh", b, i)
            yield
            need("dve", ("pTh", b, i))
            done("dve", dve.tensor_tensor(PTl[:, o], bk[:, 0:(i + 1) * P], PTh[:, o].bitcast(F32), ALU.subtract), "pTl", b, i)
            rd.append(("pTl", b, i))
            yield

    def b3_values(b):
        need("dve", ("exp", b, NT - 1))
        done("dve", dve.reciprocal(RI[b % 2][:], RS[b % 2][:]), "rinv", b)
        need("pe", ("Xl", b))
        for i in range(NT):
            need("pe", ("pTl", b, i))
            bk, rd = yield from take()
            for k in range(i + 1):
                o = slice(OFF[i] + k * P, OFF[i] + (k + 1) * P)
                pe.matmul(bk[:, 0:D], PTh[:, o], Xh[:, k, :], start=k == 0, stop=False)
                pe.matmul(bk[:, 0:D], PTh[:, o], Xl[:, k, :], start=False, stop=False)
                last = pe.matmul(bk[:, 0:D], PTl[:, o], Xh[:, k, :], start=False, stop=k == i)
            done("pe", last, "pv", b, i)
            yield
            need("dve", ("pv", b, i), ("rinv", b))
            if b >= 1 and i == 0:
                yield from once("dve", ("x1T", b - 1), ("x2", b - 1, NT - 1))
            done("dve", dve.scalar_tensor_tensor(X1[:, i, :], bk[:, 0:D], RI[b % 2][:, i:i + 1], X[b % 2][:, i, :],
                                                 ALU.mult, ALU.add), "x1", b, i)
            rd.append(("x1", b, i))
            yield
            need("dve", ("x1", b, i))
            bn(X1[:, i, :], 0, b, i)
            yield
            aggregate(0, b, i)
        yield
        yield from root(0, b)
        for i in range(NT):
            done("dve", normalise(X1[:, i, :], X1[:, i, :], 0, b, i), "x1n", b, i)
            yield

    def transposed(b, src, hi, lo, name, ready, reread, sums=None):
        for c in range(DC):
            bk, rd = yield from take()
            for j in range(NT):
                if c == 0:
                    need("pe", (ready, b, j))
                last = pe.transpose(bk[:, j * P:(j + 1) * P], src[:, j, c * P:(c + 1) * P], ident[:])
            done("pe", last, name, b, c)
            yield
            need("act", (name, b, c))
            if reread is not None:
                yield from once("act", reread)
            extra = dict(accum_out=sums[:, c:c + 1]) if sums is not None else {}
            done("act", act.activation(hi[:, c, :], bk[:], ACT.Copy, **extra), name + "h", b, c)
            yield
            need("dve", (name + "h", b, c))
            h = hi[:, c, :].bitcast(F32) if hi.dtype == F32R else hi[:, c, :]
            done("dve", dve.tensor_tensor(lo[:, c, :], bk[:], h, ALU.subtract), name + "l", b, c)
            rd.append((name + "l", b, c))
            yield
        st.at[(name, b)] = st.at[(name, b, DC - 1)]

    def c1_transpose(b):
        yield from transposed(b, X1, T1h, T1l, "x1T", "x1n", ("ffn", b - 1) if b >= 1 else None)

    def c2_linear(b):
        x2 = X2[b % NX2]
        if b == 0:
            need("pe", ("W0T",))
        for j in range(NT):
            need("pe", ("x1Tl", b, DC - 1))
            bk, rd = yield from take()
            for c in range(DC):
                pe.matmul(bk[:, 0:D], T1h[:, c, j * P:(j + 1) * P], W0T[:, c, :], start=c == 0, stop=False)
                last = pe.matmul(bk[:, 0:D], T1l[:, c, j * P:(j + 1) * P], W0T[:, c, :], start=False, stop=c == DC - 1)
            done("pe", last, "ffn", b, j)
            yield
            need("dve", ("ffn", b, j))
            if b >= NX2 and j == 0:
                yield from once("dve", ("r", b - NX2))
            done("dve", dve.scalar_tensor_tensor(x2[:, j, :], bk[:, 0:D], sc0[:], X1[:, j, :], ALU.mult, ALU.add),
                 "x2", b, j)
            rd.append(("x2", b, j))
            yield
            need("dve", ("x2", b, j))
            bn(x2[:, j, :], 1, b, j)
            yield
            aggregate(1, b, j)
        st.at[("ffn", b)] = st.at[("ffn", b, NT - 1)]
        yield
        yield from root(1, b)
        for j in range(NT):
            done("dve", normalise(x2[:, j, :], x2[:, j, :], 1, b, j), "x2n", b, j)
            yield

    def d1_transpose(b):
        if b >= 2:
            need("act", ("gate1", b - 2))
        yield from transposed(b, X2[b % NX2], TTh, TTl, "x2T", "x2n", ("u", b - 1) if b >= 1 else None, sums=SUMS[b % 2])
        need("pool", ("x2T", b))
        done("pool", pool.tensor_tensor(X2[b % NX2][:], X2[b % NX2][:], pb_row[:, None, :].to_broadcast([P, NT, D]), ALU.add),
             "x2b", b)
        yield

    last_of = {}

    def d2_stats(b):
        g, col = b // GB, (b % GB) * NT
        need("pe", ("x2Tl", b, DC - 1), ("x2Th", b, DC - 1))
        bk, rd = yield from take()
        for c in range(DC):
            last = pe.matmul(bk[0:RED, 0:1], cw1[:, c, :], SUMS[b % 2][:, c:c + 1], start=c == 0, stop=c == DC - 1)
        done("pe", last, "gate1", b)
        yield
        need("act", ("gate1", b))
        if b >= 1:
            need("act", ("gate2", b - 1))
        done("act", act.activation(R1[:], bk[0:RED, 0:1], ACT.Relu, bias=cb1[:], scale=1.0 / SEQ), "gate_r", b)
        rd.append(("gate_r", b))

        def tile(j):
            bk, rd = yield from take()
            for c in range(DC):
                o = slice(j * P, (j + 1) * P)
                pe.matmul(bk[:], TTh[:, c, o], WCh[:, c, :], start=c == 0, stop=False)
                pe.matmul(bk[:], TTh[:, c, o], WCl[:, c, :], start=False, stop=False)
                last = pe.matmul(bk[:], TTl[:, c, o], WCh[:, c, :], start=False, stop=c == DC - 1)
            done("pe", last, "dqk", b, j)
            yield
            need("act", ("dqk", b, j))
            if "qk" in last_of:
                need("act", last_of["qk"])
            act.activation(DK[:], bk[:, D:2 * D], ACT.Copy)
            if g >= 2 and b % GB == 0 and j == 0:
                need("act", ("ode", g - 2))
            need("act", last_of.get("sq", ("zero", 2)))
            done("act", act.activation(junk_a[:], bk[:], ACT.Square, accum_out=S2[g % 2][:, col + j:col + j + 1]), "sq", b, j)
            last_of["sq"] = ("sq", b, j)
            yield
            need("dve", ("sq", b, j))
            done("dve", dve.tensor_tensor_reduce(out=bk[:, 0:D], in0=bk[:, 0:D], in1=DK[:], scale=1.0, scalar=0.0,
                                                 op0=ALU.mult, op1=ALU.add,
                                                 accum_out=SQK[g % 2][:, col + j:col + j + 1]), "sqk", b, j)
            last_of["qk"] = ("sqk", b, j)
            rd.append(("sqk", b, j))

        yield from tile(0)
        need("pe", ("gate_r", b))
        bk, rd = yield from take()
        for c in range(DC):
            last = pe.matmul(bk[:, c:c + 1], cw2[:, c * P:(c + 1) * P], R1[:], start=True, stop=True)
        done("pe", last, "gate2", b)
        yield
        need("dve", ("gate2", b))
        if b >= 1:
            need("dve", ("ps", b - 1))
        yield from vstep(dve.tensor_tensor(CHW[:], bk[:, 0:DC], cb2[:], ALU.add))
        rd.append(mine[0])
        yield from vstep(dve.tensor_scalar(CHW[:], CHW[:], -80.0, None, ALU.max))
        need("act", mine[0])
        done("act", act.activation(CHW[:], CHW[:], ACT.Exp, scale=-1.0), "gexp", b)
        yield from tile(1)
        need("dve", ("gexp", b))
        yield from vstep(dve.tensor_scalar(CHW[:], CHW[:], 1.0, None, ALU.add))
        yield from vstep(dve.reciprocal(CHW[:], CHW[:]))
        need("act", mine[0])
        if b >= 1:
            need("act", ("fuse", b - 1))
        for c in range(DC):
            last = act.activation(PS[:, c, :], pw[:, c, :], ACT.Copy, scale=CHW[:, c:c + 1])
        done("act", last, "ps", b)
        yield from tile(2)
        yield from tile(3)
        need("pe", ("ps", b))
        bk, rd = yield from take()
        for m in range(DC):
            for c in range(DC):
                last = pe.matmul(bk[:, m * D:(m + 1) * D], wvT[:, c, m * P:(m + 1) * P], PS[:, c, :], start=c == 0,
                                 stop=c == DC - 1)
        done("pe", last, "fuse", b)
        yield
        need("act", ("fuse", b))
        if b >= 1:
            need("act", ("u", b - 1))
        fused = bk[:].rearrange("p (m n) -> p m n", m=DC)
        done("act", act.activation(Mh[:, :, 0:D], fused, ACT.Copy), "Mh", b)
        yield
        need("dve", ("Mh", b))
        done("dve", dve.tensor_tensor(Ml[:, :, 0:D], fused, Mh[:, :, 0:D].bitcast(F32), ALU.subtract), "Ml", b)
        rd.append(("Ml", b))
        yield

    def d3_values(b):
        need("pe", ("Ml", b))
        if b >= NU:
            yield from until("x3", b - NU, NT - 1)
        for j in range(NT):
            bk, rd = yield from take()
            for c in range(DC):
                o = slice(j * P, (j + 1) * P)
                pe.matmul(bk[:, 0:D + 2], TTh[:, c, o], Mh[:, c, :], start=c == 0, stop=False)
                pe.matmul(bk[:, 0:D + 2], TTh[:, c, o], Ml[:, c, :], start=False, stop=False)
                last = pe.matmul(bk[:, 0:D + 2], TTl[:, c, o], Mh[:, c, :], start=False, stop=c == DC - 1)
            done("pe", last, "u", b, j)
            yield
            need("act", ("u", b, j))
            if b >= NU:
                need("act", ("x3", b - NU, NT - 1))
            done("act", act.activation(U[b % NU][:, j, :], bk[:, 0:D + 2], ACT.Copy), "U", b, j)
            rd.append(("U", b, j))
        st.at[("u", b)] = st.at[("u", b, NT - 1)]
        yield

    o_mm = sb("o_mm", [P, GC])
    o_d1 = sb("o_d1", [P, GC])
    o_kk = sb("o_kk", [P, GC])
    o_n2 = sb("o_n2", [P, GC])
    o_A = sb("o_A", [P, GB, NT])
    o_h = sb("o_h", [P, 2, GB, 2, NT])
    o_sq = sb("o_sq", [P, 2, GB, 2, NT])
    o_mean = sb("o_mean", [P, 2 * GB])
    o_rs = sb("o_rs", [P, 2 * GB])
    o_t = sb("o_t", [P, TAPS, GB, NT])
    o_e = sb("o_e", [P, GB, NT])
    o_s = sb("o_s", [P, GB])

    def neighbours(out, prev, nxt, extra=None):
        o1, o2 = out
        pe.matmul(o1, from_prev[:], prev, start=True, stop=False)
        pe.matmul(o1[:, :, 1:NT], edge_prev[:], prev[:, :, 0:NT - 1], start=False, stop=extra is None)
        if extra is not None:
            pe.matmul(o1, ident[:], extra, start=False, stop=False)
        pe.matmul(o2, from_next[:], nxt, start=extra is None, stop=False)
        return pe.matmul(o2[:, :, 0:NT - 1], edge_next[:], nxt[:, :, 1:NT], start=False, stop=True)

    def ode(g):
        last_b = GB * g + GB - 1
        need("dve", *[("U", b, NT - 1) for b in range(GB * g, last_b + 1)], ("sqk", last_b, NT - 1), ("sq", last_b, NT - 1))
        for i in range(GB):
            b = GB * g + i
            mq, mk = U[b % NU][:, :, D], U[b % NU][:, :, D + 1]
            c = slice(i * NT, (i + 1) * NT)
            dve.tensor_tensor(o_mm[:, c], mq, mk, ALU.mult)
            dve.tensor_tensor(o_d1[:, c], mq, mq, ALU.mult)
            last = dve.tensor_tensor(o_kk[:, c], mk, mk, ALU.mult)
        yield from vstep(last)
        c1, c2 = cc[:, 0:1], cc[:, 1:2]
        s2, sqk = S2[g % 2][:], SQK[g % 2][:]
        dve.tensor_scalar(o_mm[:], o_mm[:], 2.0, c1, ALU.mult, ALU.add)
        dve.scalar_tensor_tensor(o_d1[:], o_d1[:], c1, o_kk[:], ALU.add, ALU.add)
        dve.tensor_scalar(o_n2[:], sqk, 2.0 / (D - 1), c2, ALU.mult, ALU.add)
        yield from vstep(dve.tensor_scalar(s2, s2, 1.0 / (D - 1), c2, ALU.mult, ALU.add))
        dve.tensor_tensor(o_mm[:], o_mm[:], o_n2[:], ALU.mult)
        yield from vstep(dve.tensor_tensor(o_d1[:], o_d1[:], s2, ALU.mult))
        yield from vstep(dve.tensor_scalar(o_d1[:], o_d1[:], 1e-7, None, ALU.add))
        yield from vstep(dve.reciprocal(o_d1[:], o_d1[:]))
        yield from vstep(dve.tensor_tensor(o_mm[:], o_mm[:], o_d1[:], ALU.mult))
        A = o_A[:].rearrange("p b j -> p (b j)")
        yield from vstep(dve.tensor_tensor(A, o_mm[:], o_mm[:], ALU.mult))
        st.at[("ode", g)] = st.at[mine[0]]
        need("pe", mine[0])
        bk, rd = yield from take()
        left = bk[:, 0:GC].rearrange("p (b j) -> p b j", b=GB)
        right = bk[:, GC:2 * GC].rearrange("p (b j) -> p b j", b=GB)
        done("pe", neighbours((left, right), o_A[:], o_A[:]), "nb", g)
        yield
        need("dve", ("nb", g))
        h = [o_h[:, ch // 2, :, ch % 2, :] for ch in range(CH)]
        for tap, src in enumerate((left, o_A[:], right)):
            for ch in range(CH):
                w = c1w[:, ch * TAPS + tap:ch * TAPS + tap + 1]
                if tap == 0:
                    last = dve.tensor_scalar(h[ch], src, w, None, ALU.mult)
                else:
                    last = dve.scalar_tensor_tensor(h[ch], src, w, h[ch], ALU.mult, ALU.add)
            yield from vstep(last)
        rd.append(mine[0])
        hf = o_h[:].rearrange("p g b c j -> p (g b) (c j)")
        sqf = o_sq[:].rearrange("p g b c j -> p (g b) (c j)")
        flat = o_h[:].rearrange("p g b c j -> p (g b c j)")

        def over_tokens(src, key):
            need("pe", mine[0])
            bk, rd = yield from take()
            done("pe", pe.matmul(bk[:, 0:src.shape[-1]], ones[:], src, start=True, stop=True), key, g)
            yield
            need("dve", (key, g))
            return bk, rd

        bk, rd = yield from over_tokens(flat, "gn1")
        yield from vstep(dve.tensor_reduce(o_mean[:], bk[:, 0:2 * GB * 2 * NT].rearrange("p (k m) -> p k m", k=2 * GB), AX.X, ALU.add))
        rd.append(mine[0])
        yield from vstep(dve.tensor_scalar(o_mean[:], o_mean[:], 1.0 / (2 * SEQ), None, ALU.mult))
        yield from vstep(dve.tensor_tensor(hf, hf, o_mean[:, :, None].to_broadcast([P, 2 * GB, 2 * NT]), ALU.subtract))
        yield from vstep(dve.tensor_tensor(sqf, hf, hf, ALU.mult))
        bk, rd = yield from over_tokens(o_sq[:].rearrange("p g b c j -> p (g b c j)"), "gn2")
        yield from vstep(dve.tensor_reduce(o_rs[:], bk[:, 0:2 * GB * 2 * NT].rearrange("p (k m) -> p k m", k=2 * GB), AX.X, ALU.add))
        rd.append(mine[0])
        yield from vstep(dve.tensor_scalar(o_rs[:], o_rs[:], 1.0 / (2 * SEQ), 1e-5, ALU.mult, ALU.add))
        need("pool", mine[0])
        done("pool", pool.tensor_tensor(o_rs[:], o_rs[:], mhalf[:, 0:2 * GB], ALU.pow), "gnr", g)
        yield
        need("dve", ("gnr", g))
        yield from vstep(dve.tensor_tensor(hf, hf, o_rs[:, :, None].to_broadcast([P, 2 * GB, 2 * NT]), ALU.mult))
        for ch in range(CH):
            last = dve.tensor_scalar(h[ch], h[ch], gng[:, ch:ch + 1], gnb[:, ch:ch + 1], ALU.mult, ALU.add)
        yield from vstep(last)
        yield from vstep(dve.tensor_scalar(flat, flat, 0.0, None, ALU.max))
        for ch in range(CH):
            for tap in range(TAPS):
                w = c2w[:, ch * TAPS + tap:ch * TAPS + tap + 1]
                if ch == 0:
                    last = dve.tensor_scalar(o_t[:, tap], h[ch], w, None, ALU.mult)
                else:
                    last = dve.scalar_tensor_tensor(o_t[:, tap], h[ch], w, o_t[:, tap], ALU.mult, ALU.add)
            yield from vstep(last)
        need("pe", mine[0])
        bk, rd = yield from take()
        y = bk[:, 0:GC].rearrange("p (b j) -> p b j", b=GB)
        done("pe", neighbours((y, y), o_t[:, 0], o_t[:, 2], extra=o_t[:, 1]), "nb2", g)
        yield
        need("dve", ("nb2", g))
        yield from vstep(dve.scalar_tensor_tensor(o_e[:], y, c2b[:], o_A[:], ALU.add, ALU.add))
        rd.append(mine[0])
        yield from vstep(dve.tensor_scalar(o_e[:], o_e[:], -80.0, None, ALU.max))
        need("act", mine[0])
        done("act", act.activation(o_e[:], o_e[:], ACT.Exp, scale=-1.0), "oexp", g)
        yield
        need("dve", ("oexp", g))
        yield from vstep(dve.tensor_scalar(o_e[:], o_e[:], 1.0, None, ALU.add))
        yield from vstep(dve.reciprocal(o_e[:], o_e[:]))
        need("act", mine[0])
        done("act", act.activation(o_e[:], o_e[:], ACT.Exp), "oexp2", g)
        yield
        need("dve", ("oexp2", g))
        yield from vstep(dve.tensor_reduce(o_s[:], o_e[:], AX.X, ALU.add))
        bk, rd = yield from over_tokens(o_s[:], "osum")
        yield from vstep(dve.reciprocal(o_s[:], bk[:, 0:GB]))
        rd.append(mine[0])
        yield from vstep(dve.tensor_tensor(WT[g % 2][:], o_e[:], o_s[:, :, None].to_broadcast([P, GB, NT]), ALU.mult))
        st.at[("weights", g)] = st.at[mine[0]]

    recv = rec[0:TOK, :].rearrange("(b j p) c -> b p j c", j=NT, p=P)

    def f1_norms(b):
        g = b // GB
        x3 = X2[b % NX2]
        need("dve", ("weights", g), ("x2b", b), ("U", b, NT - 1))
        for j in range(NT):
            done("dve", dve.scalar_tensor_tensor(x3[:, j, :], U[b % NU][:, j, 0:D], WT[g % 2][:, b % GB, j:j + 1],
                                                 x3[:, j, :], ALU.mult, ALU.add), "x3", b, j)
            yield
            need("dve", ("x3", b, j))
            bn(x3[:, j, :], 2, b, j)
            yield
            aggregate(2, b, j)
        yield
        yield from root(2, b)
        for j in range(NT):
            done("dve", normalise(x3[:, j, :], x3[:, j, :], 2, b, j), "x3n", b, j)
            if j == 0:
                if b >= 1:
                    yield from once("dve", ("hn", b - 1, NT - 1))
                yield from vstep(dve.tensor_tensor(rstd[3][:], mv[2][:, :, 1], rstd[2][:], ALU.mult))
                yield from vstep(dve.tensor_tensor(rstd[3][:], rstd[3][:], rstd[2][:], ALU.mult))
                yield from vstep(dve.tensor_scalar(rstd[3][:], rstd[3][:], LN_EPS, None, ALU.add))
                need("pool", mine[0])
                done("pool", pool.tensor_tensor(rstd[3][:], rstd[3][:], mhalf[:, 0:NT], ALU.pow), "rstd", 3, b)
            yield

    def f1_h(b):
        x3 = X2[b % NX2]
        need("act", ("rstd", 3, b))
        if b >= 1:
            yield from once("act", ("h16", b - 1))
        for j in range(NT):
            need("act", ("x3n", b, j))
            done("act", act.activation(HN[:, j, :], x3[:, j, :], ACT.Copy, scale=rstd[3][:, j:j + 1]), "hn", b, j)
            yield
        need("pool", ("hn", b, NT - 1))
        done("pool", pool.tensor_tensor(HN[:], HN[:], gam[:, None, :].to_broadcast([P, NT, D]), ALU.mult), "hg", b)
        yield
        need("pool", ("hg", b))
        done("pool", pool.tensor_tensor(HN[:], HN[:], bet[:, None, :].to_broadcast([P, NT, D]), ALU.add), "h", b)
        yield

    def ht_of(b):
        return HT[b - (B - HELD) + 1] if B - HELD <= b < B - 1 else HT[0]

    def f2_router(b):
        h16 = H16
        need("act", ("h", b))
        if b >= 1:
            need("act", ("hrec", b - 1), ("hT", b - 1))
        done("act", act.activation(h16[:, :, 0, :], HN[:], ACT.Copy), "hhi", b)
        yield
        need("pool", ("hhi", b))
        done("pool", pool.tensor_tensor(h16[:, :, 1, :], HN[:], h16[:, :, 0, :], ALU.subtract), "h16", b)
        yield
        need("sp", ("h16", b))
        moved(sp.dma_start(recv[b][:, :, 0:D], h16[:].rearrange("p j s d -> p j (s d)").bitcast(F32)),
              "hrec", "hrec", b)
        ht = ht_of(b)
        need("pe", ("h16", b))
        for s in range(2):
            bk, rd = yield from take()
            b16 = bk[:].bitcast(F16)
            for c in range(DC):
                for j in range(NT):
                    o = c * SEQ + j * P
                    last = pe.transpose(b16[:, o:o + P], h16[:, j, s, c * P:(c + 1) * P], ident16[:])
            done("pe", last, "hT", b, s)
            yield
            if b > 0:
                yield from once("act", ("up", min(b, B - HELD) - 1, FC - 1))
            if b == B - HELD and s == 0:
                yield from once("act", ("u", B - 1), ("Ml", B - 1), ("Xl", B - 1))
            need("act", ("hT", b, s))
            done("act", act.activation(ht[:, s].rearrange("p c n -> p (c n)"), b16, ACT.Copy), "HT", b, s)
            rd.append(("HT", b, s))
        st.at[("hT", b)] = st.at[("hT", b, 1)]
        yield
        need("pe", ("HT", b, 1))
        bk, rd = yield from take()
        W3 = 3 * NE
        for j in range(NT):
            for k, (s, c) in enumerate([(s, c) for s in range(2) for c in range(DC)]):
                last = pe.matmul(bk[:, j * W3:(j + 1) * W3], ht[:, s, c, j * P:(j + 1) * P],
                                 RW3[:, c].rearrange("p k e -> p (k e)"), start=k == 0, stop=k == 3)
        done("pe", last, "logits", b)
        yield
        need("dve", ("logits", b))
        lg = r_lg
        yield from vstep(dve.tensor_reduce(lg[:], bk[:, 0:NT * W3].rearrange("p (j k e) -> p j e k", j=NT, k=3), AX.X, ALU.add))
        rd.append(mine[0])
        T = slice(b * NT, (b + 1) * NT)

        def wide(x):
            return x[:, :, None].to_broadcast([P, NT, NE])

        yield from vstep(dve.tensor_reduce(r_mx[:], lg[:], AX.X, ALU.max))
        dve.tensor_tensor(r_eq[:], lg[:], wide(r_mx), ALU.is_equal)
        yield from vstep(dve.tensor_tensor(lg[:], lg[:], wide(r_mx), ALU.subtract))
        need("act", mine[0])
        done("act", act.activation(lg[:], lg[:], ACT.Exp, scale=hdn[:]), "rexp", b)
        yield from vstep(dve.tensor_tensor(r_eq[:], r_eq[:], desc8[:, None, :].to_broadcast([P, NT, NE]), ALU.mult))
        yield from vstep(dve.tensor_reduce(r_mx[:], r_eq[:], AX.X, ALU.max))
        yield from vstep(dve.tensor_tensor(OH[:, T, :], r_eq[:], wide(r_mx), ALU.is_equal))
        need("dve", ("rexp", b))
        yield from vstep(dve.tensor_reduce(r_mx[:], lg[:], AX.X, ALU.add))
        yield from vstep(dve.reciprocal(GATE[:, T], r_mx[:]))
        st.at[("gate", b)] = st.at[mine[0]]

    r_lg = sb("r_lg", [P, NT, NE])
    r_mx = sb("r_mx", [P, NT])
    r_eq = sb("r_eq", [P, NT, NE])

    def g1_shared(b):
        ht = ht_of(b)
        for f0 in range(0, FC, 2):
            held = []
            for f in (f0, f0 + 1):
                bk, rd = yield from take()
                held.append((bk, rd))
                for k, (s, c) in enumerate([(s, c) for s in range(2) for c in range(DC)]):
                    last = pe.matmul(bk[:], E1T[:, NE, c, f * P:(f + 1) * P], ht[:, s, c, :], start=k == 0, stop=k == 3)
                done("pe", last, "up", b, f)
                yield
            for f, (bk, rd) in zip((f0, f0 + 1), held):
                n = b * FC + f
                need("act", ("up", b, f))
                if n >= 2:
                    need("act", ("Sl", n - 2))
                done("act", act.activation(S[n % 2][:], bk[:], ACT.Silu, scale=e1s[:, NE, f:f + 1]), "silu", n)
                rd.append(("silu", n))
            yield
            for f in (f0, f0 + 1):
                n = b * FC + f
                s = S[n % 2]
                need("act", ("silu", n))
                if f == 0 and b >= 1:
                    yield from once("act", ("down", b - 1, NT - 1))
                done("act", act.activation(Sh[:, f, :], s[:], ACT.Copy, scale=sdn[:]), "Sh", n)
                yield
                need("dve", ("Sh", n))
                done("dve", dve.scalar_tensor_tensor(Sl[:, f, :], s[:], sdn[:], Sh[:, f, :], ALU.mult, ALU.subtract), "Sl", n)
                yield

    def g2_shared(b):
        need("pe", ("Sl", b * FC + FC - 1))
        r = R
        for j in range(NT):
            bk, rd = yield from take()
            for k, (f, s) in enumerate([(f, s) for f in range(FC) for s in (Sh, Sl)]):
                last = pe.matmul(bk[:, 0:D], s[:, f, j * P:(j + 1) * P], E2T[:, NE, f, :], start=k == 0, stop=k == 2 * FC - 1)
            done("pe", last, "down", b, j)
            yield
            need("dve", ("down", b, j))
            if b >= 1 and j == 0:
                need("dve", ("rrec", b - 1))
            done("dve", dve.tensor_tensor(r[:, j, 0:D], bk[:, 0:D], e2s[:, NE, :], ALU.mult), "y", b, j)
            rd.append(("y", b, j))
            yield
        need("dve", ("gate", b))
        done("dve", dve.tensor_copy(r[:, :, D:D + 2], GATE[:, b * NT:(b + 1) * NT, None].to_broadcast([P, NT, 2])), "rg", b)
        yield
        need("pool", ("y", b, NT - 1), ("x3n", b, NT - 1))
        done("pool", pool.tensor_tensor(r[:, :, 0:D], r[:, :, 0:D], X2[b % NX2][:], ALU.add), "r", b)
        yield
        need("sp", ("r", b), ("rg", b))
        moved(sp.dma_start(recv[b][:, :, D:REC], r[:]), "rrec", "rrec", b)

    sort_bank = []

    def sort_places():
        need("pe", ("gate", B - 1))
        ohv = OH[:].rearrange("p t e -> p e t")
        bk1, rd1 = yield from take()
        bk2, rd2 = yield from take()
        pe.matmul(bk1[:], before[:], ohv, start=True, stop=True)
        done("pe", pe.matmul(bk2[:], onesb[:], ohv, start=True, stop=True), "counts")
        yield
        need("dve", ("counts",))
        dve.memset(q_z[:], 0.0)
        dve.tensor_copy(part_f[:], part_i[:])
        dve.tensor_copy(q_C[:], bk1[:].rearrange("p (e t) -> p e t", e=NE))
        yield from vstep(dve.tensor_copy(q_tot[:], bk2[:].rearrange("p (e t) -> p e t", e=NE)))
        rd1.append(mine[0])
        rd2.append(mine[0])
        dve.tensor_tensor(q_C[:], q_C[:], q_tot[:], ALU.subtract)
        yield from vstep(dve.tensor_reduce(q_n[:], q_tot[:], AX.X, ALU.add))
        yield from vstep(dve.tensor_scalar(q_ni[:], q_n[:], float(SLOT - 1), None, ALU.add))
        yield from vstep(dve.tensor_scalar(q_ni[:], q_ni[:], SLOT.bit_length() - 1, SLOT.bit_length() - 1,
                                ALU.logical_shift_right, ALU.logical_shift_left))
        yield from vstep(dve.tensor_copy(q_n[:], q_ni[:]))
        yield from vstep(dve.tensor_tensor_scan(q_end[:], q_n[:], q_z[:, 0:NE], 0.0, ALU.add, ALU.add))
        yield from vstep(dve.tensor_tensor(q_n[:], q_end[:], q_n[:], ALU.subtract))
        for e in range(NE):
            last = dve.tensor_tensor_scan(q_tot[:, e, :], q_tot[:, e, :], q_z[:], q_n[:, e:e + 1], ALU.add, ALU.add)
        yield from vstep(last)
        yield from vstep(dve.tensor_tensor(q_C[:], q_C[:], q_tot[:], ALU.add))
        yield from vstep(dve.tensor_tensor(q_C[:], q_C[:], ohv, ALU.mult))
        yield from vstep(dve.tensor_reduce(q_pos[:], q_C[:].rearrange("p e t -> p t e"), AX.X, ALU.add))
        yield from vstep(dve.tensor_copy(q_i[:], q_pos[:]))
        yield from vstep(dve.tensor_scalar(q_i[:], q_i[:], 7, None, ALU.logical_shift_right))
        yield from vstep(dve.tensor_copy(q_hi[:], q_i[:]))
        yield from vstep(dve.scalar_tensor_tensor(q_lo[:], q_hi[:], -float(P), q_pos[:], ALU.mult, ALU.add))
        yield from vstep(dve.tensor_tensor(q_ge[:], q_end[:, :, None].to_broadcast([P, NE, NG]), group_first[:, None, :].to_broadcast([P, NE, NG]), ALU.is_le))
        yield from vstep(dve.tensor_reduce(q_ex[:], q_ge[:].rearrange("p e g -> p g e"), AX.X, ALU.add))
        yield from vstep(dve.tensor_scalar(q_exi[:], q_ex[:], float(NE - 1), None, ALU.min))
        st.at[("experts",)] = st.at[mine[0]]

    def sort_invert(k):
        if k == 0:
            sort_bank.extend((yield from take()))
        bk, _ = sort_bank
        a, bb = q_A[k % 2], q_B[k % 2]
        T = slice(k * CHK, (k + 1) * CHK)
        if k >= 2:
            need("dve", ("inv", k - 2))
        dve.tensor_tensor(a[:], q_lo[:, T, None].to_broadcast([P, CHK, P]), iota_f[:, None, :].to_broadcast([P, CHK, P]), ALU.is_equal)
        hot = HN[:, k % 2, :].bitcast(BF16)[:, 0:CHK * NST].rearrange("p (i h) -> p i h", i=CHK)
        yield from vstep(dve.tensor_tensor(hot, q_hi[:, T, None].to_broadcast([P, CHK, NST]),
                                           iota_f[:, None, 0:NST].to_broadcast([P, CHK, NST]), ALU.is_equal))
        need("pe", mine[0])
        need("act", mine[0])
        if k >= 2:
            need("act", ("inv", k - 2))
        for i in range(CHK):
            act.activation(bb[:, i, 0, :], hot[:, i, :], ACT.Copy, scale=float(k * CHK + i - NTILE))
        done("act", act.activation(bb[:, :, 1, :], hot, ACT.Copy, scale=part_f[:]), "hot", k)
        yield
        need("pe", ("hot", k))
        for i in range(CHK):
            tt = k * CHK + i
            last = pe.matmul(bk[:, 0:2 * NST], a[:, i, :], bb[:, i].rearrange("p s h -> p (s h)"),
                             start=tt == 0, stop=tt == NTILE - 1)
        done("pe", last, "inv", k)
        yield

    def sort_ids():
        bk, rd = sort_bank
        need("dve", ("inv", NTILE // CHK - 1))
        yield from vstep(dve.tensor_scalar(ids_f[:], bk[:, 0:NST], float(P), float(TOK), ALU.mult, ALU.add))
        yield from vstep(dve.tensor_tensor(ids_f[:], ids_f[:], bk[:, NST:2 * NST], ALU.add))
        rd.append(mine[0])
        yield from vstep(dve.tensor_copy(ids[:], ids_f[:]))
        st.at[("ids",)] = st.at[mine[0]]

    pool_chain(pool.iota(group_first[:].bitcast(I32), pattern=[[SLOT, NG]], base=0, channel_multiplier=0))
    done("pool", pool.tensor_copy(group_first[:], group_first[:].bitcast(I32)), "gfirst")
    need("dve", ("gfirst",))

    expert_of = {}

    def gather(s):
        if s == 0:
            need("pool", ("ids",), ("hrec", B - 1), ("rrec", B - 1), ("zero", 2), *front_free)
        for j in range(NGT):
            tt = s * NGT + j
            if s >= NGR:
                need("pool", ("gx", s - NGR, j), ("gTr", s - NGR))
            moved(pool.indirect_dma_start(G_rec[s % NGR][:, j, :], None, rec[:],
                                          bass.IndirectOffsetOnAxis(ids[:, tt:tt + 1], 0)), f"gat{s % NGR}", "gat", s, j)
            yield

    def routed_transpose(s):
        g = G_rec[s % NGR]
        need("pe", ("gat", s, NGT - 1))
        bk, rd = yield from take()
        b16 = bk[:].bitcast(F16)
        for j in range(NGT):
            h16 = g[:, j, 0:D].bitcast(F16)
            for s2 in range(2):
                for c in range(DC):
                    o = (s2 * DC + c) * SLOT + j * P
                    last = pe.transpose(b16[:, o:o + P], h16[:, s2 * D + c * P:s2 * D + (c + 1) * P], ident16[:])
        done("pe", last, "gTr", s)
        yield
        need("act", ("gTr", s))
        if s >= NGB:
            yield from once("act", ("gup", s - NGB, FC - 1))
        done("act", act.activation(G_T[s % NGB][:].rearrange("p s c n -> p (s c n)"), b16, ACT.Copy), "gT", s)
        rd.append(("gT", s))
        yield

    def routed_up(s):
        for eng in ("pe", "act"):
            need(eng, ("experts",))
            expert_of[eng, s] = st.engines[eng].value_load(q_exi[0:1, s:s + 1], min_val=0, max_val=NE - 1)
        ep, ea = expert_of["pe", s], expert_of["act", s]
        need("act", ("ids",))
        need("pe", ("gT", s))
        gt = G_T[s % NGB]
        for f in range(0, FC, 2):
            bk, rd = yield from take()
            for ff in (f, f + 1):
                o = (ff - f) * SLOT
                for k, (s2, c) in enumerate([(s2, c) for s2 in range(2) for c in range(DC)]):
                    last = pe.matmul(bk[:, o:o + SLOT], E1T[:, bass.DynSlice(ep, 1), c, ff * P:(ff + 1) * P], gt[:, s2, c, :],
                                     start=k == 0, stop=k == 3)
                done("pe", last, "gup", s, ff)
            yield
            need("act", ("gup", s, f + 1))
            if f == 0:
                if s >= NT:
                    need("act", ("gy", s - NT, NGT - 1))
                done("act", act.activation(HN[:, s % NT, :], e2s[:, bass.DynSlice(ea, 1), :].rearrange("p o d -> p (o d)"),
                                           ACT.Copy), "ge2", s)
            if s >= 2 and f == 0:
                need("act", ("gSl", s - 2, FC - 2))
            for ff in (f, f + 1):
                done("act", act.activation(G_S[s % 2][:, ff, :], bk[:, (ff - f) * SLOT:(ff - f + 1) * SLOT], ACT.Silu,
                                           scale=e1s[:, bass.DynSlice(ea, 1), ff]), "gsilu", s, ff)
            rd.append(("gsilu", s, f + 1))
            yield
            if s >= NGB and f == 0:
                yield from once("act", ("gdown", s - NGB, NGT - 1))
            o = slice(f, f + 2)
            need("act", ("gsilu", s, f + 1))
            done("act", act.activation(G_Sh[s % NGB][:, o], G_S[s % 2][:, o], ACT.Copy, scale=sdn[:]), "gSh", s, f)
            yield
            need("dve", ("gSh", s, f))
            done("dve", dve.scalar_tensor_tensor(G_Sl[s % NGB][:, o], G_S[s % 2][:, o], sdn[:], G_Sh[s % NGB][:, o],
                                                 ALU.mult, ALU.subtract), "gSl", s, f)
            yield

    def routed_down(s):
        ep = expert_of["pe", s]
        need("pe", ("gSl", s, FC - 2))
        g, y = G_rec[s % NGR], G_y[s % 3]
        key = ("g", s)
        w = s % 4
        for j in range(NGT):
            bk, rd = yield from take()
            for k, (f, sx) in enumerate([(f, sx) for f in range(FC) for sx in (G_Sh, G_Sl)]):
                last = pe.matmul(bk[:, 0:D], sx[s % NGB][:, f, j * P:(j + 1) * P], E2T[:, bass.DynSlice(ep, 1), f, :],
                                 start=k == 0, stop=k == 2 * FC - 1)
            done("pe", last, "gdown", s, j)
            yield
            need("dve", ("gdown", s, j), ("gat", s, NGT - 1), ("ge2", s))
            if s >= 3 and j == 0:
                yield from once("dve", ("gout", s - 3, NGT - 1))
            done("dve", dve.scalar_tensor_tensor(y[:, j, :], bk[:, 0:D], g[:, j, 2 * D:2 * D + 1],
                                                 HN[:, s % NT, :], ALU.mult, ALU.mult), "gy", s, j)
            rd.append(("gy", s, j))
            yield
            need("dve", ("gy", s, j))
            done("dve", dve.tensor_tensor(y[:, j, :], y[:, j, :], g[:, j, D:2 * D], ALU.add), "gx", s, j)
            yield
            need("dve", ("gx", s, j))
            bn(y[:, j, :], w, key, j)
            yield
            aggregate(w, key, j)

    def routed_root(s):
        yield from root(s % 4, ("g", s), NGT)

    def routed_norm(s):
        y, key, w = G_y[s % 3], ("g", s), s % 4
        for j in range(NGT):
            done("dve", normalise(y[:, j, :], y[:, j, :], w, key, j), "gn", s, j)
            yield

    def routed_out(s):
        for j in range(NGT):
            need("pool", ("gn", s, j))
            tt = s * NGT + j
            moved(pool.indirect_dma_start(t["out"], bass.IndirectOffsetOnAxis(ids[:, tt:tt + 1], 0), G_y[s % 3][:, j, :],
                                          None, bounds_check=TOK - 1, oob_is_err=False), f"out{s % 3}", "gout", s, j)
            yield

    def together(*threads):
        live = [[0.0, n, thread] for n, thread in enumerate(threads)]
        while live:
            x = min(live)
            issued = len(st.at)
            if next(x[2], "end") == "end":
                live.remove(x)
            elif len(st.at) == issued:
                x[0] = max(x[0], min((y[0] for y in live if y is not x), default=x[0])) + STUCK
            else:
                x[0] = st.latest

    over = set()

    def after(*parts):
        while not over.issuperset(parts):
            yield

    def series(name, part, count, earlier):
        for i in range(count):
            yield from after(*(x for x in earlier(i) if x[1] >= 0))
            yield from part(i)
            over.add((name, i))

    def project(b):
        yield from until("X", b)
        yield from until("XT", b)
        yield from a1_split(b)
        yield from a2_project(b)
        if b + 1 < B:
            load_xT(b + 1)

    def scores(b):
        yield from b1_scores(b)
        yield from b2_transpose(b)

    def values(b):
        yield from b3_values(b)
        if b + 2 < B:
            load_x(b + 2)

    def linear(b):
        yield from c1_transpose(b)
        yield from c2_linear(b)
        yield from d1_transpose(b)

    def rest(_):
        yield from setup_rest()

    def maps(which):
        def part(_):
            for e in reversed(range(NE + 1)):
                yield from expert_map(which, e)
        return part

    def guard(_):
        yield from guards()
        for eng in ("act", "dve", "pool"):
            need(eng, ("guards",))

    def sorting():
        yield from after(("router", B - 1))
        need("dve", ("h16", B - 1))
        for eng in ("dve", "act"):
            need(eng, *front_free)
        yield from sort_places()
        for k in range(NTILE // CHK):
            yield from sort_invert(k)
        yield from sort_ids()

    front_free = [("u", B - 1), ("x3", B - 1, NT - 1), ("U", B - 1, NT - 1), ("Ml", B - 1), ("Xl", B - 1)]
    load_x(1)
    together(setup_first())
    together(
        series("norms", f1_norms, B, lambda b: [("ode", b // GB), ("guard", 0)]),
        series("h", f1_h, B, lambda b: [("norms", b)]),
        series("router", f2_router, B, lambda b: [("h", b)]),
        series("down", g2_shared, B, lambda b: [("up", b)]),
        series("up", g1_shared, B, lambda b: [("router", b)]),
        series("ode", ode, B // GB, lambda g: [("projections", g * GB + GB - 1)]),
        series("projections", d3_values, B, lambda b: [("stats", b)]),
        series("stats", d2_stats, B, lambda b: [("linear", b), ("rest", 0)]),
        series("linear", linear, B, lambda b: [("values", b), ("rest", 0)]),
        series("values", values, B, lambda b: [("scores", b)]),
        series("scores", scores, B, lambda b: [("project", b)]),
        series("project", project, B, lambda b: [("values", b - 2)]),
        series("rest", rest, 1, lambda i: []),
        series("maps0", maps(0), 1, lambda i: []),
        series("maps1", maps(1), 1, lambda i: []),
        series("guard", guard, 1, lambda i: [("rest", 0), ("maps0", 0), ("maps1", 0)]),
        sorting())
    stages = {"R": (routed_root, 2), "N": (routed_norm, 3), "G": (gather, -2), "U": (routed_up, 0), "D": (routed_down, 2),
              "T": (routed_transpose, -1), "O": (routed_out, 3)}
    ROUND = "D U DD U NN U G OO D D U U T D U T D G U D D RR U"
    for s in range(-2, NG + 3):
        threads = {k: stage(s - lag) for k, (stage, lag) in stages.items() if 0 <= s - lag < NG}
        for k in ROUND.replace(" ", ""):
            next(threads.get(k, iter(())), None)
        for k in threads:
            for _ in threads[k]:
                pass
    for s in range(NG - 3, NG):
        need("sp", ("gout", s, NGT - 1))
    for lane in ("small", "zero"):
        sp.wait_ge(st.sems["d_" + lane], st.count["d_" + lane])


def kernel(**inputs):
    import concourse.bacc as bacc
    from concourse.bass_utils import run_bass_kernel_spmd

    a = {k: np.ascontiguousarray(v) for k, v in inputs.items()}
    x = a["L0_attn_x"].reshape(TOK, D)
    wqk = np.zeros((D, 4, 32), x.dtype)
    bqk = np.zeros((4, 32, 1), x.dtype)
    for s, (w, b) in enumerate([("w_q", "b_q")] * 2 + [("w_k", "b_k")] * 2):
        wqk[:, s, :QK] = a["L0_attn_" + w].T
        bqk[s, :QK, 0] = a["L0_attn_" + b]
    wall = a["L1_attn_qkv_w"]
    arrays = {
        "x": x, "xT": np.ascontiguousarray(x.T), "wqk": wqk.reshape(D, P), "bqk": bqk.reshape(P, 1),
        "w0": a["L0_ffn_weight"], "wall": wall, "wvT": np.ascontiguousarray(wall[:, 2 * D:].T),
        "pw": a["L1_attn_proj_w"], "cw1": a["L1_attn_ch_w1"], "cb1": a["L1_attn_ch_b1"].reshape(RED, 1),
        "cw2": a["L1_attn_ch_w2"], "cb2": np.ascontiguousarray(a["L1_attn_ch_b2"].reshape(DC, P).T),
        "pb": a["L1_attn_proj_b"].reshape(1, D), "gam": a["L1_ffn_ln_gamma"].reshape(1, D),
        "bet": a["L1_ffn_ln_beta"].reshape(1, D),
        "cc": np.stack([a["L1_attn_c1"].reshape(()), a["L1_attn_c2"].reshape(())]).reshape(1, 2),
        "c1w": a["L1_attn_conv1_w"].reshape(1, CH * TAPS), "c2w": a["L1_attn_conv2_w"].reshape(1, CH * TAPS),
        "gng": a["L1_attn_gn_g"].reshape(1, CH), "gnb": a["L1_attn_gn_b"].reshape(1, CH),
        "c2b": a["L1_attn_conv2_b"].reshape(1, 1), "rw": np.ascontiguousarray(a["L1_ffn_router_w"].T),
        "sw1": a["L1_ffn_shared_w1"], "sw2": a["L1_ffn_shared_w2"],
        "ew1": a["L1_ffn_expert_w1"], "ew2": a["L1_ffn_expert_w2"],
    }
    nc = bacc.Bacc("TRN2", target_bir_lowering=False, num_devices=1)
    t = {k: nc.dram_tensor("in_" + k, v.shape, mybir.dt.from_np(v.dtype), kind="ExternalInput").ap() for k, v in arrays.items()}
    t["out"] = nc.dram_tensor("out", (TOK, D), F32, kind="ExternalOutput").ap()
    build_program(nc, t)
    r = run_bass_kernel_spmd(nc, [{"in_" + k: v for k, v in arrays.items()}], core_ids=[0])
    return r.results[0]["out"].reshape(B, SEQ, D)
```
